# Optimizing a Trainium2 kernel written in Bass

```python
import numpy as np
import jax
import jax.numpy as jnp

def _softmax(x, axis=-1):
    return jax.nn.softmax(x, axis=axis)

def _gelu(x):
    return jax.nn.gelu(x, approximate=True)

def _silu(x):
    return jax.nn.silu(x)

def _sigmoid(x):
    return jax.nn.sigmoid(x)

def _layernorm(x, axis=-1, eps=1e-05):
    m = jnp.mean(x, axis=axis, keepdims=True)
    v = jnp.var(x, axis=axis, keepdims=True)
    return (x - m) / jnp.sqrt(v + eps)

def _scatter_add(tgt, idx, src, axis=0):
    return tgt.at[idx].add(src)

def _segment_sum(src, seg, n):
    return jax.ops.segment_sum(src, seg, n)
kernel_name = 'mk_decoder_postln_d2_seqx_r4_b1785e'

def setup_inputs(seed: int=0):
    np.random.seed(seed)
    _w = jnp.asarray

    def _rec_inputs():
        import jax
        import jax.numpy as jnp
        _rk = jax.random.key(seed)
        x = -0.000125 + 0.9999 * jax.random.normal(jax.random.fold_in(_rk, 1), (2, 512, 512), jnp.float32)
        _lenS = 512 - jax.random.randint(jax.random.fold_in(_rk, 7), (2,), 0, max(1, 512 // 4) + 1, jnp.int32)
        _lenS2 = 1024 - jax.random.randint(jax.random.fold_in(_rk, 8), (2,), 0, max(1, 1024 // 4) + 1, jnp.int32)
        _ctx_2048P = jax.random.normal(jax.random.fold_in(_rk, 11), (2, 16, 512), jnp.float32)
        _ctx_2048c = jax.random.dirichlet(jax.random.fold_in(_rk, 511), 0.3 * jnp.ones((16,), jnp.float32), (2, 1024))
        _ctx_2048t = jnp.einsum('bsk,bkd->bsd', _ctx_2048c, _ctx_2048P)
        _ctx_2048t = _ctx_2048t * jax.lax.rsqrt(jnp.mean(jnp.square(_ctx_2048t)) + 1e-12) * 0.953939
        ctx_2048 = -0.000514642 + 1.00011 * (_ctx_2048t + 0.3 * jax.random.normal(jax.random.fold_in(_rk, 611), (2, 1024, 512), jnp.float32))
        _validS = jnp.arange(512)[None, :] < _lenS[:, None]
        _validS2 = jnp.arange(1024)[None, :] < _lenS2[:, None]
        _causal = jnp.tril(jnp.ones((512, 512), dtype=bool))
        mask_BxS2_bk0 = jnp.logical_not(jnp.broadcast_to(_validS2[:, :], (2, 1024)))
        return (x, ctx_2048, mask_BxS2_bk0)
    x, ctx_2048, mask_BxS2_bk0 = _rec_inputs()

    def _L0_attn_setup():
        import jax, jax.numpy as jnp
        import numpy as np
        DIM = 512
        N_HEAD = 16
        N_KV_HEAD = 4
        DQK = 128
        DV = DIM // N_HEAD
        N_REP = N_HEAD // N_KV_HEAD
        WIN = 128
        FRONT = 64
        SEQ = 1024
        THETA = 10000.0

        def rope_cos_sin(seq_len, dim, theta=THETA):
            inv_freq = 1.0 / theta ** (np.arange(0, dim, 2)[:dim // 2].astype(np.float32) / dim)
            t = np.arange(seq_len, dtype=np.float32)
            ang = np.outer(t, inv_freq)
            return (jnp.asarray(np.cos(ang)), jnp.asarray(np.sin(ang)))

        def apply_rope(x, cos, sin):
            xr = x[..., 0::2]
            xi = x[..., 1::2]
            c = cos[None, :, None, :]
            s = sin[None, :, None, :]
            out_r = xr * c - xi * s
            out_i = xr * s + xi * c
            return jnp.stack([out_r, out_i], axis=-1).reshape(x.shape)

        def build_mask(seq_len, window, front):
            i = jnp.arange(seq_len)[:, None]
            j = jnp.arange(seq_len)[None, :]
            band = (j <= i) & (j > i - window)
            front_ok = (j < front) & (j <= i - window)
            allowed = band | front_ok
            return jnp.where(allowed, 0.0, -jnp.inf).astype(jnp.float32)
        key = jax.random.key(seed)
        ks = jax.random.split(key, 5)
        B = 1
        scale_in = 1.0 / np.sqrt(DIM)
        x = jax.random.normal(ks[0], (B, SEQ, DIM), dtype=jnp.float32)
        wq = jax.random.normal(ks[1], (DIM, N_HEAD * DQK), dtype=jnp.float32) * scale_in
        wk = jax.random.normal(ks[2], (DIM, N_KV_HEAD * DQK), dtype=jnp.float32) * scale_in
        wv = jax.random.normal(ks[3], (DIM, N_KV_HEAD * DV), dtype=jnp.float32) * scale_in
        wo = jax.random.normal(ks[4], (N_HEAD * DV, DIM), dtype=jnp.float32) * scale_in
        return {'x': x, 'wq': wq, 'wk': wk, 'wv': wv, 'wo': wo}
    _L0_attn_all = _L0_attn_setup()
    _L0_attn_in = {k: v for k, v in _L0_attn_all.items() if k in ('wq', 'wk', 'wv', 'wo')}
    del _L0_attn_all

    def _L0_xattn_setup():
        import jax, jax.numpy as jnp
        import numpy as np
        key = jax.random.key(seed)
        k1, k2, k3 = jax.random.split(key, 3)
        B, S, D, M = (8, 512, 512, 128)
        hidden_states = jax.random.normal(k1, (B, S, D), dtype=jnp.float32)
        memory_tokens = jax.random.normal(k2, (B, M, D), dtype=jnp.float32)
        memory_mask = jax.random.randint(k3, (B, M), 0, 2).astype(jnp.bool_)
        return {'hidden_states': hidden_states, 'memory_tokens': memory_tokens, 'memory_mask': memory_mask}
    _L0_xattn_all = _L0_xattn_setup()
    _L0_xattn_in = {k: v for k, v in _L0_xattn_all.items() if k in ()}
    del _L0_xattn_all

    def _L0_ffn_setup():
        import jax, jax.numpy as jnp
        import numpy as np
        H = 512
        I = 2048
        NE = 8
        S = 2
        N = NE - S
        K = N
        E = I // NE
        C = 2
        RESIDUAL = True
        B, L = (2, 512)

        def _swiglu(h, W, b):
            return jax.nn.silu(h @ W + b) * h
        key = jax.random.key(seed)
        ks = jax.random.split(key, 16)
        s = 0.02
        inp = {'x': jax.random.normal(ks[0], (B, L, H), dtype=jnp.float32), 'Wg': jax.random.normal(ks[1], (C, H, NE)) * s, 'bg': jnp.zeros((C, NE)), 'Wup': jax.random.normal(ks[2], (N, H, E)) * s, 'bup': jnp.zeros((N, E)), 'Wsw': jax.random.normal(ks[3], (N, E, E)) * s, 'bsw': jnp.zeros((N, E)), 'Wdn': jax.random.normal(ks[4], (N, E, H)) * s, 'bdn': jnp.zeros((N, H)), 'Wsu': jax.random.normal(ks[5], (H, S * E)) * s, 'bsu': jnp.zeros((S * E,)), 'Wsa': jax.random.normal(ks[6], (E, E)) * s, 'bsa': jnp.zeros((E,)), 'Wsd': jax.random.normal(ks[7], (S * E, H)) * s, 'bsd': jnp.zeros((H,))}
        return inp
    _L0_ffn_all = _L0_ffn_setup()
    _L0_ffn_in = {k: v for k, v in _L0_ffn_all.items() if k in ('Wg', 'bg', 'Wup', 'bup', 'Wsw', 'bsw', 'Wdn', 'bdn', 'Wsu', 'bsu', 'Wsa', 'bsa', 'Wsd', 'bsd')}
    del _L0_ffn_all

    def _L1_attn_setup():
        import jax, jax.numpy as jnp
        import numpy as np
        BATCH, SEQ, D_MODEL, N_HEADS, D_HEAD = (2, 512, 512, 16, 128)
        ATTN_SCALE = np.sqrt(D_HEAD).astype(np.float32)
        IGNORE = jnp.float32(-100000.0)
        key = jax.random.key(seed)
        ks = jax.random.split(key, 5)
        init = 1.0 / np.sqrt(D_MODEL)
        return {'x': jax.random.normal(ks[0], (BATCH, SEQ, D_MODEL), jnp.float32), 'W_Q': jax.random.normal(ks[1], (N_HEADS, D_MODEL, D_HEAD), jnp.float32) * init, 'W_K': jax.random.normal(ks[2], (N_HEADS, D_MODEL, D_HEAD), jnp.float32) * init, 'W_V': jax.random.normal(ks[3], (N_HEADS, D_MODEL, D_HEAD), jnp.float32) * init, 'W_O': jax.random.normal(ks[4], (N_HEADS, D_HEAD, D_MODEL), jnp.float32) * init, 'b_Q': jnp.zeros((N_HEADS, D_HEAD), jnp.float32), 'b_K': jnp.zeros((N_HEADS, D_HEAD), jnp.float32), 'b_V': jnp.zeros((N_HEADS, D_HEAD), jnp.float32), 'b_O': jnp.zeros((D_MODEL,), jnp.float32)}
    _L1_attn_all = _L1_attn_setup()
    _L1_attn_in = {k: v for k, v in _L1_attn_all.items() if k in ('W_Q', 'W_K', 'W_V', 'W_O', 'b_Q', 'b_K', 'b_V', 'b_O')}
    del _L1_attn_all

    def _L1_xattn_setup():
        import math
        import jax, jax.numpy as jnp
        import numpy as np
        HEADS = 16
        MASKED_BIAS = -10000.0

        def _mha(q, k, v):
            B, Sq, D = q.shape
            Sk = k.shape[-2]
            hd = D // HEADS
            qh = q.reshape(B, Sq, HEADS, hd).transpose(0, 2, 1, 3)
            kh = k.reshape(B, Sk, HEADS, hd).transpose(0, 2, 1, 3)
            vh = v.reshape(B, Sk, HEADS, hd).transpose(0, 2, 1, 3)
            scores = jnp.einsum('bhqd,bhkd->bhqk', qh, kh) / math.sqrt(hd)
            qi = jnp.arange(Sq)[:, None] + (Sk - Sq)
            ki = jnp.arange(Sk)[None, :]
            causal = ki <= qi
            scores = jnp.where(causal[None, None], scores, jnp.asarray(MASKED_BIAS, scores.dtype))
            attn = jax.nn.softmax(scores, axis=-1)
            out = jnp.einsum('bhqk,bhkd->bhqd', attn, vh)
            return out.transpose(0, 2, 1, 3).reshape(B, Sq, D)
        key = jax.random.key(seed)
        kq, kk, kv = jax.random.split(key, 3)
        B, S, D = (4, 256, 512)
        q = jax.random.normal(kq, (B, S, D), dtype=jnp.float32)
        k = jax.random.normal(kk, (B, S, D), dtype=jnp.float32)
        v = jax.random.normal(kv, (B, S, D), dtype=jnp.float32)
        return {'q': q, 'k': k, 'v': v}
    _L1_xattn_all = _L1_xattn_setup()
    _L1_xattn_in = {k: v for k, v in _L1_xattn_all.items() if k in ()}
    del _L1_xattn_all

    def _L1_ffn_setup():
        import jax, jax.numpy as jnp
        import numpy as np
        NUM_ROUTED = 7
        TOP_K = 3
        D = 512
        H = 512
        B, S = (4, 512)

        def _expert_ffn(x, w1, wg, w2):
            return jax.nn.silu(x @ w1) * (x @ wg) @ w2
        key = jax.random.key(seed)
        ks = jax.random.split(key, 8)
        s = 0.02
        return {'x': jax.random.normal(ks[0], (B, S, D), jnp.float32), 'W1': jax.random.normal(ks[1], (NUM_ROUTED, D, H), jnp.float32) * s, 'Wg': jax.random.normal(ks[2], (NUM_ROUTED, D, H), jnp.float32) * s, 'W2': jax.random.normal(ks[3], (NUM_ROUTED, H, D), jnp.float32) * s, 'Ws1': jax.random.normal(ks[4], (D, H), jnp.float32) * s, 'Wsg': jax.random.normal(ks[5], (D, H), jnp.float32) * s, 'Ws2': jax.random.normal(ks[6], (H, D), jnp.float32) * s, 'gate_w': jax.random.normal(ks[7], (D, NUM_ROUTED), jnp.float32) * s, 'gate_b': jnp.zeros((NUM_ROUTED,), jnp.float32), 'biases': jnp.zeros((NUM_ROUTED,), jnp.float32)}
    _L1_ffn_all = _L1_ffn_setup()
    _L1_ffn_in = {k: v for k, v in _L1_ffn_all.items() if k in ('W1', 'Wg', 'W2', 'Ws1', 'Wsg', 'Ws2', 'gate_w', 'gate_b', 'biases')}
    del _L1_ffn_all
    return {'x': x, 'ctx_2048': ctx_2048, 'mask_BxS2_bk0': mask_BxS2_bk0, 'L0_attn_wq': _L0_attn_in['wq'], 'L0_attn_wk': _L0_attn_in['wk'], 'L0_attn_wv': _L0_attn_in['wv'], 'L0_attn_wo': _L0_attn_in['wo'], 'L0_ffn_Wg': _L0_ffn_in['Wg'], 'L0_ffn_bg': _L0_ffn_in['bg'], 'L0_ffn_Wup': _L0_ffn_in['Wup'], 'L0_ffn_bup': _L0_ffn_in['bup'], 'L0_ffn_Wsw': _L0_ffn_in['Wsw'], 'L0_ffn_bsw': _L0_ffn_in['bsw'], 'L0_ffn_Wdn': _L0_ffn_in['Wdn'], 'L0_ffn_bdn': _L0_ffn_in['bdn'], 'L0_ffn_Wsu': _L0_ffn_in['Wsu'], 'L0_ffn_bsu': _L0_ffn_in['bsu'], 'L0_ffn_Wsa': _L0_ffn_in['Wsa'], 'L0_ffn_bsa': _L0_ffn_in['bsa'], 'L0_ffn_Wsd': _L0_ffn_in['Wsd'], 'L0_ffn_bsd': _L0_ffn_in['bsd'], 'L1_attn_W_Q': _L1_attn_in['W_Q'], 'L1_attn_W_K': _L1_attn_in['W_K'], 'L1_attn_W_V': _L1_attn_in['W_V'], 'L1_attn_W_O': _L1_attn_in['W_O'], 'L1_attn_b_Q': _L1_attn_in['b_Q'], 'L1_attn_b_K': _L1_attn_in['b_K'], 'L1_attn_b_V': _L1_attn_in['b_V'], 'L1_attn_b_O': _L1_attn_in['b_O'], 'L1_ffn_W1': _L1_ffn_in['W1'], 'L1_ffn_Wg': _L1_ffn_in['Wg'], 'L1_ffn_W2': _L1_ffn_in['W2'], 'L1_ffn_Ws1': _L1_ffn_in['Ws1'], 'L1_ffn_Wsg': _L1_ffn_in['Wsg'], 'L1_ffn_Ws2': _L1_ffn_in['Ws2'], 'L1_ffn_gate_w': _L1_ffn_in['gate_w'], 'L1_ffn_gate_b': _L1_ffn_in['gate_b'], 'L1_ffn_biases': _L1_ffn_in['biases']}

def reference(x, ctx_2048, mask_BxS2_bk0, L0_attn_wq, L0_attn_wk, L0_attn_wv, L0_attn_wo, L0_ffn_Wg, L0_ffn_bg, L0_ffn_Wup, L0_ffn_bup, L0_ffn_Wsw, L0_ffn_bsw, L0_ffn_Wdn, L0_ffn_bdn, L0_ffn_Wsu, L0_ffn_bsu, L0_ffn_Wsa, L0_ffn_bsa, L0_ffn_Wsd, L0_ffn_bsd, L1_attn_W_Q, L1_attn_W_K, L1_attn_W_V, L1_attn_W_O, L1_attn_b_Q, L1_attn_b_K, L1_attn_b_V, L1_attn_b_O, L1_ffn_W1, L1_ffn_Wg, L1_ffn_W2, L1_ffn_Ws1, L1_ffn_Wsg, L1_ffn_Ws2, L1_ffn_gate_w, L1_ffn_gate_b, L1_ffn_biases):
    import jax
    import jax.numpy as jnp

    def _L0_attn_ref(x, wq, wk, wv, wo):
        import jax, jax.numpy as jnp
        import numpy as np
        DIM = 512
        N_HEAD = 16
        N_KV_HEAD = 4
        DQK = 128
        DV = DIM // N_HEAD
        N_REP = N_HEAD // N_KV_HEAD
        WIN = 128
        FRONT = 64
        SEQ = 1024
        THETA = 10000.0

        def rope_cos_sin(seq_len, dim, theta=THETA):
            inv_freq = 1.0 / theta ** (np.arange(0, dim, 2)[:dim // 2].astype(np.float32) / dim)
            t = np.arange(seq_len, dtype=np.float32)
            ang = np.outer(t, inv_freq)
            return (jnp.asarray(np.cos(ang)), jnp.asarray(np.sin(ang)))

        def apply_rope(x, cos, sin):
            xr = x[..., 0::2]
            xi = x[..., 1::2]
            c = cos[None, :, None, :]
            s = sin[None, :, None, :]
            out_r = xr * c - xi * s
            out_i = xr * s + xi * c
            return jnp.stack([out_r, out_i], axis=-1).reshape(x.shape)

        def build_mask(seq_len, window, front):
            i = jnp.arange(seq_len)[:, None]
            j = jnp.arange(seq_len)[None, :]
            band = (j <= i) & (j > i - window)
            front_ok = (j < front) & (j <= i - window)
            allowed = band | front_ok
            return jnp.where(allowed, 0.0, -jnp.inf).astype(jnp.float32)
        B, S, _ = x.shape
        q = (x @ wq).reshape(B, S, N_HEAD, DQK)
        k = (x @ wk).reshape(B, S, N_KV_HEAD, DQK)
        v = (x @ wv).reshape(B, S, N_KV_HEAD, DV)
        cos, sin = rope_cos_sin(S, DQK)
        q = apply_rope(q, cos, sin)
        k = apply_rope(k, cos, sin)
        q = q.transpose(0, 2, 1, 3)
        k = k.transpose(0, 2, 1, 3)
        v = v.transpose(0, 2, 1, 3)
        k = jnp.repeat(k, N_REP, axis=1)
        v = jnp.repeat(v, N_REP, axis=1)
        mask = build_mask(S, WIN, FRONT)
        scores = jnp.einsum('bhqd,bhkd->bhqk', q, k) / np.sqrt(DQK).astype(np.float32)
        scores = scores + mask[None, None, :, :]
        attn = jax.nn.softmax(scores, axis=-1)
        out = jnp.einsum('bhqk,bhkd->bhqd', attn, v)
        out = out.transpose(0, 2, 1, 3).reshape(B, S, N_HEAD * DV)
        return out @ wo

    def _L0_xattn_ref(hidden_states, memory_tokens, memory_mask):
        import jax, jax.numpy as jnp
        import numpy as np
        B, S, D = hidden_states.shape
        scale = 1.0 / jnp.sqrt(jnp.asarray(D, hidden_states.dtype))
        scores = jnp.einsum('bsd,bmd->bsm', hidden_states, memory_tokens) * scale
        neg_inf = jnp.asarray(-1e+30, scores.dtype)
        scores = jnp.where(memory_mask[:, None, :], scores, neg_inf)
        attn = jax.nn.softmax(scores, axis=-1)
        readout = jnp.einsum('bsm,bmd->bsd', attn, memory_tokens)
        valid_b = jnp.any(memory_mask, axis=-1)
        out = jnp.where(valid_b[:, None, None], readout, jnp.zeros_like(readout))
        return out

    def _L0_ffn_ref(x, Wg, bg, Wup, bup, Wsw, bsw, Wdn, bdn, Wsu, bsu, Wsa, bsa, Wsd, bsd):
        import jax, jax.numpy as jnp
        import numpy as np
        H = 512
        I = 2048
        NE = 8
        S = 2
        N = NE - S
        K = N
        E = I // NE
        C = 2
        RESIDUAL = True
        B, L = (2, 512)

        def _swiglu(h, W, b):
            return jax.nn.silu(h @ W + b) * h
        bsz, seq, _ = x.shape
        xt = x.reshape(-1, H)
        res = xt
        for j in range(C):
            gate = xt @ Wg[j] + bg[j]
            _, ids = jax.lax.top_k(gate, K)
            in_top = jax.nn.one_hot(ids, NE, dtype=gate.dtype).sum(-2) > 0
            w = jax.nn.softmax(jnp.where(in_top, gate, -jnp.inf), axis=-1)
            h = jnp.einsum('th,nhe->nte', xt, Wup) + bup[:, None, :]
            h = jax.nn.silu(jnp.einsum('nte,nef->ntf', h, Wsw) + bsw[:, None, :]) * h
            eo = jnp.einsum('nte,neh->nth', h, Wdn) + bdn[:, None, :]
            out = jnp.einsum('nth,tn->th', eo, w[:, :N])
            sh = (xt @ Wsu + bsu).reshape(-1, S, E)
            sh = _swiglu(sh, Wsa, bsa)
            out = out + sh.reshape(-1, S * E) @ Wsd + bsd
            xt = res + out if RESIDUAL else out
        return xt.reshape(bsz, seq, H)

    def _L1_attn_ref(x, W_Q, W_K, W_V, W_O, b_Q, b_K, b_V, b_O):
        import jax, jax.numpy as jnp
        import numpy as np
        BATCH, SEQ, D_MODEL, N_HEADS, D_HEAD = (2, 512, 512, 16, 128)
        ATTN_SCALE = np.sqrt(D_HEAD).astype(np.float32)
        IGNORE = jnp.float32(-100000.0)
        q = jnp.einsum('bpd,hde->bphe', x, W_Q) + b_Q
        k = jnp.einsum('bpd,hde->bphe', x, W_K) + b_K
        v = jnp.einsum('bpd,hde->bphe', x, W_V) + b_V
        scores = jnp.einsum('bqhe,bkhe->bhqk', q, k) / ATTN_SCALE
        S = x.shape[1]
        causal = jnp.tril(jnp.ones((S, S), bool))
        scores = jnp.where(causal, scores, IGNORE)
        attn = jax.nn.softmax(scores, axis=-1)
        z = jnp.einsum('bkhe,bhqk->bqhe', v, attn)
        out = jnp.einsum('bqhe,hed->bqd', z, W_O) + b_O
        return out

    def _L1_xattn_ref(q, k, v):
        import math
        import jax, jax.numpy as jnp
        import numpy as np
        HEADS = 16
        MASKED_BIAS = -10000.0

        def _mha(q, k, v):
            B, Sq, D = q.shape
            Sk = k.shape[-2]
            hd = D // HEADS
            qh = q.reshape(B, Sq, HEADS, hd).transpose(0, 2, 1, 3)
            kh = k.reshape(B, Sk, HEADS, hd).transpose(0, 2, 1, 3)
            vh = v.reshape(B, Sk, HEADS, hd).transpose(0, 2, 1, 3)
            scores = jnp.einsum('bhqd,bhkd->bhqk', qh, kh) / math.sqrt(hd)
            qi = jnp.arange(Sq)[:, None] + (Sk - Sq)
            ki = jnp.arange(Sk)[None, :]
            causal = ki <= qi
            scores = jnp.where(causal[None, None], scores, jnp.asarray(MASKED_BIAS, scores.dtype))
            attn = jax.nn.softmax(scores, axis=-1)
            out = jnp.einsum('bhqk,bhkd->bhqd', attn, vh)
            return out.transpose(0, 2, 1, 3).reshape(B, Sq, D)
        return _mha(q, k, v)

    def _L1_ffn_ref(x, W1, Wg, W2, Ws1, Wsg, Ws2, gate_w, gate_b, biases):
        import jax, jax.numpy as jnp
        import numpy as np
        NUM_ROUTED = 7
        TOP_K = 3
        D = 512
        H = 512
        B, S = (4, 512)

        def _expert_ffn(x, w1, wg, w2):
            return jax.nn.silu(x @ w1) * (x @ wg) @ w2
        output = _expert_ffn(x, Ws1, Wsg, Ws2)
        gate_logits = x @ gate_w + gate_b
        gate_probas = jax.nn.softmax(gate_logits, axis=-1)
        biased_probas = gate_probas + biases
        _, topk_idxs = jax.lax.top_k(biased_probas, TOP_K)
        topk_probas = jnp.take_along_axis(gate_probas, topk_idxs, axis=-1)
        topk_probas = topk_probas / jnp.sum(topk_probas, axis=-1, keepdims=True)
        for e in range(NUM_ROUTED):
            w_e = jnp.sum(topk_probas * (topk_idxs == e), axis=-1)
            output = output + _expert_ffn(x, W1[e], Wg[e], W2[e]) * w_e[..., None]
        return output
    x = _layernorm(x + _L0_attn_ref(x, L0_attn_wq, L0_attn_wk, L0_attn_wv, L0_attn_wo), axis=-1)
    x = _layernorm(x + _L0_xattn_ref(x, ctx_2048, mask_BxS2_bk0), axis=-1)
    x = _layernorm(x + _L0_ffn_ref(x, L0_ffn_Wg, L0_ffn_bg, L0_ffn_Wup, L0_ffn_bup, L0_ffn_Wsw, L0_ffn_bsw, L0_ffn_Wdn, L0_ffn_bdn, L0_ffn_Wsu, L0_ffn_bsu, L0_ffn_Wsa, L0_ffn_bsa, L0_ffn_Wsd, L0_ffn_bsd), axis=-1)
    x = _layernorm(x + _L1_attn_ref(x, L1_attn_W_Q, L1_attn_W_K, L1_attn_W_V, L1_attn_W_O, L1_attn_b_Q, L1_attn_b_K, L1_attn_b_V, L1_attn_b_O), axis=-1)
    x = _layernorm(x + _L1_xattn_ref(x, ctx_2048, ctx_2048), axis=-1)
    x = _layernorm(x + _L1_ffn_ref(x, L1_ffn_W1, L1_ffn_Wg, L1_ffn_W2, L1_ffn_Ws1, L1_ffn_Wsg, L1_ffn_Ws2, L1_ffn_gate_w, L1_ffn_gate_b, L1_ffn_biases), axis=-1)
    return x

_drawn_inputs = setup_inputs


def setup_inputs(seed=0):
    import zlib

    import numpy as np

    out = dict(_drawn_inputs(seed))
    spreads = {'L0_ffn_bg': (0.0, 0.8),
     'L0_ffn_bup': (0.0, 0.8),
     'L0_ffn_bsw': (0.0, 0.8),
     'L0_ffn_bdn': (0.0, 2.0),
     'L0_ffn_bsu': (0.0, 0.8),
     'L0_ffn_bsa': (0.0, 0.8),
     'L0_ffn_bsd': (0.0, 0.8),
     'L1_attn_b_Q': (0.0, 0.607),
     'L1_attn_b_K': (0.0, 2.0),
     'L1_attn_b_V': (0.0, 0.1),
     'L1_attn_b_O': (0.0, 0.1),
     'L1_ffn_gate_b': (0.0, 2.0),
     'L1_ffn_biases': (0.0, 2.0)}
    factors = {'L0_ffn_Wg': 7.58,
     'L0_ffn_Wup': 8.0,
     'L0_ffn_Wsw': 8.0,
     'L0_ffn_Wdn': 8.0,
     'L0_ffn_Wsu': 8.0,
     'L0_ffn_Wsa': 8.0,
     'L0_ffn_Wsd': 7.961,
     'L1_ffn_gate_w': 2.715}
    for name, (base, spread) in spreads.items():
        noise = np.random.default_rng([zlib.crc32(name.encode()), seed]).standard_normal(out[name].shape)
        drawn = base * np.exp(spread * noise) if base else spread * noise
        out[name] = jnp.asarray(drawn.astype(out[name].dtype))
    for name, factor in factors.items():
        out[name] = (out[name] * factor).astype(out[name].dtype)
    return out
```

```python
from contextlib import ExitStack

import numpy as np

import concourse.bass as bass
from concourse import mybir

ALU = mybir.AluOpType
ACT = mybir.ActivationFunctionType
AX = mybir.AxisListType
F32 = mybir.dt.float32
F16 = mybir.dt.float16
F32R = mybir.dt.float32r
BF16 = mybir.dt.bfloat16
U8 = mybir.dt.uint8
I32 = mybir.dt.int32

P = 128
B, S, D = 2, 512, 512
NT = B * S // P
KD = D // P
QT = S // P
S2 = 1024
CT = S2 // P
H = 16
DQK = 128
KVH = 4
REP = H // KVH
DV = D // H
WIN, FRONT = 128, 64
NE = 8
E0 = 256
EPS = 1e-5
NEG = -2.0 ** 100

XS = 2.0 ** 5
WS = 2.0 ** 8
PS_ = 2.0 ** 10
SP0 = [P, 2 * P, 3 * P, 3 * P]
SO0 = [0, P, 3 * P, 6 * P]
KT0 = [(0,), (0, 1), (0, 1, 2), (0, 2, 3)]


def need(engine, sem, value):
    if isinstance(value, int) and value <= 0:
        return
    engine.wait_ge(sem, value)


def passed(engine, sem, n):
    if not isinstance(n, int):
        engine.sem_inc(sem, 1)


def products(pe, out, a, b, start=True, stop=True):
    pe.matmul(out, a[0], b[0], start=start, stop=False, skip_group_check=True)
    pe.matmul(out, a[0], b[1], start=False, stop=False, skip_group_check=True)
    return pe.matmul(out, a[1], b[0], start=False, stop=stop, skip_group_check=True)


def plain(a):
    return a.bitcast(F32) if a.dtype == F32R else a


class Core:

    def __init__(self, nc, ctx, inputs, out):
        self.nc, self.ctx, self.inp, self.out = nc, ctx, inputs, out
        self.n = 0
        self.sems = []
        self.X = self.sb(ctx, "X", [P, NT, D], F32)
        self.XTh = self.sb(ctx, "XTh", [P, KD, B * S], F16)
        self.XTl = self.sb(ctx, "XTl", [P, KD, B * S], F16)
        self.ident = self.sb(ctx, "ident", [P, P], F32)
        self.identb = self.sb(ctx, "identb", [P, P], BF16)
        self.PS = ctx.enter_context(nc.psum_tensor("PS", [P, 8, 512], F32))
        self.pool_passed = ctx.enter_context(nc.semaphore("pool_passed"))
        self.act_passed = ctx.enter_context(nc.semaphore("act_passed"))
        self.ctxT = [nc.dram_tensor(f"ctxT_{n}", [B, D, S2], F16, kind="Internal").ap() for n in ("hi", "lo")]

    def sb(self, ctx, name, shape, dt):
        self.n += 1
        return ctx.enter_context(self.nc.sbuf_tensor(f"{name}_{self.n}", shape, dt))

    def sem(self, ctx, name):
        self.n += 1
        if not self.sems:
            ctx.callback(self.free_sems)
        self.sems.append(self.nc.alloc_semaphore(f"{name}_{self.n}"))
        return self.sems[-1]

    def free_sems(self):
        self.nc.clear_and_free_semaphores(self.sems)
        self.nc.all_engine_barrier()
        self.sems = []


def phase_load(c):
    nc = c.nc
    with ExitStack() as ctx:
        x_in = c.sem(ctx, "x_in")
        ident_in = c.sem(ctx, "ident_in")
        block = ctx.enter_context(nc.Block())

        @block.sync
        def _(sp):
            sp.dma_start(c.ident[:], c.inp["c_ident"]).then_inc(ident_in, 16)
            sp.dma_start(c.X[:], c.inp["x"].rearrange("(t p) d -> p t d", p=P)).then_inc(x_in, 16)
            sp.wait_ge(x_in, 16)

        @block.vector
        def _(dve):
            dve.wait_ge(ident_in, 16)
            nc.vector.tensor_copy(c.identb[:], c.ident[:])


def phase_norm(c, norm=True, transpose=True, store=False, wide=False):
    nc = c.nc
    XTh, XTl, scale = c.wide if wide else (c.XTh, c.XTl, XS)
    with ExitStack() as ctx:
        stats = c.sb(ctx, "stats", [P, NT, 6], F32)
        mv = c.sb(ctx, "mv", [P, NT, 2], F32)
        veps = c.sb(ctx, "veps", [P, NT], F32)
        std = c.sb(ctx, "std", [P, NT], F32)
        rstd = c.sb(ctx, "rstd", [P, NT], F32)
        stats_done = c.sem(ctx, "stats_done")
        mv_done = c.sem(ctx, "mv_done")
        veps_done = c.sem(ctx, "veps_done")
        std_done = c.sem(ctx, "std_done")
        rstd_done = c.sem(ctx, "rstd_done")
        normed = c.sem(ctx, "normed")
        turned = c.sem(ctx, "turned")
        hi_done = c.sem(ctx, "hi_done")
        lo_done = c.sem(ctx, "lo_done")
        stored = c.sem(ctx, "stored")
        block = ctx.enter_context(nc.Block())

        @block.vector
        def _(dve):
            if norm:
                for t in range(NT):
                    nc.vector.bn_stats(stats[:, t, :], c.X[:, t, :]).then_inc(stats_done, 1)
                for t in range(NT):
                    dve.wait_ge(stats_done, t + 1)
                    nc.vector.bn_aggr(mv[:, t, :], stats[:, t, :]).then_inc(mv_done, 1)
                dve.wait_ge(mv_done, NT)
                nc.vector.tensor_scalar(veps[:], mv[:, :, 1], EPS, None, ALU.add).then_inc(veps_done, 1)
                dve.wait_ge(std_done, 1)
                nc.vector.reciprocal(rstd[:], std[:]).then_inc(rstd_done, 1)
                dve.wait_ge(rstd_done, 1)
            for t in range(NT + 2):
                if norm and t < NT:
                    nc.vector.tensor_scalar(c.X[:, t, :], c.X[:, t, :], mv[:, t, 0:1], rstd[:, t:t + 1],
                                            ALU.subtract, ALU.mult).then_inc(normed, 1)
                if transpose and t >= 2:
                    u = t - 2
                    dve.wait_ge(hi_done, u + 1)
                    nc.vector.scalar_tensor_tensor(
                        out=XTl[:, :, u * P:(u + 1) * P],
                        in0=c.PS[:, u % 4, :].rearrange("p (k q) -> p k q", k=KD), scalar=scale,
                        in1=plain(XTh[:, :, u * P:(u + 1) * P]), op0=ALU.mult, op1=ALU.subtract).then_inc(lo_done, 1)

        @block.scalar
        def _(act):
            if norm:
                act.wait_ge(veps_done, 1)
                nc.scalar.activation(std[:], veps[:], ACT.Sqrt).then_inc(std_done, 1)
            if transpose:
                for t in range(NT):
                    act.wait_ge(turned, t + 1)
                    nc.scalar.activation(XTh[:, :, t * P:(t + 1) * P],
                                         c.PS[:, t % 4, :].rearrange("p (k q) -> p k q", k=KD),
                                         ACT.Copy, scale=scale).then_inc(hi_done, 1)

        @block.tensor
        def _(pe):
            if transpose:
                for t in range(NT):
                    if norm:
                        pe.wait_ge(normed, t + 1)
                    need(pe, lo_done, t - 3)
                    for k in range(KD):
                        last = pe.transpose(c.PS[:, t % 4, k * P:(k + 1) * P], c.X[:, t, k * P:(k + 1) * P], c.ident[:])
                    last.then_inc(turned, 1)

        @block.sync
        def _(sp):
            if store:
                y = c.out.rearrange("(t p) d -> p t d", p=P)
                for t in range(NT):
                    sp.wait_ge(normed, t + 1)
                    sp.dma_start(y[:, t, :], c.X[:, t, :]).then_inc(stored, 16)
                sp.wait_ge(stored, 16 * NT)


def phase_gate(c, W, wg, bias, n, top, selection_bias=None, wide=False):
    nc = c.nc
    XTh, XTl, xs = c.wide if wide else (c.XTh, c.XTl, XS)
    part, wsc = (F32R, 1.0) if wide else (F16, WS)
    with ExitStack() as ctx:
        w32 = c.sb(ctx, "gate_w32", [P, KD, n], F32)
        wh = c.sb(ctx, "gate_wh", [P, KD, n], part)
        wl = c.sb(ctx, "gate_wl", [P, KD, n], part)
        bb = c.sb(ctx, "gate_bias", [P, n], F32)
        sel_b = c.sb(ctx, "gate_selection", [P, n], F32)
        below = c.sb(ctx, "below", [P, 8, 8], F32)
        G = c.sb(ctx, "G", [P, NT, n], F32)
        K = c.sb(ctx, "keys", [P, NT, n], F32)
        E = c.sb(ctx, "E", [P, NT, n], F32)
        gt = c.sb(ctx, "gt", [P, NT, n, n], F32)
        eq = c.sb(ctx, "eq", [P, NT, n, n], F32)
        rank = c.sb(ctx, "rank", [P, NT, n], F32)
        m = c.sb(ctx, "m", [P, NT], F32)
        total = c.sb(ctx, "total", [P, NT], F32)
        gate_in = c.sem(ctx, "gate_in")
        parts = c.sem(ctx, "gate_parts")
        gates = c.sem(ctx, "gates")
        step = c.sem(ctx, "gate_step")
        shifted = c.sem(ctx, "shifted")
        exp_done = c.sem(ctx, "gate_exp")
        block = ctx.enter_context(nc.Block())

        @block.sync
        def _(sp):
            sp.dma_start(w32[:], wg.rearrange("(k p) n -> p k n", p=P)).then_inc(gate_in, 16)
            sp.dma_start(bb[:], bias.partition_broadcast(P)).then_inc(gate_in, 16)
            sp.dma_start(below[:], c.inp["c_below"].partition_broadcast(P)).then_inc(gate_in, 16)
            sb_ = selection_bias if selection_bias is not None else bias
            sp.dma_start(sel_b[:], sb_.partition_broadcast(P)).then_inc(gate_in, 16)

        @block.tensor
        def _(pe):
            pe.wait_ge(parts, 2)
            for t in range(NT):
                for k in range(KD):
                    tok = slice(t * P, (t + 1) * P)
                    last = products(pe, c.PS[:, 0, t * 8:t * 8 + n], (XTh[:, k, tok], XTl[:, k, tok]),
                                    (wh[:, k, :], wl[:, k, :]), start=(k == 0), stop=(k == KD - 1))
            last.then_inc(gates, 1)

        def over_e(a):
            return a[:].unsqueeze(2).broadcast_to([P, NT, n])

        @block.scalar
        def _(act):
            act.wait_ge(shifted, 1)
            nc.scalar.activation(E[:], E[:], ACT.Exp).then_inc(exp_done, 1)

        @block.vector
        def _(dve):
            count = [0]

            def link(instruction):
                count[0] += 1
                instruction.then_inc(step, 1)
                dve.wait_ge(step, count[0])

            dve.wait_ge(gate_in, 64)
            nc.vector.tensor_scalar(wh[:], w32[:], wsc, None, ALU.mult).then_inc(parts, 1)
            dve.wait_ge(parts, 1)
            nc.vector.scalar_tensor_tensor(out=wl[:], in0=w32[:], scalar=wsc, in1=plain(wh[:]),
                                           op0=ALU.mult, op1=ALU.subtract).then_inc(parts, 1)
            link(nc.vector.memset(W[:], 1.0))
            dve.wait_ge(gates, 1)
            link(nc.vector.tensor_scalar(E[:], c.PS[:, 0, 0:64].rearrange("p (t e) -> p t e", e=8)[:, :, 0:n],
                                         1.0 / (xs * wsc), None, ALU.mult))
            link(nc.vector.tensor_tensor(G[:], E[:], bb[:].unsqueeze(1).broadcast_to([P, NT, n]), ALU.add))
            link(nc.vector.tensor_reduce(m[:], G[:], AX.X, ALU.max))
            nc.vector.tensor_tensor(E[:], G[:], over_e(m), ALU.subtract).then_inc(shifted, 1)
            dve.wait_ge(exp_done, 1)
            if selection_bias is None:
                keys = G
            else:
                keys = K
                link(nc.vector.tensor_reduce(total[:], E[:], AX.X, ALU.add))
                link(nc.vector.reciprocal(m[:], total[:]))
                link(nc.vector.tensor_tensor(E[:], E[:], over_e(m), ALU.mult))
                link(nc.vector.tensor_tensor(K[:], E[:], sel_b[:].unsqueeze(1).broadcast_to([P, NT, n]), ALU.add))
            for i in range(n):
                me = keys[:, :, i:i + 1].broadcast_to([P, NT, n])
                nc.vector.tensor_tensor(gt[:, :, i, :], keys[:], me, ALU.is_gt)
                a = nc.vector.tensor_tensor(eq[:, :, i, :], keys[:], me, ALU.is_equal)
            link(a)
            for t in range(NT):
                a = nc.vector.tensor_tensor(eq[:, t], eq[:, t], below[:, 0:n, 0:n], ALU.mult)
            link(a)
            link(nc.vector.tensor_tensor(gt[:], gt[:], eq[:], ALU.add))
            link(nc.vector.tensor_reduce(rank[:], gt[:], AX.X, ALU.add))
            link(nc.vector.tensor_scalar(rank[:], rank[:], float(top), None, ALU.is_lt))
            link(nc.vector.tensor_tensor(E[:], E[:], rank[:], ALU.mult))
            link(nc.vector.tensor_reduce(total[:], E[:], AX.X, ALU.add))
            link(nc.vector.reciprocal(m[:], total[:]))
            if selection_bias is None:
                n_routed = NE - 2
            else:
                n_routed = NE - 1
            link(nc.vector.tensor_tensor(W[:, :, 0:n_routed], E[:, :, 0:n_routed],
                                         m[:].unsqueeze(2).broadcast_to([P, NT, n_routed]), ALU.mult))


def phase_ffn1(c, W):
    nc = c.nc
    with ExitStack() as ctx:
        st = [c.sb(ctx, f"stage{i}", [P, KD, D], F32) for i in range(3)]
        wh = [[c.sb(ctx, f"wh{i}{q}", [P, KD, D], F16) for i in range(3)] for q in range(2)]
        wl = [[c.sb(ctx, f"wl{i}{q}", [P, KD, D], F16) for i in range(3)] for q in range(2)]
        Gh = c.sb(ctx, "Gh", [P, KD, B * S], F16)
        Gl = c.sb(ctx, "Gl", [P, KD, B * S], F16)
        s32 = c.sb(ctx, "s32", [P, 2, S], F32)
        g32 = c.sb(ctx, "g32", [P, 2, S], F32)
        ws = c.sb(ctx, "ws", [P, NT, NE], F32)
        w_in = [c.sem(ctx, f"w{i}_in") for i in range(3)]
        w_hi = c.sem(ctx, "w_hi")
        w_lo = c.sem(ctx, "w_lo")
        ws_done = c.sem(ctx, "ws_done")
        up_done = c.sem(ctx, "up_done")
        silu_done = c.sem(ctx, "silu_done")
        g_done = c.sem(ctx, "g_done")
        g_hi = c.sem(ctx, "g_hi")
        g_lo = c.sem(ctx, "g_lo")
        down_done = c.sem(ctx, "down_done")
        added = c.sem(ctx, "added")
        block = ctx.enter_context(nc.Block())
        UP = B * KD
        CH = 3 * KD
        dram = [c.inp[k] for k in ("ffn1_W1", "ffn1_Wg", "ffn1_W2")]

        @block.sync
        def _(sp):
            def load(e):
                for i in range(3):
                    need(sp, w_lo, CH * (e - 1) + KD * (i + 1))
                    sp.dma_start(st[i][:], dram[i][e].rearrange("(k p) n -> p k n", p=P)
                                 if isinstance(e, int) else
                                 dram[i][bass.ds(e, 1)].rearrange("e (k p) n -> p (e k) n", p=P)).then_inc(w_in[i], 16)
            load(0)
            with sp.Fori(1, NE) as e:
                load(e)

        def split_hi(pool, e, q, ch):
            i, k = divmod(ch, KD)
            if k == 0:
                pool.wait_ge(w_in[i], 16 * (e + 1))
                need(pool, down_done, NT * (e - 1))
                passed(pool, c.pool_passed, e)
            nc.gpsimd.tensor_scalar(wh[q][i][:, k, :], st[i][:, k, :], WS, None, ALU.mult).then_inc(w_hi, 1)

        def split_lo(dve, e, q, ch):
            i, k = divmod(ch, KD)
            dve.wait_ge(w_hi, CH * e + ch + 1)
            nc.vector.scalar_tensor_tensor(out=wl[q][i][:, k, :], in0=st[i][:, k, :], scalar=WS,
                                           in1=wh[q][i][:, k, :], op0=ALU.mult, op1=ALU.subtract).then_inc(w_lo, 1)

        @block.gpsimd
        def _(pool):
            def body(e, q, more):
                for m in range(UP):
                    n = UP * e + m
                    if more:
                        for ch in range(CH * m // UP, CH * (m + 1) // UP):
                            split_hi(pool, e + 1, 1 - q, ch)
                    pool.wait_ge(g_done, n + 1)
                    if m == 0:
                        need(pool, down_done, NT * e)
                    g = Gh[:, m % KD, (m // KD) * S:(m // KD + 1) * S]
                    passed(pool, c.pool_passed, e)
                    nc.gpsimd.tensor_copy(g, g32[:, m % 2, :]).then_inc(g_hi, 1)
                    pool.wait_ge(g_hi, n + 1)
                    nc.gpsimd.tensor_tensor(Gl[:, m % KD, (m // KD) * S:(m // KD + 1) * S], g32[:, m % 2, :], g,
                                            ALU.subtract).then_inc(g_lo, 1)
            for ch in range(CH):
                split_hi(pool, 0, 0, ch)
            body(0, 0, True)
            with pool.Fori(0, NE // 2 - 1) as i:
                body(2 * i + 1, 1, True)
                body(2 * i + 2, 0, True)
            body(NE - 1, 1, False)

        @block.tensor
        def _(pe):
            def body(e, q):
                pe.wait_ge(w_lo, CH * e + 2 * KD)
                for m in range(UP):
                    b, ht = divmod(m, KD)
                    need(pe, g_done, UP * e + m - 1)
                    for i in range(2):
                        for k in range(KD):
                            last = products(pe, c.PS[:, 2 * (m % 2) + i, :],
                                            (wh[q][i][:, k, ht * P:(ht + 1) * P], wl[q][i][:, k, ht * P:(ht + 1) * P]),
                                            (c.XTh[:, k, b * S:(b + 1) * S], c.XTl[:, k, b * S:(b + 1) * S]),
                                            start=(k == 0), stop=(k == KD - 1))
                    last.then_inc(up_done, 1)
                pe.wait_ge(w_lo, CH * (e + 1))
                for t in range(NT):
                    if t % QT == 0:
                        pe.wait_ge(g_lo, UP * e + KD * (t // QT + 1))
                    need(pe, added, NT * e + t - 3)
                    for k in range(KD):
                        tok = slice(t * P, (t + 1) * P)
                        last = products(pe, c.PS[:, 4 + t % 4, :], (Gh[:, k, tok], Gl[:, k, tok]),
                                        (wh[q][2][:, k, :], wl[q][2][:, k, :]), start=(k == 0), stop=(k == KD - 1))
                    last.then_inc(down_done, 1)
            body(0, 0)
            with pe.Fori(0, NE // 2 - 1) as i:
                body(2 * i + 1, 1)
                body(2 * i + 2, 0)
            body(NE - 1, 1)

        @block.scalar
        def _(act):
            def body(e):
                for m in range(UP):
                    n = UP * e + m
                    act.wait_ge(up_done, n + 1)
                    need(act, g_done, n - 1)
                    nc.scalar.activation(s32[:, m % 2, :], c.PS[:, 2 * (m % 2), :], ACT.Silu,
                                         scale=1.0 / (XS * WS)).then_inc(silu_done, 1)
            body(0)
            with act.Fori(1, NE) as e:
                body(e)

        @block.vector
        def _(dve):
            def body(e, q, more):
                for m in range(UP + NT):
                    n = UP * e + m
                    if m < UP:
                        dve.wait_ge(silu_done, n + 1)
                        need(dve, g_lo, n - 1)
                        nc.vector.scalar_tensor_tensor(out=g32[:, m % 2, :], in0=c.PS[:, 2 * (m % 2) + 1, :],
                                                       scalar=1.0 / WS, in1=s32[:, m % 2, :],
                                                       op0=ALU.mult, op1=ALU.mult).then_inc(g_done, 1)
                        if more:
                            for ch in range(CH * m // UP, CH * (m + 1) // UP):
                                split_lo(dve, e + 1, 1 - q, ch)
                    else:
                        t = m - UP
                        dve.wait_ge(down_done, NT * e + t + 1)
                        need(dve, added, NT * (e - 1) + t + 1)
                        w = ws[:, t, e:e + 1] if isinstance(e, int) else ws[:, t, bass.ds(e, 1)]
                        nc.vector.scalar_tensor_tensor(out=c.X[:, t, :], in0=c.PS[:, 4 + t % 4, :], scalar=w,
                                                       in1=c.X[:, t, :], op0=ALU.mult, op1=ALU.add).then_inc(added, 1)
            nc.vector.tensor_scalar(ws[:], W[:], 1.0 / (XS * WS), None, ALU.mult).then_inc(ws_done, 1)
            dve.wait_ge(ws_done, 1)
            for ch in range(CH):
                split_lo(dve, 0, 0, ch)
            body(0, 0, True)
            with dve.Fori(0, NE // 2 - 1) as i:
                body(2 * i + 1, 1, True)
                body(2 * i + 2, 0, True)
            body(NE - 1, 1, False)


def phase_ffn0(c, W, res):
    nc = c.nc
    XTh, XTl, _ = c.wide
    M0 = E0 // P
    with ExitStack() as ctx:
        st = [c.sb(ctx, f"stage{i}", [P, k, n], F32) for i, (k, n) in enumerate([(KD, E0), (M0, E0), (M0, D)])]
        wh = [[c.sb(ctx, f"wh{i}{q}", [P, k, n], F32R) for i, (k, n) in enumerate([(KD, E0), (M0, E0), (M0, D)])] for q in range(2)]
        wl = [[c.sb(ctx, f"wl{i}{q}", [P, k, n], F32R) for i, (k, n) in enumerate([(KD, E0), (M0, E0), (M0, D)])] for q in range(2)]
        bup = c.sb(ctx, "bup", [P, NE, M0], F32)
        bsw = c.sb(ctx, "bsw", [P, NE, M0], F32)
        bdn = c.sb(ctx, "bdn", [NE, D], F32)
        WT = c.sb(ctx, "WT", [NE, NT, P], F32)
        Hh = c.sb(ctx, "Hh", [P, M0, B * S], F32R)
        Hl = c.sb(ctx, "Hl", [P, M0, B * S], F32R)
        Gh = c.sb(ctx, "Gh", [P, M0, B * S], F32R)
        Gl = c.sb(ctx, "Gl", [P, M0, B * S], F32R)
        UP = B * M0
        h32 = c.sb(ctx, "h32", [P, UP, S], F32)
        s32 = c.sb(ctx, "s32", [P, 2, S], F32)
        g32 = c.sb(ctx, "g32", [P, 2, S], F32)
        w_in = [c.sem(ctx, f"w{i}_in") for i in range(3)]
        bias_in = c.sem(ctx, "bias_in")
        w_hi = c.sem(ctx, "w_hi")
        w_lo = c.sem(ctx, "w_lo")
        wt_turned = c.sem(ctx, "wt_turned")
        wt_done = c.sem(ctx, "wt_done")
        res_done = c.sem(ctx, "res_done")
        biases_done = c.sem(ctx, "biases_done")
        up_done = c.sem(ctx, "up_done")
        h_done = c.sem(ctx, "h_done")
        h_hi = c.sem(ctx, "h_hi")
        h_lo = c.sem(ctx, "h_lo")
        sw_done = c.sem(ctx, "sw_done")
        silu_done = c.sem(ctx, "silu_done")
        g_done = c.sem(ctx, "g_done")
        g_hi = c.sem(ctx, "g_hi")
        g_lo = c.sem(ctx, "g_lo")
        down_done = c.sem(ctx, "down_done")
        added = c.sem(ctx, "added")
        block = ctx.enter_context(nc.Block())
        dram = [c.inp[k] for k in ("ffn0_Wup", "ffn0_Wsw", "ffn0_Wdn")]
        parts = [(i, h) for i in range(3) for h in range(2 if i != 1 else 1)]
        CH = len(parts)
        LAST = [2, 3, 5]

        def piece(buffer, ch):
            i, h = parts[ch]
            flat = buffer[i][:].rearrange("p k n -> p (k n)")
            return flat[:, h * 512:(h + 1) * 512]

        def col(a, e, m):
            return a[:, e, m:m + 1] if isinstance(e, int) else a[:, bass.ds(e, 1), m:m + 1].rearrange("p e m -> p (e m)")

        @block.sync
        def _(sp):
            def load(e):
                for i in range(3):
                    need(sp, w_lo, CH * (e - 1) + LAST[i])
                    sp.dma_start(st[i][:], dram[i][e].rearrange("(k p) n -> p k n", p=P)
                                 if isinstance(e, int) else
                                 dram[i][bass.ds(e, 1)].rearrange("e (k p) n -> p (e k) n", p=P)).then_inc(w_in[i], 16)
            load(0)
            sp.dma_start(bup[:], c.inp["ffn0_bup"]).then_inc(bias_in, 16)
            sp.dma_start(bsw[:], c.inp["ffn0_bsw"]).then_inc(bias_in, 16)
            sp.dma_start(bdn[:], c.inp["ffn0_bdn"]).then_inc(bias_in, 16)
            with sp.Fori(1, NE) as e:
                load(e)

        def split_hi(pool, e, q, ch):
            i, h = parts[ch]
            if h == 0:
                pool.wait_ge(w_in[i], 16 * (e + 1))
                need(pool, down_done, NT * (e - 1))
                passed(pool, c.pool_passed, e)
            nc.gpsimd.tensor_copy(piece(wh[q], ch), piece(st, ch)).then_inc(w_hi, 1)

        def split_lo(dve, e, q, ch):
            dve.wait_ge(w_hi, CH * e + ch + 1)
            nc.vector.tensor_tensor(piece(wl[q], ch), piece(st, ch), plain(piece(wh[q], ch)), ALU.subtract).then_inc(w_lo, 1)

        def at(buffer, m):
            return buffer[:, m % M0, (m // M0) * S:(m // M0 + 1) * S]

        @block.gpsimd
        def _(pool):
            def body(e, q, more):
                for m in range(UP):
                    if m == 0:
                        need(pool, sw_done, UP * e)
                    pool.wait_ge(h_done, UP * e + m + 1)
                    passed(pool, c.pool_passed, e)
                    nc.gpsimd.tensor_copy(at(Hh, m), h32[:, m, :]).then_inc(h_hi, 1)
                if more:
                    for ch in range(CH):
                        split_hi(pool, e + 1, 1 - q, ch)
                for m in range(UP):
                    n = UP * e + m
                    if m == 0:
                        need(pool, down_done, NT * e)
                    pool.wait_ge(g_done, n + 1)
                    passed(pool, c.pool_passed, e)
                    nc.gpsimd.tensor_copy(at(Gh, m), g32[:, m % 2, :]).then_inc(g_hi, 1)
                    pool.wait_ge(g_hi, n + 1)
                    nc.gpsimd.tensor_tensor(at(Gl, m), g32[:, m % 2, :], plain(at(Gh, m)), ALU.subtract).then_inc(g_lo, 1)
            for ch in range(CH):
                split_hi(pool, 0, 0, ch)
            body(0, 0, True)
            with pool.Fori(0, NE // 2 - 1) as i:
                body(2 * i + 1, 1, True)
                body(2 * i + 2, 0, True)
            body(NE - 1, 1, False)

        @block.tensor
        def _(pe):
            pe.wait_ge(bias_in, 48)
            for t in range(NT):
                last = pe.transpose(c.PS[0:NE, t // 4, (t % 4) * P:(t % 4 + 1) * P], W[:, t, :], c.ident[:])
            last.then_inc(wt_turned, 1)
            pe.wait_ge(wt_done, 1)
            for t in range(NT):
                need(pe, res_done, t - 3)
                pe.matmul(c.PS[:, 4 + t % 4, :], WT[:, t, :], bdn[:], start=True, stop=True).then_inc(biases_done, 1)

            def body(e, q):
                pe.wait_ge(w_lo, CH * e + LAST[0])
                for m in range(UP):
                    b, mt = divmod(m, M0)
                    need(pe, h_done, UP * e + m - 1)
                    for k in range(KD):
                        w = slice(mt * P, (mt + 1) * P)
                        last = products(pe, c.PS[:, m % 2, :], (wh[q][0][:, k, w], wl[q][0][:, k, w]),
                                        (XTh[:, k, b * S:(b + 1) * S], XTl[:, k, b * S:(b + 1) * S]),
                                        start=(k == 0), stop=(k == KD - 1))
                    last.then_inc(up_done, 1)
                pe.wait_ge(w_lo, CH * e + LAST[1])
                for m in range(UP):
                    b, mt = divmod(m, M0)
                    pe.wait_ge(h_lo, UP * e + M0 * (b + 1))
                    need(pe, silu_done, UP * e + m - 1)
                    for k in range(M0):
                        w = slice(mt * P, (mt + 1) * P)
                        last = products(pe, c.PS[:, 2 + m % 2, :], (wh[q][1][:, k, w], wl[q][1][:, k, w]),
                                        (Hh[:, k, b * S:(b + 1) * S], Hl[:, k, b * S:(b + 1) * S]),
                                        start=(k == 0), stop=(k == M0 - 1))
                    last.then_inc(sw_done, 1)
                pe.wait_ge(w_lo, CH * e + LAST[2])
                if isinstance(e, int) and e == 0:
                    pe.wait_ge(res_done, NT)
                for t in range(NT):
                    if t % QT == 0:
                        pe.wait_ge(g_lo, UP * e + M0 * (t // QT + 1))
                    need(pe, added, NT * e + t - 3)
                    for k in range(M0):
                        tok = slice(t * P, (t + 1) * P)
                        last = products(pe, c.PS[:, 4 + t % 4, :], (Gh[:, k, tok], Gl[:, k, tok]),
                                        (wh[q][2][:, k, :], wl[q][2][:, k, :]), start=(k == 0), stop=(k == M0 - 1))
                    last.then_inc(down_done, 1)
            body(0, 0)
            with pe.Fori(0, NE // 2 - 1) as i:
                body(2 * i + 1, 1)
                body(2 * i + 2, 0)
            body(NE - 1, 1)

        @block.scalar
        def _(act):
            def body(e):
                for m in range(UP):
                    n = UP * e + m
                    act.wait_ge(up_done, n + 1)
                    need(act, g_done, n - UP + 1)
                    passed(act, c.act_passed, e)
                    nc.scalar.activation(h32[:, m, :], c.PS[:, m % 2, :], ACT.Identity, bias=col(bup, e, m % M0)).then_inc(h_done, 1)
                for m in range(UP):
                    n = UP * e + m
                    act.wait_ge(sw_done, n + 1)
                    need(act, g_done, n - 1)
                    passed(act, c.act_passed, e)
                    nc.scalar.activation(s32[:, m % 2, :], c.PS[:, 2 + m % 2, :], ACT.Silu, bias=col(bsw, e, m % M0)).then_inc(silu_done, 1)
            act.wait_ge(bias_in, 48)
            act.wait_ge(wt_turned, 1)
            nc.scalar.activation(WT[:].rearrange("e t p -> e (t p)"), c.PS[0:NE, 0:2, :].rearrange("e a b -> e (a b)"),
                                 ACT.Copy).then_inc(wt_done, 1)
            act.wait_ge(wt_done, 1)
            body(0)
            with act.Fori(1, NE) as e:
                body(e)

        @block.vector
        def _(dve):
            def body(e, q, more):
                for m in range(UP):
                    n = UP * e + m
                    dve.wait_ge(h_hi, n + 1)
                    nc.vector.tensor_tensor(at(Hl, m), h32[:, m, :], plain(at(Hh, m)), ALU.subtract).then_inc(h_lo, 1)
                for m in range(UP):
                    n = UP * e + m
                    dve.wait_ge(silu_done, n + 1)
                    need(dve, g_lo, n - 1)
                    nc.vector.tensor_tensor(g32[:, m % 2, :], h32[:, m, :], s32[:, m % 2, :], ALU.mult).then_inc(g_done, 1)
                if more:
                    for ch in range(CH):
                        split_lo(dve, e + 1, 1 - q, ch)
                for t in range(NT):
                    dve.wait_ge(down_done, NT * e + t + 1)
                    need(dve, added, NT * (e - 1) + t + 1)
                    w = W[:, t, e:e + 1] if isinstance(e, int) else W[:, t, bass.ds(e, 1)]
                    nc.vector.scalar_tensor_tensor(out=c.X[:, t, :], in0=c.PS[:, 4 + t % 4, :], scalar=w,
                                                   in1=c.X[:, t, :], op0=ALU.mult, op1=ALU.add).then_inc(added, 1)
            for ch in range(CH):
                split_lo(dve, 0, 0, ch)
            for t in range(NT):
                dve.wait_ge(biases_done, t + 1)
                nc.vector.scalar_tensor_tensor(out=c.X[:, t, :], in0=c.X[:, t, :], scalar=float(res),
                                               in1=c.PS[:, 4 + t % 4, :], op0=ALU.mult, op1=ALU.add).then_inc(res_done, 1)
            dve.wait_ge(res_done, NT)
            body(0, 0, True)
            with dve.Fori(0, NE // 2 - 1) as i:
                body(2 * i + 1, 1, True)
                body(2 * i + 2, 0, True)
            body(NE - 1, 1, False)


def phase_keep(c, keep, back):
    nc = c.nc
    with ExitStack() as ctx:
        block = ctx.enter_context(nc.Block())

        @block.vector
        def _(dve):
            nc.vector.tensor_copy(c.X[:] if back else keep[:], keep[:] if back else c.X[:])


def phase_attn1(c):
    nc = c.nc
    GH = 4
    NG = H // GH
    U = GH * B
    SC = 1.0 / float(np.sqrt(DQK)) / (XS * XS)
    with ExitStack() as ctx:
        sb = lambda name, shape, dt: c.sb(ctx, name, shape, dt)
        sem = lambda name: c.sem(ctx, name)
        st = [sb(f"stage{i}", [P, KD, GH * DQK], F32) for i in range(4)]
        wh = [sb(f"wh{i}", [P, KD, GH * DQK], F16) for i in range(4)]
        wl = [sb(f"wl{i}", [P, KD, GH * DQK], F16) for i in range(4)]
        bq = sb("bq", [P, 3, H], F32)
        bo = sb("bo", [P, D], F32)
        tri = sb("tri", [P, P], BF16)
        tri32 = sb("tri32", [P, P], F32)
        Vh = sb("Vh", [P, NT, GH * DQK], F16)
        Vl = sb("Vl", [P, NT, GH * DQK], F16)
        q32 = sb("q32", [P, 2, 2, S], F32)
        Qh = sb("Qh", [P, 2, 2, S], F16)
        Ql = sb("Ql", [P, 2, 2, S], F16)
        Pr = sb("Pr", [P, QT, S], F32)
        PTh = sb("PTh", [P, 2, KD, S], F16)
        PTl = sb("PTl", [P, 2, KD, S], F16)
        z32 = sb("z32", [P, 2, S], F32)
        Zh = sb("Zh", [P, GH, B * S], F16)
        Zl = sb("Zl", [P, GH, B * S], F16)
        nmax = sb("nmax", [P, 2 * QT], F32)
        nbias = sb("nbias", [P, 2 * QT], F32)
        rsum = sb("rsum", [P, 2 * QT], F32)
        rinv = sb("rinv", [P, 2 * QT], F32)
        w_in = [sem(f"w{i}_in") for i in range(4)]
        bias_in, tri_in, const_done = sem("bias_in"), sem("tri_in"), sem("const_done")
        w_hi, w_lo = sem("w_hi"), sem("w_lo")
        v_done, v_hi, v_lo = sem("v_done"), sem("v_hi"), sem("v_lo")
        qk_done, qk_act, qk_lo = sem("qk_done"), sem("qk_act"), sem("qk_lo")
        s_done, max_done, bias_done = sem("s_done"), sem("max_done"), sem("bias_done")
        exp_done, inv_done, norm_done = sem("exp_done"), sem("inv_done"), sem("norm_done")
        t_done, pt_hi, pt_lo = sem("t_done"), sem("pt_hi"), sem("pt_lo")
        z_done, z_act, z_hi, z_lo = sem("z_done"), sem("z_act"), sem("z_hi"), sem("z_lo")
        o_done, added = sem("o_done"), sem("added")
        block = ctx.enter_context(nc.Block())
        dram = [c.inp[k] for k in ("attn1_WV", "attn1_WQ", "attn1_WK", "attn1_WO")]

        @block.sync
        def _(sp):
            def load(g):
                for i in range(4):
                    need(sp, w_lo, 4 * (g - 1) + i + 1)
                    for h in range(GH):
                        cols = slice(h * DQK, (h + 1) * DQK)
                        head = dram[i][GH * g + h] if isinstance(g, int) else dram[i][bass.ds(GH * g + h, 1)]
                        if i < 3:
                            pat = "(k p) e -> p k e" if isinstance(g, int) else "o (k p) e -> p (o k) e"
                            sp.dma_start(st[i][:, :, cols], head.rearrange(pat, p=P)).then_inc(w_in[i], 16)
                        else:
                            pat = "e d -> e d" if isinstance(g, int) else "o e d -> e (o d)"
                            sp.dma_start(st[i][:, h, :], head.rearrange(pat)).then_inc(w_in[i], 16)
            load(0)
            sp.dma_start(bq[:], c.inp["attn1_bT"]).then_inc(bias_in, 16)
            sp.dma_start(bo[:], c.inp["attn1_bO"].partition_broadcast(P)).then_inc(bias_in, 16)
            sp.dma_start(tri32[:], c.inp["c_tri"]).then_inc(tri_in, 16)
            with sp.Fori(1, NG) as g:
                load(g)

        @block.gpsimd
        def _(pool):
            def norm(u, qt, uq):
                pool.wait_ge(inv_done, QT * u + qt + 1)
                w = (qt + 1) * P
                passed(pool, c.pool_passed, u)
                nc.gpsimd.tensor_scalar(Pr[:, qt, 0:w], Pr[:, qt, 0:w], rinv[:, uq * QT + qt:uq * QT + qt + 1],
                                        None, ALU.mult).then_inc(norm_done, 1)

            def z_parts(g, u, uu):
                hh, b = divmod(uu, B)
                pool.wait_ge(z_act, u + 1)
                if uu == 0:
                    need(pool, o_done, NT * g)
                to = slice(b * S, (b + 1) * S)
                passed(pool, c.pool_passed, u)
                nc.gpsimd.tensor_copy(Zh[:, hh, to], z32[:, uu % 2, :]).then_inc(z_hi, 1)
                pool.wait_ge(z_hi, u + 1)
                nc.gpsimd.tensor_tensor(Zl[:, hh, to], z32[:, uu % 2, :], Zh[:, hh, to], ALU.subtract).then_inc(z_lo, 1)

            def body(g):
                for uu in range(U):
                    u = U * g + uu
                    for qt in range(QT):
                        norm(u, qt, uu % 2)
                    if uu > 0:
                        z_parts(g, u - 1, uu - 1)
                z_parts(g, U * g + U - 1, U - 1)
            body(0)
            with pool.Fori(1, NG) as g:
                body(g)

        @block.tensor
        def _(pe):
            def qk(g, u, uu):
                hh, b = divmod(uu, B)
                for j in range(2):
                    if uu == 0:
                        pe.wait_ge(v_lo, NT * (g + 1))
                    else:
                        pe.wait_ge(qk_act, 4 * (u - 1) + 2 * j + 2)
                    for k in range(KD):
                        w = slice(hh * DQK, (hh + 1) * DQK)
                        last = products(pe, c.PS[:, j, :], (wh[1 + j][:, k, w], wl[1 + j][:, k, w]),
                                        (c.XTh[:, k, b * S:(b + 1) * S], c.XTl[:, k, b * S:(b + 1) * S]),
                                        start=(k == 0), stop=(k == KD - 1))
                    last.then_inc(qk_done, 1)

            def scores(u, q):
                pe.wait_ge(qk_lo, 2 * u + 2)
                for qt in range(QT):
                    need(pe, exp_done, QT * u + qt - 1)
                    w = (qt + 1) * P
                    out = c.PS[:, 2 + qt % 2, 0:w]
                    tok = slice(qt * P, (qt + 1) * P)
                    products(pe, out, (Qh[:, q, 0, tok], Ql[:, q, 0, tok]),
                             (Qh[:, q, 1, 0:w], Ql[:, q, 1, 0:w]), stop=False)
                    pe.matmul(c.PS[:, 2 + qt % 2, w - P:w], c.identb[:], tri[:], start=False, stop=True,
                              skip_group_check=True).then_inc(s_done, 1)

            def turn(u):
                for qt in range(QT):
                    pe.wait_ge(norm_done, QT * u + qt + 1)
                    need(pe, pt_lo, QT * u + qt - 1)
                    for kt in range(qt + 1):
                        last = pe.transpose(c.PS[:, 4 + qt % 2, kt * P:(kt + 1) * P], Pr[:, qt, kt * P:(kt + 1) * P],
                                            c.ident[:])
                    last.then_inc(t_done, 1)

            def values(u, uu):
                hh, b = divmod(uu, B)
                q = uu % 2
                pe.wait_ge(pt_lo, QT * u + QT)
                need(pe, z_act, u - 1)
                for kt in range(KD):
                    v = slice(hh * DQK, (hh + 1) * DQK)
                    last = products(pe, c.PS[:, 6 + q, kt * P:S], (Vh[:, b * QT + kt, v], Vl[:, b * QT + kt, v]),
                                    (PTh[:, q, kt, kt * P:S], PTl[:, q, kt, kt * P:S]),
                                    start=(kt == 0), stop=(kt == KD - 1))
                last.then_inc(z_done, 1)

            def body(g):
                pe.wait_ge(w_lo, 4 * g + 1)
                for t in range(NT):
                    if t < 2:
                        need(pe, added, NT * g)
                    else:
                        pe.wait_ge(v_lo, NT * g + t - 1)
                    for k in range(KD):
                        tok = slice(t * P, (t + 1) * P)
                        last = products(pe, c.PS[:, t % 2, :], (c.XTh[:, k, tok], c.XTl[:, k, tok]),
                                        (wh[0][:, k, :], wl[0][:, k, :]), start=(k == 0), stop=(k == KD - 1))
                    last.then_inc(v_done, 1)
                pe.wait_ge(w_lo, 4 * g + 3)
                qk(g, U * g, 0)
                for uu in range(U):
                    u = U * g + uu
                    scores(u, uu % 2)
                    if uu < U - 1:
                        qk(g, u + 1, uu + 1)
                    turn(u)
                    if uu > 0:
                        values(u - 1, uu - 1)
                values(U * g + U - 1, U - 1)
                pe.wait_ge(w_lo, 4 * g + 4)
                pe.wait_ge(z_lo, U * (g + 1))
                for t in range(NT):
                    if t < 2:
                        pe.wait_ge(qk_act, 4 * U * (g + 1))
                    else:
                        pe.wait_ge(added, NT * g + t - 1)
                    tok = slice(t * P, (t + 1) * P)
                    for hh in range(GH):
                        last = products(pe, c.PS[:, t % 2, :], (Zh[:, hh, tok], Zl[:, hh, tok]),
                                        (wh[3][:, hh, :], wl[3][:, hh, :]), start=(hh == 0), stop=(hh == GH - 1))
                    last.then_inc(o_done, 1)
            pe.wait_ge(const_done, 1)
            body(0)
            with pe.Fori(1, NG) as g:
                body(g)

        @block.scalar
        def _(act):
            def head_bias(i, g, hh):
                return bq[:, i, GH * g + hh:GH * g + hh + 1] if isinstance(g, int) else bq[:, i, bass.ds(GH * g + hh, 1)]

            def qk(g, u, uu):
                hh, q = uu // B, uu % 2
                for j in range(2):
                    act.wait_ge(qk_done, 2 * u + j + 1)
                    need(act, s_done, QT * (u - 1))
                    need(act, qk_lo, 2 * (u - 2) + j + 1)
                    passed(act, c.act_passed, u)
                    nc.scalar.activation(q32[:, q, j, :], c.PS[:, j, :], ACT.Identity, bias=head_bias(j, g, hh),
                                         scale=1.0 / WS).then_inc(qk_act, 1)
                    nc.scalar.activation(Qh[:, q, j, :], c.PS[:, j, :], ACT.Identity, bias=head_bias(j, g, hh),
                                         scale=1.0 / WS).then_inc(qk_act, 1)

            def z_out(g, u, uu):
                act.wait_ge(z_done, u + 1)
                need(act, z_lo, u - 1)
                passed(act, c.act_passed, u)
                nc.scalar.activation(z32[:, uu % 2, :], c.PS[:, 6 + uu % 2, :], ACT.Identity,
                                     bias=head_bias(2, g, uu // B), scale=1.0 / PS_).then_inc(z_act, 1)

            def body(g):
                for t in range(NT):
                    act.wait_ge(v_done, NT * g + t + 1)
                    if t == 0:
                        need(act, z_done, U * g)
                    nc.scalar.activation(Vh[:, t, :], c.PS[:, t % 2, :], ACT.Copy, scale=1.0 / WS).then_inc(v_hi, 1)
                qk(g, U * g, 0)
                for uu in range(U):
                    u = U * g + uu
                    for qt in range(QT):
                        i = (uu % 2) * QT + qt
                        w = (qt + 1) * P
                        act.wait_ge(bias_done, QT * u + qt + 1)
                        need(act, t_done, QT * (u - 1) + qt + 1)
                        nc.scalar.activation(Pr[:, qt, 0:w], c.PS[:, 2 + qt % 2, 0:w], ACT.Exp, bias=nbias[:, i:i + 1],
                                             scale=SC, accum_out=rsum[:, i:i + 1]).then_inc(exp_done, 1)
                    if uu < U - 1:
                        qk(g, u + 1, uu + 1)
                    for qt in range(QT):
                        act.wait_ge(t_done, QT * u + qt + 1)
                        if qt == 0:
                            need(act, z_done, u - 1)
                        nc.scalar.activation(PTh[:, uu % 2, 0:qt + 1, qt * P:(qt + 1) * P],
                                             c.PS[:, 4 + qt % 2, 0:(qt + 1) * P].rearrange("p (k q) -> p k q", q=P),
                                             ACT.Copy, scale=PS_).then_inc(pt_hi, 1)
                    if uu > 0:
                        z_out(g, u - 1, uu - 1)
                z_out(g, U * g + U - 1, U - 1)
            act.wait_ge(const_done, 2)
            body(0)
            with act.Fori(1, NG) as g:
                body(g)

        @block.vector
        def _(dve):
            def qk_lo_part(u, uu):
                q = uu % 2
                for j in range(2):
                    dve.wait_ge(qk_act, 4 * u + 2 * j + 2)
                    nc.vector.tensor_tensor(Ql[:, q, j, :], q32[:, q, j, :], Qh[:, q, j, :],
                                            ALU.subtract).then_inc(qk_lo, 1)

            def inverse(u, uu, qt):
                i = (uu % 2) * QT + qt
                dve.wait_ge(exp_done, QT * u + qt + 1)
                nc.vector.reciprocal(rinv[:, i:i + 1], rsum[:, i:i + 1]).then_inc(inv_done, 1)

            def body(g):
                for i in range(4):
                    dve.wait_ge(w_in[i], 16 * GH * (g + 1))
                    if i == 0:
                        need(dve, z_done, U * g)
                    if i == 3:
                        need(dve, o_done, NT * g)
                    nc.vector.tensor_scalar(wh[i][:], st[i][:], WS, None, ALU.mult).then_inc(w_hi, 1)
                    dve.wait_ge(w_hi, 4 * g + i + 1)
                    flat = lambda a: a[:].rearrange("p k n -> p (k n)")
                    nc.vector.scalar_tensor_tensor(out=flat(wl[i]), in0=flat(st[i]), scalar=WS, in1=flat(wh[i]),
                                                   op0=ALU.mult, op1=ALU.subtract).then_inc(w_lo, 1)
                for t in range(NT):
                    dve.wait_ge(v_hi, NT * g + t + 1)
                    nc.vector.scalar_tensor_tensor(out=Vl[:, t, :], in0=c.PS[:, t % 2, :], scalar=1.0 / WS,
                                                   in1=Vh[:, t, :], op0=ALU.mult, op1=ALU.subtract).then_inc(v_lo, 1)
                qk_lo_part(U * g, 0)
                for uu in range(U):
                    u = U * g + uu
                    for qt in range(QT):
                        i = (uu % 2) * QT + qt
                        dve.wait_ge(s_done, QT * u + qt + 1)
                        nc.vector.tensor_reduce(nmax[:, i:i + 1], c.PS[:, 2 + qt % 2, 0:(qt + 1) * P], AX.X, ALU.max,
                                                negate=True).then_inc(max_done, 1)
                        dve.wait_ge(max_done, QT * u + qt + 1)
                        nc.vector.tensor_scalar(nbias[:, i:i + 1], nmax[:, i:i + 1], SC, None,
                                                ALU.mult).then_inc(bias_done, 1)
                        if qt > 0:
                            inverse(u, uu, qt - 1)
                    inverse(u, uu, QT - 1)
                    if uu < U - 1:
                        qk_lo_part(u + 1, uu + 1)
                    for qt in range(QT):
                        dve.wait_ge(pt_hi, QT * u + qt + 1)
                        part = (slice(None), uu % 2, slice(0, qt + 1), slice(qt * P, (qt + 1) * P))
                        nc.vector.scalar_tensor_tensor(
                            out=PTl[part], in0=c.PS[:, 4 + qt % 2, 0:(qt + 1) * P].rearrange("p (k q) -> p k q", q=P),
                            scalar=PS_, in1=PTh[part], op0=ALU.mult, op1=ALU.subtract).then_inc(pt_lo, 1)
                for t in range(NT):
                    dve.wait_ge(o_done, NT * g + t + 1)
                    need(dve, added, NT * (g - 1) + t + 1)
                    nc.vector.scalar_tensor_tensor(out=c.X[:, t, :], in0=c.PS[:, t % 2, :], scalar=1.0 / (XS * WS),
                                                   in1=c.X[:, t, :], op0=ALU.mult, op1=ALU.add).then_inc(added, 1)
            dve.wait_ge(tri_in, 16)
            nc.vector.tensor_copy(tri[:], tri32[:]).then_inc(const_done, 1)
            dve.wait_ge(bias_in, 32)
            nc.vector.tensor_scalar(bq[:], bq[:], XS, None, ALU.mult).then_inc(const_done, 1)
            for t in range(NT):
                last = nc.vector.tensor_tensor(c.X[:, t, :], c.X[:, t, :], bo[:], ALU.add)
            last.then_inc(const_done, 1)
            dve.wait_ge(const_done, 3)
            body(0)
            with dve.Fori(1, NG) as g:
                body(g)


def phase_attn0(c):
    nc = c.nc
    U = REP * B
    TL = U + B
    SC = 1.0 / float(np.sqrt(DQK)) / (XS * XS)
    NS = 3

    def tiles(uu):
        b, hh = divmod(uu, REP)
        first = b * (REP + 1)
        return [first, first + 1] if hh == 0 else [first + 1 + hh]

    with ExitStack() as ctx:
        sb = lambda name, shape, dt: c.sb(ctx, name, shape, dt)
        sem = lambda name: c.sem(ctx, name)
        wq32 = sb("wq32", [P, KD, REP * DQK], F32)
        wk32 = sb("wk32", [P, KD, DQK], F32)
        wv32 = sb("wv32", [P, KD, KVH * DV], F32)
        wo32 = sb("wo32", [P, KD, D], F32)
        wh = sb("wh", [P, REP + 1, KD, DQK], F16)
        wl = sb("wl", [P, REP + 1, KD, DQK], F16)
        wvh, wvl = sb("wvh", [P, KD, KVH * DV], F16), sb("wvl", [P, KD, KVH * DV], F16)
        woh, wol = sb("woh", [P, KD, D], F16), sb("wol", [P, KD, D], F16)
        rot32, rot = sb("rot32", [P, P], F32), sb("rot", [P, P], F16)
        cos, sin = sb("cos", [P, S], F32), sb("sin", [P, S], F32)
        mask32, mask = sb("mask32", [P, 9 * P], F32), sb("mask", [P, 9 * P], BF16)
        Vh, Vl = sb("Vh", [P, NT, KVH * DV], F16), sb("Vl", [P, NT, KVH * DV], F16)
        Ah, Al = sb("Ah", [P, 2, S], F16), sb("Al", [P, 2, S], F16)
        t1, t2, r32 = sb("t1", [P, 2, S], F32), sb("t2", [P, 2, S], F32), sb("r32", [P, 2, S], F32)
        Kh, Kl = sb("Kh", [P, 2, S], F16), sb("Kl", [P, 2, S], F16)
        Qh, Ql = sb("Qh", [P, 2, S], F16), sb("Ql", [P, 2, S], F16)
        Pr = sb("Pr", [P, QT, NS * P], F32)
        PTh, PTl = sb("PTh", [P, 2, QT, NS * P], F16), sb("PTl", [P, 2, QT, NS * P], F16)
        Z = sb("Z", [P, NT, D], F32)
        ZTh, ZTl = sb("ZTh", [P, KD, B * S], F16), sb("ZTl", [P, KD, B * S], F16)
        nmax, nbias = sb("nmax", [P, 2 * QT], F32), sb("nbias", [P, 2 * QT], F32)
        rsum, rinv = sb("rsum", [P, 2 * QT], F32), sb("rinv", [P, 2 * QT], F32)
        wq_in, wk_in, wv_in, wo_in, const_in = sem("wq_in"), sem("wk_in"), sem("wv_in"), sem("wo_in"), sem("const_in")
        const_done = sem("const_done")
        wv_hi, wv_lo, wo_hi, wo_lo = sem("wv_hi"), sem("wv_lo"), sem("wo_hi"), sem("wo_lo")
        w_hi, w_lo = sem("w_hi"), sem("w_lo")
        v_done, v_hi, v_lo = sem("v_done"), sem("v_hi"), sem("v_lo")
        a_done, a_hi, a_lo, a_cos = sem("a_done"), sem("a_hi"), sem("a_lo"), sem("a_cos")
        r_done, r_sin, r_sum, r_hi, r_lo = sem("r_done"), sem("r_sin"), sem("r_sum"), sem("r_hi"), sem("r_lo")
        s_done, max_done, bias_done = sem("s_done"), sem("max_done"), sem("bias_done")
        exp_done, inv_done = sem("exp_done"), sem("inv_done")
        t_done, pt_hi, pt_lo = sem("t_done"), sem("pt_hi"), sem("pt_lo")
        z_done, z_out = sem("z_done"), sem("z_out")
        zt_done, zt_hi, zt_lo = sem("zt_done"), sem("zt_hi"), sem("zt_lo")
        o_done, added = sem("o_done"), sem("added")
        block = ctx.enter_context(nc.Block())

        @block.sync
        def _(sp):
            def load(g):
                need(sp, w_lo, 10 * g)
                if isinstance(g, int):
                    q, k = c.inp["attn0_wq"][g], c.inp["attn0_wk"][g]
                    pat = "(k p) n -> p k n"
                else:
                    q, k = c.inp["attn0_wq"][bass.ds(g, 1)], c.inp["attn0_wk"][bass.ds(g, 1)]
                    pat = "g (k p) n -> p (g k) n"
                sp.dma_start(wk32[:], k.rearrange(pat, p=P)).then_inc(wk_in, 16)
                sp.dma_start(wq32[:], q.rearrange(pat, p=P)).then_inc(wq_in, 16)
            sp.dma_start(wv32[:], c.inp["attn0_wv"].rearrange("(k p) n -> p k n", p=P)).then_inc(wv_in, 16)
            load(0)
            for to, name in ((rot32, "c_rot"), (cos, "c_cos"), (sin, "c_sin"), (mask32, "c_mask0")):
                sp.dma_start(to[:], c.inp[name]).then_inc(const_in, 16)
            sp.dma_start(wo32[:], c.inp["attn0_wo"].rearrange("(k p) n -> p k n", p=P)).then_inc(wo_in, 16)
            with sp.Fori(1, KVH) as g:
                load(g)

        @block.gpsimd
        def _(pool):
            def rotate(g, uu):
                for tl in tiles(uu):
                    n = TL * g + tl
                    b, hh = divmod(tl, REP + 1)
                    q = tl % 2
                    hi, lo = (Kh[:, b, :], Kl[:, b, :]) if hh == 0 else (Qh[:, uu % 2, :], Ql[:, uu % 2, :])
                    pool.wait_ge(r_sin, n + 1)
                    need(pool, r_lo, n - 1)
                    nc.gpsimd.tensor_tensor(r32[:, q, :], t1[:, q, :], t2[:, q, :], ALU.add).then_inc(r_sum, 1)
                    pool.wait_ge(r_sum, n + 1)
                    need(pool, s_done, QT * (U * g + uu - (REP + 1 if hh == 0 else 1)))
                    passed(pool, c.pool_passed, g)
                    nc.gpsimd.tensor_copy(hi, r32[:, q, :]).then_inc(r_hi, 1)
                    pool.wait_ge(r_hi, n + 1)
                    nc.gpsimd.tensor_tensor(lo, r32[:, q, :], hi, ALU.subtract).then_inc(r_lo, 1)

            def body(g):
                for uu in range(U):
                    rotate(g, uu)
            body(0)
            with pool.Fori(1, KVH) as g:
                body(g)

        @block.tensor
        def _(pe):
            def project(g, uu):
                for tl in tiles(uu):
                    n = TL * g + tl
                    b, hh = divmod(tl, REP + 1)
                    need(pe, a_cos, n - 1)
                    for k in range(KD):
                        last = products(pe, c.PS[:, tl % 2, :], (wh[:, hh, k, :], wl[:, hh, k, :]),
                                        (c.XTh[:, k, b * S:(b + 1) * S], c.XTl[:, k, b * S:(b + 1) * S]),
                                        start=(k == 0), stop=(k == KD - 1))
                    last.then_inc(a_done, 1)

            def rotate(g, uu):
                for tl in tiles(uu):
                    n = TL * g + tl
                    pe.wait_ge(a_lo, n + 1)
                    need(pe, r_sin, n)
                    pe.matmul(c.PS[:, 7, :], rot[:], Ah[:, tl % 2, :], start=True, stop=False)
                    pe.matmul(c.PS[:, 7, :], rot[:], Al[:, tl % 2, :], start=False, stop=True).then_inc(r_done, 1)

            def scores(g, uu):
                u = U * g + uu
                b, hh = divmod(uu, REP)
                pe.wait_ge(r_lo, TL * g + tiles(uu)[-1] + 1)
                for qt in range(QT):
                    need(pe, exp_done, QT * u + qt - 1)
                    bank = c.PS[:, 2 + qt % 2, :]
                    tok = slice(qt * P, (qt + 1) * P)
                    pe.matmul(bank[:, 0:SP0[qt]], c.identb[:], mask[:, SO0[qt]:SO0[qt] + SP0[qt]], start=True,
                              stop=False, skip_group_check=True)
                    runs = [(0, 0, SP0[qt])] if qt < 3 else [(0, 0, P), (P, 2 * P, 2 * P)]
                    for to, of, w in runs:
                        last = products(pe, bank[:, to:to + w], (Qh[:, uu % 2, tok], Ql[:, uu % 2, tok]),
                                        (Kh[:, b, of:of + w], Kl[:, b, of:of + w]), start=False)
                    last.then_inc(s_done, 1)

            def turn(g, uu):
                u = U * g + uu
                for qt in range(QT):
                    pe.wait_ge(exp_done, QT * u + qt + 1)
                    need(pe, pt_lo, QT * u + qt - 1)
                    for i in range(len(KT0[qt])):
                        last = pe.transpose(c.PS[:, 4 + qt % 2, i * P:(i + 1) * P], Pr[:, qt, i * P:(i + 1) * P],
                                            c.ident[:])
                    last.then_inc(t_done, 1)

            def values(g, uu):
                u = U * g + uu
                b = uu // REP
                q = uu % 2
                pe.wait_ge(pt_lo, QT * u + QT)
                need(pe, z_out, QT * u)
                for qt in range(QT):
                    for i, kt in enumerate(KT0[qt]):
                        vh, vl = value_columns(g, b * QT + kt)
                        last = products(pe, c.PS[:, 6, qt * DV:(qt + 1) * DV],
                                        (PTh[:, q, qt, i * P:(i + 1) * P], PTl[:, q, qt, i * P:(i + 1) * P]), (vh, vl),
                                        start=(i == 0), stop=(i == len(KT0[qt]) - 1))
                last.then_inc(z_done, 1)

            def value_columns(g, t):
                if isinstance(g, int):
                    return Vh[:, t, g * DV:(g + 1) * DV], Vl[:, t, g * DV:(g + 1) * DV]
                return Vh[:, t, bass.ds(g * DV, DV)], Vl[:, t, bass.ds(g * DV, DV)]

            pe.wait_ge(wv_lo, 1)
            for t in range(NT):
                need(pe, v_lo, t - 1)
                for k in range(KD):
                    tok = slice(t * P, (t + 1) * P)
                    last = products(pe, c.PS[:, t % 2, 0:KVH * DV], (c.XTh[:, k, tok], c.XTl[:, k, tok]),
                                    (wvh[:, k, :], wvl[:, k, :]), start=(k == 0), stop=(k == KD - 1))
                last.then_inc(v_done, 1)
            pe.wait_ge(const_done, 2)

            def body(g):
                pe.wait_ge(w_lo, 10 * g + 10)
                if isinstance(g, int):
                    pe.wait_ge(v_lo, NT)
                project(g, 0)
                rotate(g, 0)
                project(g, 1)
                for uu in range(U):
                    scores(g, uu)
                    if uu + 1 < U:
                        rotate(g, uu + 1)
                    if uu + 2 < U:
                        project(g, uu + 2)
                    turn(g, uu)
                    if uu > 0:
                        values(g, uu - 1)
                values(g, U - 1)
            body(0)
            with pe.Fori(1, KVH) as g:
                body(g)
            for t in range(NT):
                if t == 0:
                    pe.wait_ge(z_out, QT * U * KVH)
                need(pe, zt_lo, t - 1)
                for k in range(KD):
                    last = pe.transpose(c.PS[:, 4 + t % 2, k * P:(k + 1) * P], Z[:, t, k * P:(k + 1) * P], c.ident[:])
                last.then_inc(zt_done, 1)
            pe.wait_ge(wo_lo, 1)
            for t in range(NT):
                pe.wait_ge(zt_lo, t + 1)
                need(pe, added, t - 1)
                for k in range(KD):
                    tok = slice(t * P, (t + 1) * P)
                    last = products(pe, c.PS[:, t % 2, :], (ZTh[:, k, tok], ZTl[:, k, tok]), (woh[:, k, :], wol[:, k, :]),
                                    start=(k == 0), stop=(k == KD - 1))
                last.then_inc(o_done, 1)

        @block.scalar
        def _(act):
            def a_parts(g, uu):
                for tl in tiles(uu):
                    n = TL * g + tl
                    act.wait_ge(a_done, n + 1)
                    need(act, r_done, n - 1)
                    nc.scalar.activation(Ah[:, tl % 2, :], c.PS[:, tl % 2, :], ACT.Copy, scale=1.0 / WS).then_inc(a_hi, 1)

            for t in range(NT):
                act.wait_ge(v_done, t + 1)
                nc.scalar.activation(Vh[:, t, :], c.PS[:, t % 2, 0:KVH * DV], ACT.Copy, scale=1.0 / WS).then_inc(v_hi, 1)

            def body(g):
                a_parts(g, 0)
                a_parts(g, 1)
                for uu in range(U):
                    u = U * g + uu
                    for qt in range(QT):
                        i = (uu % 2) * QT + qt
                        w = SP0[qt]
                        act.wait_ge(bias_done, QT * u + qt + 1)
                        need(act, t_done, QT * (u - 1) + qt + 1)
                        nc.scalar.activation(Pr[:, qt, 0:w], c.PS[:, 2 + qt % 2, 0:w], ACT.Exp, bias=nbias[:, i:i + 1],
                                             scale=SC, accum_out=rsum[:, i:i + 1]).then_inc(exp_done, 1)
                    if uu + 2 < U:
                        a_parts(g, uu + 2)
                    for qt in range(QT):
                        act.wait_ge(t_done, QT * u + qt + 1)
                        if qt == 0:
                            need(act, z_done, u - 1)
                        nc.scalar.activation(PTh[:, uu % 2, qt, 0:SP0[qt]], c.PS[:, 4 + qt % 2, 0:SP0[qt]],
                                             ACT.Copy, scale=PS_).then_inc(pt_hi, 1)
            body(0)
            with act.Fori(1, KVH) as g:
                body(g)
            for t in range(NT):
                act.wait_ge(zt_done, t + 1)
                nc.scalar.activation(ZTh[:, :, t * P:(t + 1) * P], c.PS[:, 4 + t % 2, :].rearrange("p (k q) -> p k q", k=KD),
                                     ACT.Copy, scale=XS).then_inc(zt_hi, 1)

        @block.vector
        def _(dve):
            def weights(g):
                n = 0
                for hh in range(REP + 1):
                    if hh < 2:
                        dve.wait_ge(wk_in if hh == 0 else wq_in, 16 * (g + 1))
                    if hh == 0:
                        need(dve, a_done, TL * g)
                    for o in range(2):
                        src = wk32[:, :, o::2] if hh == 0 else wq32[:, :, (hh - 1) * DQK + o:hh * DQK:2]
                        to = (slice(None), hh, slice(None), slice(o * 64, o * 64 + 64))
                        nc.vector.tensor_scalar(wh[to], src, WS, None, ALU.mult).then_inc(w_hi, 1)
                        n += 1
                        dve.wait_ge(w_hi, 10 * g + n)
                        nc.vector.scalar_tensor_tensor(out=wl[to], in0=src, scalar=WS, in1=wh[to],
                                                       op0=ALU.mult, op1=ALU.subtract).then_inc(w_lo, 1)

            def a_parts(g, uu):
                for tl in tiles(uu):
                    n = TL * g + tl
                    dve.wait_ge(a_hi, n + 1)
                    nc.vector.scalar_tensor_tensor(out=Al[:, tl % 2, :], in0=c.PS[:, tl % 2, :], scalar=1.0 / WS,
                                                   in1=Ah[:, tl % 2, :], op0=ALU.mult, op1=ALU.subtract).then_inc(a_lo, 1)
                    need(dve, r_sum, n - 1)
                    nc.vector.scalar_tensor_tensor(out=t1[:, tl % 2, :], in0=c.PS[:, tl % 2, :], scalar=1.0 / WS,
                                                   in1=cos[:], op0=ALU.mult, op1=ALU.mult).then_inc(a_cos, 1)

            def sines(g, uu):
                for tl in tiles(uu):
                    n = TL * g + tl
                    dve.wait_ge(r_done, n + 1)
                    dve.wait_ge(a_cos, n + 1)
                    need(dve, r_sum, n - 1)
                    nc.vector.tensor_tensor(t2[:, tl % 2, :], c.PS[:, 7, :], sin[:], ALU.mult).then_inc(r_sin, 1)

            def inverse(u, uu, qt):
                i = (uu % 2) * QT + qt
                dve.wait_ge(exp_done, QT * u + qt + 1)
                nc.vector.reciprocal(rinv[:, i:i + 1], rsum[:, i:i + 1]).then_inc(inv_done, 1)

            def outputs(g, uu):
                u = U * g + uu
                b, hh = divmod(uu, REP)
                dve.wait_ge(z_done, u + 1)
                dve.wait_ge(inv_done, QT * (u + 1))
                for qt in range(QT):
                    i = (uu % 2) * QT + qt
                    first = (REP * g + hh) * DV
                    to = Z[:, b * QT + qt, first:first + DV] if isinstance(g, int) else Z[:, b * QT + qt, bass.ds(first, DV)]
                    nc.vector.tensor_scalar(to, c.PS[:, 6, qt * DV:(qt + 1) * DV], rinv[:, i:i + 1],
                                            1.0 / (PS_ * XS), ALU.mult, ALU.mult).then_inc(z_out, 1)

            def body(g):
                weights(g)
                a_parts(g, 0)
                sines(g, 0)
                a_parts(g, 1)
                for uu in range(U):
                    u = U * g + uu
                    for qt in range(QT):
                        i = (uu % 2) * QT + qt
                        dve.wait_ge(s_done, QT * u + qt + 1)
                        nc.vector.tensor_reduce(nmax[:, i:i + 1], c.PS[:, 2 + qt % 2, 0:SP0[qt]], AX.X, ALU.max,
                                                negate=True).then_inc(max_done, 1)
                        dve.wait_ge(max_done, QT * u + qt + 1)
                        nc.vector.tensor_scalar(nbias[:, i:i + 1], nmax[:, i:i + 1], SC, None,
                                                ALU.mult).then_inc(bias_done, 1)
                        if qt > 0:
                            inverse(u, uu, qt - 1)
                    inverse(u, uu, QT - 1)
                    if uu + 1 < U:
                        sines(g, uu + 1)
                    if uu + 2 < U:
                        a_parts(g, uu + 2)
                    for qt in range(QT):
                        dve.wait_ge(pt_hi, QT * u + qt + 1)
                        nc.vector.scalar_tensor_tensor(
                            out=PTl[:, uu % 2, qt, 0:SP0[qt]], in0=c.PS[:, 4 + qt % 2, 0:SP0[qt]], scalar=PS_,
                            in1=PTh[:, uu % 2, qt, 0:SP0[qt]], op0=ALU.mult, op1=ALU.subtract).then_inc(pt_lo, 1)
                    if uu > 0:
                        outputs(g, uu - 1)
                outputs(g, U - 1)
            dve.wait_ge(wv_in, 16)
            nc.vector.tensor_scalar(wvh[:], wv32[:], WS, None, ALU.mult).then_inc(wv_hi, 1)
            dve.wait_ge(wv_hi, 1)
            nc.vector.scalar_tensor_tensor(out=wvl[:], in0=wv32[:], scalar=WS, in1=wvh[:],
                                           op0=ALU.mult, op1=ALU.subtract).then_inc(wv_lo, 1)
            for t in range(NT):
                dve.wait_ge(v_hi, t + 1)
                nc.vector.scalar_tensor_tensor(out=Vl[:, t, :], in0=c.PS[:, t % 2, 0:KVH * DV], scalar=1.0 / WS,
                                               in1=Vh[:, t, :], op0=ALU.mult, op1=ALU.subtract).then_inc(v_lo, 1)
            dve.wait_ge(const_in, 64)
            nc.vector.tensor_copy(rot[:], rot32[:]).then_inc(const_done, 1)
            nc.vector.tensor_copy(mask[:], mask32[:]).then_inc(const_done, 1)
            body(0)
            with dve.Fori(1, KVH) as g:
                body(g)
            dve.wait_ge(wo_in, 16)
            nc.vector.tensor_scalar(woh[:], wo32[:], WS, None, ALU.mult).then_inc(wo_hi, 1)
            dve.wait_ge(wo_hi, 1)
            nc.vector.scalar_tensor_tensor(out=wol[:], in0=wo32[:], scalar=WS, in1=woh[:],
                                           op0=ALU.mult, op1=ALU.subtract).then_inc(wo_lo, 1)
            for t in range(NT):
                part = (slice(None), slice(None), slice(t * P, (t + 1) * P))
                dve.wait_ge(zt_hi, t + 1)
                nc.vector.scalar_tensor_tensor(out=ZTl[part], in0=c.PS[:, 4 + t % 2, :].rearrange("p (k q) -> p k q", k=KD),
                                               scalar=XS, in1=ZTh[part], op0=ALU.mult, op1=ALU.subtract).then_inc(zt_lo, 1)
            for t in range(NT):
                dve.wait_ge(o_done, t + 1)
                nc.vector.scalar_tensor_tensor(out=c.X[:, t, :], in0=c.PS[:, t % 2, :], scalar=1.0 / (XS * WS),
                                               in1=c.X[:, t, :], op0=ALU.mult, op1=ALU.add).then_inc(added, 1)


def phase_cross0(c):
    nc = c.nc
    SC = 1.0 / float(np.sqrt(D)) / (XS * XS)
    NC = B * CT
    with ExitStack() as ctx:
        sb = lambda name, shape, dt: c.sb(ctx, name, shape, dt)
        sem = lambda name: c.sem(ctx, name)
        C32 = sb("C32", [P, NC, D], F32)
        Ch, Cl = sb("Ch", [P, NC, D], F16), sb("Cl", [P, NC, D], F16)
        CTh, CTl = sb("CTh", [P, KD, B, S2], F16), sb("CTl", [P, KD, B, S2], F16)
        m32 = sb("m32", [P, B, S2 // 4], I32)
        m8 = m32[:].bitcast(U8)
        valid = sb("valid", [P, B], F32)
        mrow, ones = sb("mrow", [1, B, S2], BF16), sb("ones", [1, P], BF16)
        Pr = sb("Pr", [P, 2, S2], F32)
        PTh, PTl = sb("PTh", [P, 2, S2], F16), sb("PTl", [P, 2, S2], F16)
        nmax, nbias = sb("nmax", [P, 2], F32), sb("nbias", [P, 2], F32)
        rsum, rinv, rval = sb("rsum", [P, 2], F32), sb("rinv", [P, 2], F32), sb("rval", [P, 2], F32)
        c_in, m_in = [sem(f"c{b}_in") for b in range(B)], sem("m_in")
        m_done, v_done = sem("m_done"), sem("v_done")
        c_hi, c_lo = sem("c_hi"), sem("c_lo")
        ct_done, ct_hi, ct_lo = sem("ct_done"), sem("ct_hi"), sem("ct_lo")
        stored = sem("stored")
        s_done, max_done, bias_done = sem("s_done"), sem("max_done"), sem("bias_done")
        exp_done, inv_done, val_done = sem("exp_done"), sem("inv_done"), sem("val_done")
        t_done, pt_hi, pt_lo = sem("t_done"), sem("pt_hi"), sem("pt_lo")
        z_done, added = sem("z_done"), sem("added")
        block = ctx.enter_context(nc.Block())

        @block.sync
        def _(sp):
            sp.dma_start(m32[:], c.inp["mask"].partition_broadcast(P)).then_inc(m_in, 16)
            for b in range(B):
                sp.dma_start(C32[:, b * CT:(b + 1) * CT, :],
                             c.inp["ctx"][b].rearrange("(t p) d -> p t d", p=P)).then_inc(c_in[b], 16)
            for b in range(B):
                sp.wait_ge(ct_lo, CT * (b + 1))
                for n, part in enumerate((CTh, CTl)):
                    sp.dma_start(c.ctxT[n][b].rearrange("(k p) s -> p k s", p=P), part[:, :, b, :]).then_inc(stored, 16)
            sp.wait_ge(stored, 64)

        @block.gpsimd
        def _(pool):
            for t in range(NC):
                if t % CT == 0:
                    pool.wait_ge(c_in[t // CT], 16)
                nc.gpsimd.tensor_scalar(Ch[:, t, :], C32[:, t, :], XS, None, ALU.mult).then_inc(c_hi, 1)

        @block.tensor
        def _(pe):
            for t in range(NC):
                if t % CT == 0:
                    pe.wait_ge(c_in[t // CT], 16)
                need(pe, ct_lo, t - 1)
                for k in range(KD):
                    last = pe.transpose(c.PS[:, t % 2, k * P:(k + 1) * P], C32[:, t, k * P:(k + 1) * P], c.ident[:])
                last.then_inc(ct_done, 1)

            def scores(t):
                b = t // QT
                need(pe, exp_done, t - 1)
                tok = slice(t * P, (t + 1) * P)
                for half in range(2):
                    bank = c.PS[:, 2 * (t % 2) + half, :]
                    keys = slice(half * 512, half * 512 + 512)
                    pe.matmul(bank, ones[:], mrow[:, b, keys], start=True, stop=False, skip_group_check=True)
                    for k in range(KD):
                        last = products(pe, bank, (c.XTh[:, k, tok], c.XTl[:, k, tok]),
                                        (CTh[:, k, b, keys], CTl[:, k, b, keys]), start=False, stop=(k == KD - 1))
                last.then_inc(s_done, 1)

            def turn(t):
                pe.wait_ge(exp_done, t + 1)
                need(pe, pt_lo, t)
                for k in range(CT):
                    last = pe.transpose(c.PS[:, 4 + k // 4, (k % 4) * P:(k % 4 + 1) * P], Pr[:, t % 2, k * P:(k + 1) * P],
                                        c.ident[:])
                last.then_inc(t_done, 1)

            def values(t):
                pe.wait_ge(pt_lo, t + 1)
                need(pe, added, t - 1)
                for k in range(CT):
                    at = (t // QT) * CT + k
                    last = products(pe, c.PS[:, 6 + t % 2, :], (PTh[:, t % 2, k * P:(k + 1) * P], PTl[:, t % 2, k * P:(k + 1) * P]),
                                    (Ch[:, at, :], Cl[:, at, :]), start=(k == 0), stop=(k == CT - 1))
                last.then_inc(z_done, 1)

            pe.wait_ge(m_done, 2)
            pe.wait_ge(ct_lo, NC)
            pe.wait_ge(c_lo, NC)
            scores(0)
            for t in range(NT):
                if t + 1 < NT:
                    scores(t + 1)
                turn(t)
                if t > 0:
                    values(t - 1)
            values(NT - 1)

        @block.scalar
        def _(act):
            for t in range(NC):
                act.wait_ge(ct_done, t + 1)
                nc.scalar.activation(CTh[:, :, t // CT, (t % CT) * P:(t % CT + 1) * P],
                                     c.PS[:, t % 2, :].rearrange("p (k q) -> p k q", k=KD),
                                     ACT.Copy, scale=XS).then_inc(ct_hi, 1)
            for t in range(NT):
                q = t % 2
                act.wait_ge(bias_done, t + 1)
                need(act, t_done, t - 1)
                nc.scalar.activation(Pr[:, q, :], c.PS[:, 2 * q:2 * q + 2, :].rearrange("p a b -> p (a b)"), ACT.Exp,
                                     bias=nbias[:, q:q + 1], scale=SC, accum_out=rsum[:, q:q + 1]).then_inc(exp_done, 1)
                act.wait_ge(t_done, t + 1)
                need(act, z_done, t - 1)
                nc.scalar.activation(PTh[:, q, :], c.PS[:, 4:6, :].rearrange("p a b -> p (a b)"), ACT.Copy,
                                     scale=PS_).then_inc(pt_hi, 1)

        @block.vector
        def _(dve):
            dve.wait_ge(m_in, 16)
            nc.vector.tensor_scalar(mrow[:], m8[0:1], 1.0, -NEG, ALU.subtract, ALU.mult).then_inc(m_done, 1)
            nc.vector.memset(ones[:], 1.0).then_inc(m_done, 1)
            nc.vector.tensor_reduce(valid[:], m8, AX.X, ALU.max).then_inc(v_done, 1)
            dve.wait_ge(v_done, 1)
            nc.vector.tensor_scalar(valid[:], valid[:], 1.0 / (PS_ * XS), None, ALU.mult).then_inc(v_done, 1)
            for t in range(NC):
                dve.wait_ge(ct_hi, t + 1)
                to = (slice(None), slice(None), t // CT, slice((t % CT) * P, (t % CT + 1) * P))
                nc.vector.scalar_tensor_tensor(out=CTl[to], in0=c.PS[:, t % 2, :].rearrange("p (k q) -> p k q", k=KD),
                                               scalar=XS, in1=CTh[to], op0=ALU.mult, op1=ALU.subtract).then_inc(ct_lo, 1)
                dve.wait_ge(c_hi, t + 1)
                nc.vector.scalar_tensor_tensor(out=Cl[:, t, :], in0=C32[:, t, :], scalar=XS, in1=Ch[:, t, :],
                                               op0=ALU.mult, op1=ALU.subtract).then_inc(c_lo, 1)

            def maximum(t):
                q = t % 2
                dve.wait_ge(s_done, t + 1)
                nc.vector.tensor_reduce(nmax[:, q:q + 1], c.PS[:, 2 * q:2 * q + 2, :], AX.XY, ALU.max,
                                        negate=True).then_inc(max_done, 1)
                dve.wait_ge(max_done, t + 1)
                nc.vector.tensor_scalar(nbias[:, q:q + 1], nmax[:, q:q + 1], SC, None, ALU.mult).then_inc(bias_done, 1)

            def output(t):
                dve.wait_ge(z_done, t + 1)
                nc.vector.scalar_tensor_tensor(out=c.X[:, t, :], in0=c.PS[:, 6 + t % 2, :], scalar=rval[:, t % 2:t % 2 + 1],
                                               in1=c.X[:, t, :], op0=ALU.mult, op1=ALU.add).then_inc(added, 1)

            dve.wait_ge(v_done, 2)
            maximum(0)
            for t in range(NT):
                q = t % 2
                if t + 1 < NT:
                    maximum(t + 1)
                dve.wait_ge(exp_done, t + 1)
                nc.vector.reciprocal(rinv[:, q:q + 1], rsum[:, q:q + 1]).then_inc(inv_done, 1)
                dve.wait_ge(pt_hi, t + 1)
                nc.vector.scalar_tensor_tensor(out=PTl[:, q, :], in0=c.PS[:, 4:6, :].rearrange("p a b -> p (a b)"),
                                               scalar=PS_, in1=PTh[:, q, :], op0=ALU.mult, op1=ALU.subtract).then_inc(pt_lo, 1)
                if t > 0:
                    output(t - 1)
                dve.wait_ge(inv_done, t + 1)
                nc.vector.tensor_tensor(rval[:, q:q + 1], rinv[:, q:q + 1], valid[:, t // QT:t // QT + 1],
                                        ALU.mult).then_inc(val_done, 1)
                dve.wait_ge(val_done, t + 1)
            output(NT - 1)


def phase_cross1(c):
    nc = c.nc
    SC = 1.0 / float(np.sqrt(DV)) / (XS * XS)
    OFF = S2 - S
    K0 = OFF // P
    R = 3 * DV
    MS = 32.0
    with ExitStack() as ctx:
        sb = lambda name, shape, dt: c.sb(ctx, name, shape, dt)
        sem = lambda name: c.sem(ctx, name)
        KS = [sb(f"KS{b}", [P, H, S2], F16) for b in range(B)]
        QS = [sb(f"QS{b}", [P, H, S], F16) for b in range(B)]
        C32 = sb("C32", [P, 2, D], F32)
        V = sb("V", [P, CT, H, DV + 1], F32)
        tri32, triT32 = sb("tri32", [P, P], F32), sb("triT32", [P, P], F32)
        tri, triT = sb("tri", [P, P], BF16), sb("triT", [P, P], BF16)
        M = sb("M", [P, QT, H], F32)
        mh, ml = sb("mh", [H, S], F16), sb("ml", [H, S], F16)
        PT = sb("PT", [P, 2, CT, S], F32)
        rinv = sb("rinv", [P, QT], F32)
        z = sb("z", [P, 2, QT, DV], F32)
        stack_in = [sem(f"stack{b}_in") for b in range(B)]
        tri_in, const_done = sem("tri_in"), sem("const_done")
        ctx_in, v_done = [sem("ctx0_in"), sem("ctx1_in")], sem("v_done")
        ones_done = sem("ones_done")
        s_done, max_done = sem("s_done"), sem("max_done")
        m_turned, m_hi, m_lo, m_in = sem("m_turned"), sem("m_hi"), sem("m_lo"), sem("m_in")
        e_done, exp_done = sem("e_done"), sem("exp_done")
        z_done, inv_done, z_out, added = sem("z_done"), sem("inv_done"), sem("z_out"), sem("added")
        block = ctx.enter_context(nc.Block())
        PAIRS = CT // 2

        @block.sync
        def _(sp):
            for to, name in ((tri32, "c_tri"), (triT32, "c_triT")):
                sp.dma_start(to[:], c.inp[name]).then_inc(tri_in, 16)
            for b in range(B):
                for h4 in range(4):
                    rows = slice(h4 * DV, (h4 + 1) * DV)
                    for n, (qp, kp) in enumerate(((c.XTh, 0), (c.XTh, 1), (c.XTl, 0))):
                        to = slice(n * DV, (n + 1) * DV)
                        sp.dma_start(QS[b][to, h4::4, :], qp[rows, :, b * S:(b + 1) * S]).then_inc(stack_in[b], 16)
                        src = c.ctxT[kp][b].rearrange("(k f p) s -> f p k s", f=4, p=DV)[h4]
                        sp.dma_start(KS[b][to, h4::4, :], src).then_inc(stack_in[b], 16)
            for b in range(B):
                for t in range(CT):
                    n = b * CT + t
                    need(sp, v_done, n - 1)
                    sp.dma_start(C32[:, n % 2, :], c.inp["ctx"][b, t * P:(t + 1) * P, :]).then_inc(ctx_in[n % 2], 16)
                sp.wait_ge(m_lo, b + 1)
                sp.dma_start(QS[b][R:R + 1, :, :], mh[:]).then_inc(m_in, 16)
                sp.dma_start(QS[b][R + 1:R + 2, :, :], ml[:]).then_inc(m_in, 16)

        @block.gpsimd
        def _(pool):
            nc.gpsimd.memset(V[:], 1.0).then_inc(ones_done, 1)
            pool.wait_ge(ones_done, 1)
            nc.gpsimd.memset(KS[0][R:P, :, :], -MS).then_inc(ones_done, 1)
            pool.wait_ge(ones_done, 2)
            nc.gpsimd.memset(KS[1][R:P, :, :], -MS).then_inc(ones_done, 1)
            pool.wait_ge(ones_done, 3)
            for b in range(B):
                for t in range(CT):
                    n = b * CT + t
                    pool.wait_ge(ctx_in[n % 2], 16 * (n // 2 + 1))
                    if t == 0:
                        need(pool, z_done, H * b)
                    nc.gpsimd.tensor_copy(V[:, t, :, 0:DV], C32[:, n % 2, :].rearrange("p (h e) -> p h e", h=H)).then_inc(v_done, 1)
                for h in range(H):
                    n = b * H + h
                    pool.wait_ge(z_out, n + 1)
                    x = c.X[:, b * QT:(b + 1) * QT, h * DV:(h + 1) * DV]
                    nc.gpsimd.tensor_tensor(x, x, z[:, n % 2], ALU.add).then_inc(added, 1)

        @block.tensor
        def _(pe):
            def maxima(b, h):
                for qt in range(QT):
                    n = QT * (b * H + h) + qt
                    need(pe, max_done, n - 1)
                    w = OFF + (qt + 1) * P
                    lhs = QS[b][0:R, h, qt * P:(qt + 1) * P]
                    pe.matmul(c.PS[:, 2 * (n % 2), :], lhs, KS[b][0:R, h, 0:512], start=True, stop=True)
                    pe.matmul(c.PS[:, 2 * (n % 2) + 1, 0:w - 512], lhs, KS[b][0:R, h, 512:w], start=True, stop=False,
                              skip_group_check=True)
                    pe.matmul(c.PS[:, 2 * (n % 2) + 1, w - 512 - P:w - 512], c.identb[:], tri[:], start=False, stop=True,
                              skip_group_check=True).then_inc(s_done, 1)

            def exps(b, h):
                for pair in range(PAIRS):
                    n = PAIRS * (b * H + h) + pair
                    need(pe, exp_done, n)
                    for i in range(2):
                        kt = 2 * pair + i
                        q0 = max(kt - K0, 0) * P
                        bank = c.PS[:, 4 + i, :]
                        last = pe.matmul(bank[:, q0:S], KS[b][0:R + 2, h, kt * P:(kt + 1) * P], QS[b][0:R + 2, h, q0:S],
                                         start=True, stop=(kt < K0), skip_group_check=True)
                        if kt >= K0:
                            last = pe.matmul(bank[:, q0:q0 + P], c.identb[:], triT[:], start=False, stop=True,
                                             skip_group_check=True)
                    last.then_inc(e_done, 1)

            def values(b, h):
                n = b * H + h
                pe.wait_ge(exp_done, PAIRS * (n + 1))
                pe.wait_ge(v_done, CT * (b + 1))
                need(pe, z_out, n - 1)
                for qt in range(QT):
                    for kt in range(K0 + qt + 1):
                        last = pe.matmul(c.PS[:, 6 + n % 2, qt * (DV + 1):(qt + 1) * (DV + 1)],
                                         PT[:, n % 2, kt, qt * P:(qt + 1) * P], V[:, kt, h, :],
                                         start=(kt == 0), stop=(kt == K0 + qt), skip_group_check=True)
                last.then_inc(z_done, 1)

            pe.wait_ge(const_done, 2)
            pe.wait_ge(stack_in[0], 16 * 24)

            def turn_maxima(b):
                pe.wait_ge(max_done, QT * H * (b + 1))
                for qt in range(QT):
                    last = pe.transpose(c.PS[0:H, 0, qt * P:(qt + 1) * P], M[:, qt, :], c.ident[:])
                last.then_inc(m_turned, 1)

            for h in range(H):
                maxima(0, h)
            turn_maxima(0)
            pe.wait_ge(m_in, 32)
            pe.wait_ge(ones_done, 3)
            pe.wait_ge(stack_in[1], 16 * 24)
            pe.wait_ge(m_hi, 1)
            pe.wait_ge(m_lo, 1)
            for h in range(H):
                exps(0, h)
                maxima(1, h)
                if h > 0:
                    values(0, h - 1)
            turn_maxima(1)
            values(0, H - 1)
            pe.wait_ge(m_in, 64)
            for h in range(H):
                exps(1, h)
                if h > 0:
                    values(1, h - 1)
            values(1, H - 1)

        @block.scalar
        def _(act):
            def exps(b, h):
                for pair in range(PAIRS):
                    n = PAIRS * (b * H + h) + pair
                    q0 = max(2 * pair - K0, 0) * P
                    act.wait_ge(e_done, n + 1)
                    if pair == 0:
                        need(act, z_done, b * H + h - 1)
                    if 2 * pair < K0:
                        nc.scalar.activation(PT[:, (b * H + h) % 2, 2 * pair:2 * pair + 2, :], c.PS[:, 4:6, :], ACT.Exp,
                                             scale=SC).then_inc(exp_done, 1)
                    else:
                        nc.scalar.activation(PT[:, (b * H + h) % 2, 2 * pair, q0:S], c.PS[:, 4, q0:S], ACT.Exp, scale=SC)
                        nc.scalar.activation(PT[:, (b * H + h) % 2, 2 * pair + 1, q0 + P:S], c.PS[:, 5, q0 + P:S], ACT.Exp,
                                             scale=SC).then_inc(exp_done, 1)

            def maxima_hi(b):
                act.wait_ge(m_turned, b + 1)
                need(act, m_in, 32 * b)
                nc.scalar.activation(mh[:], c.PS[0:H, 0, :], ACT.Copy, scale=1.0 / MS).then_inc(m_hi, 1)

            maxima_hi(0)
            for h in range(H):
                exps(0, h)
            maxima_hi(1)
            for h in range(H):
                exps(1, h)

        @block.vector
        def _(dve):
            def maxima(b, h):
                for qt in range(QT):
                    n = QT * (b * H + h) + qt
                    w = OFF + (qt + 1) * P
                    dve.wait_ge(s_done, n + 1)
                    if h == 0 and qt == 0:
                        need(dve, m_turned, b)
                    nc.vector.tensor_reduce(M[:, qt, h:h + 1],
                                            c.PS[:, 2 * (n % 2):2 * (n % 2) + 2, :].rearrange("p a b -> p (a b)")[:, 0:w],
                                            AX.X, ALU.max).then_inc(max_done, 1)

            def maxima_lo(b):
                dve.wait_ge(m_hi, b + 1)
                nc.vector.scalar_tensor_tensor(out=ml[:], in0=c.PS[0:H, 0, :], scalar=1.0 / MS, in1=mh[:],
                                               op0=ALU.mult, op1=ALU.subtract).then_inc(m_lo, 1)

            def output(b, h):
                n = b * H + h
                dve.wait_ge(z_done, n + 1)
                need(dve, added, n - 1)
                bank = c.PS[:, 6 + n % 2, 0:QT * (DV + 1)].rearrange("p (q e) -> p q e", q=QT)
                if n > 0:
                    dve.wait_ge(z_out, n)
                nc.vector.reciprocal(rinv[:].unsqueeze(2), bank[:, :, DV:DV + 1]).then_inc(inv_done, 1)
                dve.wait_ge(inv_done, n + 1)
                nc.vector.tensor_tensor(z[:, n % 2], bank[:, :, 0:DV], rinv[:].unsqueeze(2).broadcast_to([P, QT, DV]),
                                        ALU.mult).then_inc(z_out, 1)

            dve.wait_ge(tri_in, 32)
            nc.vector.tensor_copy(tri[:], tri32[:]).then_inc(const_done, 1)
            nc.vector.tensor_copy(triT[:], triT32[:]).then_inc(const_done, 1)
            for h in range(H):
                maxima(0, h)
            maxima_lo(0)
            for h in range(H):
                maxima(1, h)
                if h > 0:
                    output(0, h - 1)
            maxima_lo(1)
            output(0, H - 1)
            for h in range(H):
                output(1, h)


def ffn0(c, W, norm, gate0, gate1):
    with ExitStack() as ctx:
        c.wide = (c.sb(ctx, "XRh", [P, KD, B * S], F32R), c.sb(ctx, "XRl", [P, KD, B * S], F32R), 1.0)
        keep = c.sb(ctx, "keep", [P, NT, D], F32)
        phase_norm(c, norm=norm, wide=True)
        phase_keep(c, keep, False)
        phase_gate(c, W, *gate0, NE, NE - 2, wide=True)
        phase_ffn0(c, W, 1.0)
        phase_norm(c, norm=False, wide=True)
        phase_gate(c, W, *gate1, NE, NE - 2, wide=True)
        phase_keep(c, keep, True)
        phase_ffn0(c, W, 2.0)


def decoder(nc, inputs, out, phases):
    ctx = ExitStack()
    with ctx:
        c = Core(nc, ctx, inputs, out)
        W = c.sb(ctx, "W", [P, NT, NE], F32)
        phase_load(c)
        for p in phases:
            p(c, W)


PHASES = [
    lambda c, W: phase_norm(c, norm=False),
    lambda c, W: phase_attn0(c),
    lambda c, W: phase_norm(c),
    lambda c, W: phase_cross0(c),
    lambda c, W: ffn0(c, W, True, (c.inp["gate0_w0"], c.inp["gate0_b0"]), (c.inp["gate0_w1"], c.inp["gate0_b1"])),
    lambda c, W: phase_norm(c),
    lambda c, W: phase_attn1(c),
    lambda c, W: phase_norm(c),
    lambda c, W: phase_cross1(c),
    lambda c, W: phase_norm(c),
    lambda c, W: phase_gate(c, W, c.inp["gate1_w"], c.inp["gate1_b"], 7, 3, c.inp["gate1_sel"]),
    lambda c, W: phase_ffn1(c, W),
    lambda c, W: phase_norm(c, transpose=False, store=True),
]


def constants():
    i, j = np.arange(S)[:, None], np.arange(S)[None, :]
    seen = ((j <= i) & (j > i - WIN)) | ((j < FRONT) & (j <= i - WIN))
    window = np.where(seen, 0.0, NEG)
    causal = np.where(np.tril(np.ones((P, P))) > 0, 0.0, NEG)
    freq = 1.0 / 10000.0 ** (np.arange(0, DQK, 2).astype(np.float32) / DQK)
    angle = np.outer(np.arange(S, dtype=np.float32), freq).T
    half = np.eye(DQK // 2)
    zero = np.zeros_like(half)
    out = {
        "c_ident": np.eye(P),
        "c_below": np.tril(np.ones((8, 8)), -1),
        "c_tri": causal,
        "c_triT": causal.T,
        "c_mask0": np.concatenate([window[q * P:(q + 1) * P, k * P:(k + 1) * P] for q in range(QT) for k in KT0[q]], 1),
        "c_cos": np.concatenate([np.cos(angle)] * 2),
        "c_sin": np.concatenate([np.sin(angle)] * 2),
        "c_rot": np.block([[zero, half], [-half, zero]]),
    }
    return {k: np.ascontiguousarray(v, dtype=np.float32) for k, v in out.items()}


def laid_out(v):
    v = {k: np.asarray(a) for k, a in v.items()}

    def by_tile(b):
        return b.reshape(NE, E0 // P, P).transpose(2, 0, 1)

    n = NE - 2
    twice = lambda a: np.stack([a, a])
    out = {
        "x": v["x"].reshape(B * S, D),
        "ctx": v["ctx_2048"],
        "mask": np.ascontiguousarray(v["mask_BxS2_bk0"]).view(np.int32),
        "attn0_wq": v["L0_attn_wq"].reshape(D, KVH, REP * DQK).transpose(1, 0, 2),
        "attn0_wk": v["L0_attn_wk"].reshape(D, KVH, DQK).transpose(1, 0, 2),
        "attn0_wv": v["L0_attn_wv"],
        "attn0_wo": v["L0_attn_wo"],
        "gate0_w0": v["L0_ffn_Wg"][0], "gate0_w1": v["L0_ffn_Wg"][1],
        "gate0_b0": v["L0_ffn_bg"][0], "gate0_b1": v["L0_ffn_bg"][1],
        "ffn0_Wup": np.concatenate([v["L0_ffn_Wup"], v["L0_ffn_Wsu"].reshape(D, 2, E0).transpose(1, 0, 2)]),
        "ffn0_Wsw": np.concatenate([v["L0_ffn_Wsw"], twice(v["L0_ffn_Wsa"])]),
        "ffn0_Wdn": np.concatenate([v["L0_ffn_Wdn"], v["L0_ffn_Wsd"].reshape(2, E0, D)]),
        "ffn0_bup": by_tile(np.concatenate([v["L0_ffn_bup"], v["L0_ffn_bsu"].reshape(2, E0)])),
        "ffn0_bsw": by_tile(np.concatenate([v["L0_ffn_bsw"], twice(v["L0_ffn_bsa"])])),
        "ffn0_bdn": np.concatenate([v["L0_ffn_bdn"], v["L0_ffn_bsd"][None], np.zeros((1, D), np.float32)]),
        "attn1_WQ": v["L1_attn_W_Q"], "attn1_WK": v["L1_attn_W_K"],
        "attn1_WV": v["L1_attn_W_V"], "attn1_WO": v["L1_attn_W_O"],
        "attn1_bT": np.stack([v["L1_attn_b_Q"].T, v["L1_attn_b_K"].T, v["L1_attn_b_V"].T], 1),
        "attn1_bO": v["L1_attn_b_O"],
        "gate1_w": v["L1_ffn_gate_w"], "gate1_b": v["L1_ffn_gate_b"], "gate1_sel": v["L1_ffn_biases"],
        "ffn1_W1": np.concatenate([v["L1_ffn_W1"], v["L1_ffn_Ws1"][None]]),
        "ffn1_Wg": np.concatenate([v["L1_ffn_Wg"], v["L1_ffn_Wsg"][None]]),
        "ffn1_W2": np.concatenate([v["L1_ffn_W2"], v["L1_ffn_Ws2"][None]]),
    }
    return {k: np.ascontiguousarray(a) for k, a in out.items()}


def kernel(**inputs):
    import concourse.bacc as bacc
    from concourse.bass_utils import run_bass_kernel_spmd

    arrays = {**laid_out(inputs), **constants()}
    nc = bacc.Bacc("TRN2", target_bir_lowering=False, num_devices=1)
    dram = {
        k: nc.dram_tensor(f"in_{k}", a.shape, mybir.dt.from_np(a.dtype), kind="ExternalInput").ap()
        for k, a in arrays.items()
    }
    out = nc.dram_tensor("out", (B * S, D), F32, kind="ExternalOutput").ap()
    decoder(nc, dram, out, PHASES)
    got = run_bass_kernel_spmd(nc, [{f"in_{k}": a for k, a in arrays.items()}], core_ids=[0])
    return got.results[0]["out"].reshape(B, S, D)
```

```python
from contextlib import ExitStack

import numpy as np

import concourse.bass as bass
from concourse import mybir

ALU = mybir.AluOpType
ACT = mybir.ActivationFunctionType
AX = mybir.AxisListType
F32 = mybir.dt.float32
F16 = mybir.dt.float16
F32R = mybir.dt.float32r
BF16 = mybir.dt.bfloat16
U8 = mybir.dt.uint8
I32 = mybir.dt.int32

P = 128
B, S, D = 2, 512, 512
NT = B * S // P
KD = D // P
QT = S // P
S2 = 1024
CT = S2 // P
H = 16
DQK = 128
KVH = 4
REP = H // KVH
DV = D // H
WIN, FRONT = 128, 64
NE = 8
E0 = 256
EPS = 1e-5
NEG = -2.0 ** 100

XS = 2.0 ** 5
WS = 2.0 ** 8
PS_ = 2.0 ** 10
SP0 = [P, 2 * P, 3 * P, 3 * P]
SO0 = [0, P, 3 * P, 6 * P]
KT0 = [(0,), (0, 1), (0, 1, 2), (0, 2, 3)]


def need(engine, sem, value):
    if isinstance(value, int) and value <= 0:
        return
    engine.wait_ge(sem, value)


def passed(engine, sem, n):
    if not isinstance(n, int):
        engine.sem_inc(sem, 1)


def products(pe, out, a, b, start=True, stop=True):
    pe.matmul(out, a[0], b[0], start=start, stop=False, skip_group_check=True)
    pe.matmul(out, a[0], b[1], start=False, stop=False, skip_group_check=True)
    return pe.matmul(out, a[1], b[0], start=False, stop=stop, skip_group_check=True)


def plain(a):
    return a.bitcast(F32) if a.dtype == F32R else a


class Core:

    def __init__(self, nc, ctx, inputs, out):
        self.nc, self.ctx, self.inp, self.out = nc, ctx, inputs, out
        self.n = 0
        self.sems = []
        self.X = self.sb(ctx, "X", [P, NT, D], F32)
        self.XTh = self.sb(ctx, "XTh", [P, KD, B * S], F16)
        self.XTl = self.sb(ctx, "XTl", [P, KD, B * S], F16)
        self.ident = self.sb(ctx, "ident", [P, P], F32)
        self.identb = self.sb(ctx, "identb", [P, P], BF16)
        self.PS = ctx.enter_context(nc.psum_tensor("PS", [P, 8, 512], F32))
        self.pool_passed = ctx.enter_context(nc.semaphore("pool_passed"))
        self.act_passed = ctx.enter_context(nc.semaphore("act_passed"))
        self.ctxT = [nc.dram_tensor(f"ctxT_{n}", [B, D, S2], F16, kind="Internal").ap() for n in ("hi", "lo")]

    def sb(self, ctx, name, shape, dt):
        self.n += 1
        return ctx.enter_context(self.nc.sbuf_tensor(f"{name}_{self.n}", shape, dt))

    def sem(self, ctx, name):
        self.n += 1
        if not self.sems:
            ctx.callback(self.free_sems)
        self.sems.append(self.nc.alloc_semaphore(f"{name}_{self.n}"))
        return self.sems[-1]

    def free_sems(self):
        self.nc.clear_and_free_semaphores(self.sems)
        self.nc.all_engine_barrier()
        self.sems = []


def phase_load(c):
    nc = c.nc
    with ExitStack() as ctx:
        x_in = c.sem(ctx, "x_in")
        ident_in = c.sem(ctx, "ident_in")
        block = ctx.enter_context(nc.Block())

        @block.sync
        def _(sp):
            sp.dma_start(c.ident[:], c.inp["c_ident"]).then_inc(ident_in, 16)
            sp.dma_start(c.X[:], c.inp["x"].rearrange("(t p) d -> p t d", p=P)).then_inc(x_in, 16)
            sp.wait_ge(x_in, 16)

        @block.vector
        def _(dve):
            dve.wait_ge(ident_in, 16)
            nc.vector.tensor_copy(c.identb[:], c.ident[:])


def phase_norm(c, norm=True, transpose=True, store=False, wide=False):
    nc = c.nc
    XTh, XTl, scale = c.wide if wide else (c.XTh, c.XTl, XS)
    with ExitStack() as ctx:
        stats = c.sb(ctx, "stats", [P, NT, 6], F32)
        mv = c.sb(ctx, "mv", [P, NT, 2], F32)
        veps = c.sb(ctx, "veps", [P, NT], F32)
        std = c.sb(ctx, "std", [P, NT], F32)
        rstd = c.sb(ctx, "rstd", [P, NT], F32)
        stats_done = c.sem(ctx, "stats_done")
        mv_done = c.sem(ctx, "mv_done")
        veps_done = c.sem(ctx, "veps_done")
        std_done = c.sem(ctx, "std_done")
        rstd_done = c.sem(ctx, "rstd_done")
        normed = c.sem(ctx, "normed")
        turned = c.sem(ctx, "turned")
        hi_done = c.sem(ctx, "hi_done")
        lo_done = c.sem(ctx, "lo_done")
        stored = c.sem(ctx, "stored")
        block = ctx.enter_context(nc.Block())

        @block.vector
        def _(dve):
            if norm:
                for t in range(NT):
                    nc.vector.bn_stats(stats[:, t, :], c.X[:, t, :]).then_inc(stats_done, 1)
                for t in range(NT):
                    dve.wait_ge(stats_done, t + 1)
                    nc.vector.bn_aggr(mv[:, t, :], stats[:, t, :]).then_inc(mv_done, 1)
                dve.wait_ge(mv_done, NT)
                nc.vector.tensor_scalar(veps[:], mv[:, :, 1], EPS, None, ALU.add).then_inc(veps_done, 1)
                dve.wait_ge(std_done, 1)
                nc.vector.reciprocal(rstd[:], std[:]).then_inc(rstd_done, 1)
                dve.wait_ge(rstd_done, 1)
            for t in range(NT + 2):
                if norm and t < NT:
                    nc.vector.tensor_scalar(c.X[:, t, :], c.X[:, t, :], mv[:, t, 0:1], rstd[:, t:t + 1],
                                            ALU.subtract, ALU.mult).then_inc(normed, 1)
                if transpose and t >= 2:
                    u = t - 2
                    dve.wait_ge(hi_done, u + 1)
                    nc.vector.scalar_tensor_tensor(
                        out=XTl[:, :, u * P:(u + 1) * P],
                        in0=c.PS[:, u % 4, :].rearrange("p (k q) -> p k q", k=KD), scalar=scale,
                        in1=plain(XTh[:, :, u * P:(u + 1) * P]), op0=ALU.mult, op1=ALU.subtract).then_inc(lo_done, 1)

        @block.scalar
        def _(act):
            if norm:
                act.wait_ge(veps_done, 1)
                nc.scalar.activation(std[:], veps[:], ACT.Sqrt).then_inc(std_done, 1)
            if transpose:
                for t in range(NT):
                    act.wait_ge(turned, t + 1)
                    nc.scalar.activation(XTh[:, :, t * P:(t + 1) * P],
                                         c.PS[:, t % 4, :].rearrange("p (k q) -> p k q", k=KD),
                                         ACT.Copy, scale=scale).then_inc(hi_done, 1)

        @block.tensor
        def _(pe):
            if transpose:
                for t in range(NT):
                    if norm:
                        pe.wait_ge(normed, t + 1)
                    need(pe, lo_done, t - 3)
                    for k in range(KD):
                        last = pe.transpose(c.PS[:, t % 4, k * P:(k + 1) * P], c.X[:, t, k * P:(k + 1) * P], c.ident[:])
                    last.then_inc(turned, 1)

        @block.sync
        def _(sp):
            if store:
                y = c.out.rearrange("(t p) d -> p t d", p=P)
                for t in range(NT):
                    sp.wait_ge(normed, t + 1)
                    sp.dma_start(y[:, t, :], c.X[:, t, :]).then_inc(stored, 16)
                sp.wait_ge(stored, 16 * NT)


def phase_gate(c, W, wg, bias, n, top, selection_bias=None, wide=False):
    nc = c.nc
    XTh, XTl, xs = c.wide if wide else (c.XTh, c.XTl, XS)
    part, wsc = (F32R, 1.0) if wide else (F16, WS)
    with ExitStack() as ctx:
        w32 = c.sb(ctx, "gate_w32", [P, KD, n], F32)
        wh = c.sb(ctx, "gate_wh", [P, KD, n], part)
        wl = c.sb(ctx, "gate_wl", [P, KD, n], part)
        bb = c.sb(ctx, "gate_bias", [P, n], F32)
        sel_b = c.sb(ctx, "gate_selection", [P, n], F32)
        below = c.sb(ctx, "below", [P, 8, 8], F32)
        G = c.sb(ctx, "G", [P, NT, n], F32)
        K = c.sb(ctx, "keys", [P, NT, n], F32)
        E = c.sb(ctx, "E", [P, NT, n], F32)
        gt = c.sb(ctx, "gt", [P, NT, n, n], F32)
        eq = c.sb(ctx, "eq", [P, NT, n, n], F32)
        rank = c.sb(ctx, "rank", [P, NT, n], F32)
        m = c.sb(ctx, "m", [P, NT], F32)
        total = c.sb(ctx, "total", [P, NT], F32)
        gate_in = c.sem(ctx, "gate_in")
        parts = c.sem(ctx, "gate_parts")
        gates = c.sem(ctx, "gates")
        step = c.sem(ctx, "gate_step")
        shifted = c.sem(ctx, "shifted")
        exp_done = c.sem(ctx, "gate_exp")
        block = ctx.enter_context(nc.Block())

        @block.sync
        def _(sp):
            sp.dma_start(w32[:], wg.rearrange("(k p) n -> p k n", p=P)).then_inc(gate_in, 16)
            sp.dma_start(bb[:], bias.partition_broadcast(P)).then_inc(gate_in, 16)
            sp.dma_start(below[:], c.inp["c_below"].partition_broadcast(P)).then_inc(gate_in, 16)
            sb_ = selection_bias if selection_bias is not None else bias
            sp.dma_start(sel_b[:], sb_.partition_broadcast(P)).then_inc(gate_in, 16)

        @block.tensor
        def _(pe):
            pe.wait_ge(parts, 2)
            for t in range(NT):
                for k in range(KD):
                    tok = slice(t * P, (t + 1) * P)
                    last = products(pe, c.PS[:, 0, t * 8:t * 8 + n], (XTh[:, k, tok], XTl[:, k, tok]),
                                    (wh[:, k, :], wl[:, k, :]), start=(k == 0), stop=(k == KD - 1))
            last.then_inc(gates, 1)

        def over_e(a):
            return a[:].unsqueeze(2).broadcast_to([P, NT, n])

        @block.scalar
        def _(act):
            act.wait_ge(shifted, 1)
            nc.scalar.activation(E[:], E[:], ACT.Exp).then_inc(exp_done, 1)

        @block.vector
        def _(dve):
            count = [0]

            def link(instruction):
                count[0] += 1
                instruction.then_inc(step, 1)
                dve.wait_ge(step, count[0])

            dve.wait_ge(gate_in, 64)
            nc.vector.tensor_scalar(wh[:], w32[:], wsc, None, ALU.mult).then_inc(parts, 1)
            dve.wait_ge(parts, 1)
            nc.vector.scalar_tensor_tensor(out=wl[:], in0=w32[:], scalar=wsc, in1=plain(wh[:]),
                                           op0=ALU.mult, op1=ALU.subtract).then_inc(parts, 1)
            link(nc.vector.memset(W[:], 1.0))
            dve.wait_ge(gates, 1)
            link(nc.vector.tensor_scalar(E[:], c.PS[:, 0, 0:64].rearrange("p (t e) -> p t e", e=8)[:, :, 0:n],
                                         1.0 / (xs * wsc), None, ALU.mult))
            link(nc.vector.tensor_tensor(G[:], E[:], bb[:].unsqueeze(1).broadcast_to([P, NT, n]), ALU.add))
            link(nc.vector.tensor_reduce(m[:], G[:], AX.X, ALU.max))
            nc.vector.tensor_tensor(E[:], G[:], over_e(m), ALU.subtract).then_inc(shifted, 1)
            dve.wait_ge(exp_done, 1)
            if selection_bias is None:
                keys = G
            else:
                keys = K
                link(nc.vector.tensor_reduce(total[:], E[:], AX.X, ALU.add))
                link(nc.vector.reciprocal(m[:], total[:]))
                link(nc.vector.tensor_tensor(E[:], E[:], over_e(m), ALU.mult))
                link(nc.vector.tensor_tensor(K[:], E[:], sel_b[:].unsqueeze(1).broadcast_to([P, NT, n]), ALU.add))
            for i in range(n):
                me = keys[:, :, i:i + 1].broadcast_to([P, NT, n])
                nc.vector.tensor_tensor(gt[:, :, i, :], keys[:], me, ALU.is_gt)
                a = nc.vector.tensor_tensor(eq[:, :, i, :], keys[:], me, ALU.is_equal)
            link(a)
            for t in range(NT):
                a = nc.vector.tensor_tensor(eq[:, t], eq[:, t], below[:, 0:n, 0:n], ALU.mult)
            link(a)
            link(nc.vector.tensor_tensor(gt[:], gt[:], eq[:], ALU.add))
            link(nc.vector.tensor_reduce(rank[:], gt[:], AX.X, ALU.add))
            link(nc.vector.tensor_scalar(rank[:], rank[:], float(top), None, ALU.is_lt))
            link(nc.vector.tensor_tensor(E[:], E[:], rank[:], ALU.mult))
            link(nc.vector.tensor_reduce(total[:], E[:], AX.X, ALU.add))
            link(nc.vector.reciprocal(m[:], total[:]))
            if selection_bias is None:
                n_routed = NE - 2
            else:
                n_routed = NE - 1
            link(nc.vector.tensor_tensor(W[:, :, 0:n_routed], E[:, :, 0:n_routed],
                                         m[:].unsqueeze(2).broadcast_to([P, NT, n_routed]), ALU.mult))


def phase_ffn1(c, W):
    nc = c.nc
    with ExitStack() as ctx:
        st = [c.sb(ctx, f"stage{i}", [P, KD, D], F32) for i in range(3)]
        wh = [[c.sb(ctx, f"wh{i}{q}", [P, KD, D], F16) for i in range(3)] for q in range(2)]
        wl = [[c.sb(ctx, f"wl{i}{q}", [P, KD, D], F16) for i in range(3)] for q in range(2)]
        Gh = c.sb(ctx, "Gh", [P, KD, B * S], F16)
        Gl = c.sb(ctx, "Gl", [P, KD, B * S], F16)
        s32 = c.sb(ctx, "s32", [P, 2, S], F32)
        g32 = c.sb(ctx, "g32", [P, 2, S], F32)
        ws = c.sb(ctx, "ws", [P, NT, NE], F32)
        w_in = [c.sem(ctx, f"w{i}_in") for i in range(3)]
        w_hi = c.sem(ctx, "w_hi")
        w_lo = c.sem(ctx, "w_lo")
        ws_done = c.sem(ctx, "ws_done")
        up_done = c.sem(ctx, "up_done")
        silu_done = c.sem(ctx, "silu_done")
        g_done = c.sem(ctx, "g_done")
        g_hi = c.sem(ctx, "g_hi")
        g_lo = c.sem(ctx, "g_lo")
        down_done = c.sem(ctx, "down_done")
        added = c.sem(ctx, "added")
        block = ctx.enter_context(nc.Block())
        UP = B * KD
        CH = 3 * KD
        dram = [c.inp[k] for k in ("ffn1_W1", "ffn1_Wg", "ffn1_W2")]

        @block.sync
        def _(sp):
            def load(e):
                for i in range(3):
                    need(sp, w_lo, CH * (e - 1) + KD * (i + 1))
                    sp.dma_start(st[i][:], dram[i][e].rearrange("(k p) n -> p k n", p=P)
                                 if isinstance(e, int) else
                                 dram[i][bass.ds(e, 1)].rearrange("e (k p) n -> p (e k) n", p=P)).then_inc(w_in[i], 16)
            load(0)
            with sp.Fori(1, NE) as e:
                load(e)

        def split_hi(dve, e, q, ch):
            i, k = divmod(ch, KD)
            if k == 0:
                dve.wait_ge(w_in[i], 16 * (e + 1))
                need(dve, down_done, NT * (e - 1))
            nc.vector.tensor_scalar(wh[q][i][:, k, :], st[i][:, k, :], WS, None, ALU.mult).then_inc(w_hi, 1)

        def split_lo(dve, e, q, ch):
            i, k = divmod(ch, KD)
            dve.wait_ge(w_hi, CH * e + ch + 1)
            nc.vector.scalar_tensor_tensor(out=wl[q][i][:, k, :], in0=st[i][:, k, :], scalar=WS,
                                           in1=wh[q][i][:, k, :], op0=ALU.mult, op1=ALU.subtract).then_inc(w_lo, 1)

        def at(buffer, m):
            return buffer[:, m % KD, (m // KD) * S:(m // KD + 1) * S]

        @block.tensor
        def _(pe):
            def body(e, q):
                pe.wait_ge(w_lo, CH * e + 2 * KD)
                for m in range(UP):
                    b, ht = divmod(m, KD)
                    need(pe, g_done, UP * e + m - 1)
                    for i in range(2):
                        for k in range(KD):
                            last = products(pe, c.PS[:, 2 * (m % 2) + i, :],
                                            (wh[q][i][:, k, ht * P:(ht + 1) * P], wl[q][i][:, k, ht * P:(ht + 1) * P]),
                                            (c.XTh[:, k, b * S:(b + 1) * S], c.XTl[:, k, b * S:(b + 1) * S]),
                                            start=(k == 0), stop=(k == KD - 1))
                    last.then_inc(up_done, 1)
                pe.wait_ge(w_lo, CH * (e + 1))
                for t in range(NT):
                    if t % QT == 0:
                        pe.wait_ge(g_lo, UP * e + KD * (t // QT + 1))
                    need(pe, added, NT * e + t - 3)
                    for k in range(KD):
                        tok = slice(t * P, (t + 1) * P)
                        last = products(pe, c.PS[:, 4 + t % 4, :], (Gh[:, k, tok], Gl[:, k, tok]),
                                        (wh[q][2][:, k, :], wl[q][2][:, k, :]), start=(k == 0), stop=(k == KD - 1))
                    last.then_inc(down_done, 1)
            body(0, 0)
            with pe.Fori(0, NE // 2 - 1) as i:
                body(2 * i + 1, 1)
                body(2 * i + 2, 0)
            body(NE - 1, 1)

        @block.scalar
        def _(act):
            def g_part(e, m):
                act.wait_ge(g_done, UP * e + m + 1)
                if m == 0:
                    need(act, down_done, NT * e)
                nc.scalar.activation(at(Gh, m), g32[:, m % 2, :], ACT.Copy).then_inc(g_hi, 1)

            def body(e):
                for m in range(UP):
                    n = UP * e + m
                    act.wait_ge(up_done, n + 1)
                    need(act, g_done, n - 1)
                    nc.scalar.activation(s32[:, m % 2, :], c.PS[:, 2 * (m % 2), :], ACT.Silu,
                                         scale=1.0 / (XS * WS)).then_inc(silu_done, 1)
                    if m > 0:
                        g_part(e, m - 1)
                g_part(e, UP - 1)
            body(0)
            with act.Fori(1, NE) as e:
                body(e)

        @block.vector
        def _(dve):
            def g_part(e, m):
                dve.wait_ge(g_hi, UP * e + m + 1)
                nc.vector.tensor_tensor(at(Gl, m), g32[:, m % 2, :], at(Gh, m), ALU.subtract).then_inc(g_lo, 1)

            def body(e, q, more):
                for m in range(UP):
                    n = UP * e + m
                    dve.wait_ge(silu_done, n + 1)
                    need(dve, g_lo, n - 1)
                    nc.vector.scalar_tensor_tensor(out=g32[:, m % 2, :], in0=c.PS[:, 2 * (m % 2) + 1, :],
                                                   scalar=1.0 / WS, in1=s32[:, m % 2, :],
                                                   op0=ALU.mult, op1=ALU.mult).then_inc(g_done, 1)
                    mine = range(CH * m // UP, CH * (m + 1) // UP) if more else ()
                    for ch in mine:
                        split_hi(dve, e + 1, 1 - q, ch)
                    if m > 0:
                        g_part(e, m - 1)
                    for ch in mine:
                        split_lo(dve, e + 1, 1 - q, ch)
                g_part(e, UP - 1)
                for t in range(NT):
                    dve.wait_ge(down_done, NT * e + t + 1)
                    need(dve, added, NT * (e - 1) + t + 1)
                    w = ws[:, t, e:e + 1] if isinstance(e, int) else ws[:, t, bass.ds(e, 1)]
                    nc.vector.scalar_tensor_tensor(out=c.X[:, t, :], in0=c.PS[:, 4 + t % 4, :], scalar=w,
                                                   in1=c.X[:, t, :], op0=ALU.mult, op1=ALU.add).then_inc(added, 1)
            for ch in range(CH):
                split_hi(dve, 0, 0, ch)
                if ch > 0:
                    split_lo(dve, 0, 0, ch - 1)
            split_lo(dve, 0, 0, CH - 1)
            nc.vector.tensor_scalar(ws[:], W[:], 1.0 / (XS * WS), None, ALU.mult).then_inc(ws_done, 1)
            dve.wait_ge(ws_done, 1)
            body(0, 0, True)
            with dve.Fori(0, NE // 2 - 1) as i:
                body(2 * i + 1, 1, True)
                body(2 * i + 2, 0, True)
            body(NE - 1, 1, False)


def phase_ffn0(c, W, res):
    nc = c.nc
    XTh, XTl, _ = c.wide
    M0 = E0 // P
    with ExitStack() as ctx:
        st = [c.sb(ctx, f"stage{i}", [P, k, n], F32) for i, (k, n) in enumerate([(KD, E0), (M0, E0), (M0, D)])]
        wh = [[c.sb(ctx, f"wh{i}{q}", [P, k, n], F32R) for i, (k, n) in enumerate([(KD, E0), (M0, E0), (M0, D)])] for q in range(2)]
        wl = [[c.sb(ctx, f"wl{i}{q}", [P, k, n], F32R) for i, (k, n) in enumerate([(KD, E0), (M0, E0), (M0, D)])] for q in range(2)]
        bup = c.sb(ctx, "bup", [P, NE, M0], F32)
        bsw = c.sb(ctx, "bsw", [P, NE, M0], F32)
        bdn = c.sb(ctx, "bdn", [NE, D], F32)
        WT = c.sb(ctx, "WT", [NE, NT, P], F32)
        Hh = c.sb(ctx, "Hh", [P, M0, B * S], F32R)
        Hl = c.sb(ctx, "Hl", [P, M0, B * S], F32R)
        Gh = c.sb(ctx, "Gh", [P, M0, B * S], F32R)
        Gl = c.sb(ctx, "Gl", [P, M0, B * S], F32R)
        UP = B * M0
        h32 = c.sb(ctx, "h32", [P, UP, S], F32)
        s32 = c.sb(ctx, "s32", [P, 2, S], F32)
        g32 = c.sb(ctx, "g32", [P, UP, S], F32)
        w_in = [c.sem(ctx, f"w{i}_in") for i in range(3)]
        bias_in = c.sem(ctx, "bias_in")
        w_hi = c.sem(ctx, "w_hi")
        w_lo = c.sem(ctx, "w_lo")
        wt_turned = c.sem(ctx, "wt_turned")
        wt_done = c.sem(ctx, "wt_done")
        res_done = c.sem(ctx, "res_done")
        biases_done = c.sem(ctx, "biases_done")
        up_done = c.sem(ctx, "up_done")
        h_done = c.sem(ctx, "h_done")
        h_hi = c.sem(ctx, "h_hi")
        h_lo = c.sem(ctx, "h_lo")
        sw_done = c.sem(ctx, "sw_done")
        silu_done = c.sem(ctx, "silu_done")
        g_done = c.sem(ctx, "g_done")
        g_hi = c.sem(ctx, "g_hi")
        g_lo = c.sem(ctx, "g_lo")
        down_done = c.sem(ctx, "down_done")
        added = c.sem(ctx, "added")
        block = ctx.enter_context(nc.Block())
        dram = [c.inp[k] for k in ("ffn0_Wup", "ffn0_Wsw", "ffn0_Wdn")]
        parts = [(i, h) for i in range(3) for h in range(2 if i != 1 else 1)]
        CH = len(parts)
        LAST = [2, 3, 5]

        def piece(buffer, ch):
            i, h = parts[ch]
            flat = buffer[i][:].rearrange("p k n -> p (k n)")
            return flat[:, h * 512:(h + 1) * 512]

        def col(a, e, m):
            return a[:, e, m:m + 1] if isinstance(e, int) else a[:, bass.ds(e, 1), m:m + 1].rearrange("p e m -> p (e m)")

        @block.sync
        def _(sp):
            def load(e):
                for i in range(3):
                    need(sp, w_lo, CH * (e - 1) + LAST[i])
                    sp.dma_start(st[i][:], dram[i][e].rearrange("(k p) n -> p k n", p=P)
                                 if isinstance(e, int) else
                                 dram[i][bass.ds(e, 1)].rearrange("e (k p) n -> p (e k) n", p=P)).then_inc(w_in[i], 16)
            load(0)
            sp.dma_start(bup[:], c.inp["ffn0_bup"]).then_inc(bias_in, 16)
            sp.dma_start(bsw[:], c.inp["ffn0_bsw"]).then_inc(bias_in, 16)
            sp.dma_start(bdn[:], c.inp["ffn0_bdn"]).then_inc(bias_in, 16)
            with sp.Fori(1, NE) as e:
                load(e)

        def split_hi(dve, e, q, ch):
            i, h = parts[ch]
            if h == 0:
                dve.wait_ge(w_in[i], 16 * (e + 1))
                need(dve, down_done, NT * (e - 1))
            nc.vector.tensor_copy(piece(wh[q], ch), piece(st, ch)).then_inc(w_hi, 1)

        def at(buffer, m):
            return buffer[:, m % M0, (m // M0) * S:(m // M0 + 1) * S]

        @block.gpsimd
        def _(pool):
            def split_lo(e, q, ch):
                pool.wait_ge(w_hi, CH * e + ch + 1)
                nc.gpsimd.tensor_tensor(piece(wl[q], ch), piece(st, ch), plain(piece(wh[q], ch)),
                                        ALU.subtract).then_inc(w_lo, 1)

            def body(e, q, more):
                if more:
                    for ch in range(CH):
                        split_lo(e + 1, 1 - q, ch)
                for m in range(UP):
                    n = UP * e + m
                    pool.wait_ge(g_hi, n + 1)
                    nc.gpsimd.tensor_tensor(at(Gl, m), g32[:, m, :], plain(at(Gh, m)), ALU.subtract).then_inc(g_lo, 1)
            for ch in range(CH):
                split_lo(0, 0, ch)
            body(0, 0, True)
            with pool.Fori(0, NE // 2 - 1) as i:
                body(2 * i + 1, 1, True)
                body(2 * i + 2, 0, True)
            body(NE - 1, 1, False)

        @block.tensor
        def _(pe):
            pe.wait_ge(bias_in, 48)
            for t in range(NT):
                last = pe.transpose(c.PS[0:NE, t // 4, (t % 4) * P:(t % 4 + 1) * P], W[:, t, :], c.ident[:])
            last.then_inc(wt_turned, 1)
            pe.wait_ge(wt_done, 1)
            for t in range(NT):
                need(pe, res_done, t - 3)
                pe.matmul(c.PS[:, 4 + t % 4, :], WT[:, t, :], bdn[:], start=True, stop=True).then_inc(biases_done, 1)

            def body(e, q):
                pe.wait_ge(w_lo, CH * e + LAST[0])
                for m in range(UP):
                    b, mt = divmod(m, M0)
                    need(pe, h_hi, UP * e + m - 1)
                    for k in range(KD):
                        w = slice(mt * P, (mt + 1) * P)
                        last = products(pe, c.PS[:, m % 2, :], (wh[q][0][:, k, w], wl[q][0][:, k, w]),
                                        (XTh[:, k, b * S:(b + 1) * S], XTl[:, k, b * S:(b + 1) * S]),
                                        start=(k == 0), stop=(k == KD - 1))
                    last.then_inc(up_done, 1)
                pe.wait_ge(w_lo, CH * e + LAST[1])
                for m in range(UP):
                    b, mt = divmod(m, M0)
                    pe.wait_ge(h_lo, UP * e + M0 * (b + 1))
                    need(pe, silu_done, UP * e + m - 1)
                    for k in range(M0):
                        w = slice(mt * P, (mt + 1) * P)
                        last = products(pe, c.PS[:, 2 + m % 2, :], (wh[q][1][:, k, w], wl[q][1][:, k, w]),
                                        (Hh[:, k, b * S:(b + 1) * S], Hl[:, k, b * S:(b + 1) * S]),
                                        start=(k == 0), stop=(k == M0 - 1))
                    last.then_inc(sw_done, 1)
                pe.wait_ge(w_lo, CH * e + LAST[2])
                if isinstance(e, int) and e == 0:
                    pe.wait_ge(res_done, NT)
                for t in range(NT):
                    if t % QT == 0:
                        pe.wait_ge(g_lo, UP * e + M0 * (t // QT + 1))
                    need(pe, added, NT * e + t - 3)
                    for k in range(M0):
                        tok = slice(t * P, (t + 1) * P)
                        last = products(pe, c.PS[:, 4 + t % 4, :], (Gh[:, k, tok], Gl[:, k, tok]),
                                        (wh[q][2][:, k, :], wl[q][2][:, k, :]), start=(k == 0), stop=(k == M0 - 1))
                    last.then_inc(down_done, 1)
            body(0, 0)
            with pe.Fori(0, NE // 2 - 1) as i:
                body(2 * i + 1, 1)
                body(2 * i + 2, 0)
            body(NE - 1, 1)

        @block.scalar
        def _(act):
            def g_part(e, m):
                act.wait_ge(g_done, UP * e + m + 1)
                if m == 0:
                    need(act, down_done, NT * e)
                nc.scalar.activation(at(Gh, m), g32[:, m, :], ACT.Copy).then_inc(g_hi, 1)

            def body(e):
                for m in range(UP):
                    n = UP * e + m
                    act.wait_ge(up_done, n + 1)
                    if m == 0:
                        need(act, sw_done, UP * e)
                    need(act, g_done, n - UP + 1)
                    passed(act, c.act_passed, e)
                    nc.scalar.activation(h32[:, m, :], c.PS[:, m % 2, :], ACT.Identity,
                                         bias=col(bup, e, m % M0)).then_inc(h_done, 1)
                    nc.scalar.activation(at(Hh, m), c.PS[:, m % 2, :], ACT.Identity,
                                         bias=col(bup, e, m % M0)).then_inc(h_hi, 1)
                for m in range(UP):
                    n = UP * e + m
                    act.wait_ge(sw_done, n + 1)
                    need(act, g_done, n - 1)
                    passed(act, c.act_passed, e)
                    nc.scalar.activation(s32[:, m % 2, :], c.PS[:, 2 + m % 2, :], ACT.Silu,
                                         bias=col(bsw, e, m % M0)).then_inc(silu_done, 1)
                    if m > 0:
                        g_part(e, m - 1)
                g_part(e, UP - 1)
            act.wait_ge(bias_in, 48)
            act.wait_ge(wt_turned, 1)
            nc.scalar.activation(WT[:].rearrange("e t p -> e (t p)"), c.PS[0:NE, 0:2, :].rearrange("e a b -> e (a b)"),
                                 ACT.Copy).then_inc(wt_done, 1)
            act.wait_ge(wt_done, 1)
            body(0)
            with act.Fori(1, NE) as e:
                body(e)

        @block.vector
        def _(dve):
            def body(e, q, more):
                for m in range(UP):
                    dve.wait_ge(h_hi, UP * e + m + 1)
                    nc.vector.tensor_tensor(at(Hl, m), h32[:, m, :], plain(at(Hh, m)), ALU.subtract).then_inc(h_lo, 1)
                if more:
                    for ch in range(CH):
                        split_hi(dve, e + 1, 1 - q, ch)
                for m in range(UP):
                    n = UP * e + m
                    dve.wait_ge(silu_done, n + 1)
                    need(dve, g_lo, n - UP + 1)
                    nc.vector.tensor_tensor(g32[:, m, :], h32[:, m, :], s32[:, m % 2, :], ALU.mult).then_inc(g_done, 1)
                for t in range(NT):
                    dve.wait_ge(down_done, NT * e + t + 1)
                    need(dve, added, NT * (e - 1) + t + 1)
                    w = W[:, t, e:e + 1] if isinstance(e, int) else W[:, t, bass.ds(e, 1)]
                    nc.vector.scalar_tensor_tensor(out=c.X[:, t, :], in0=c.PS[:, 4 + t % 4, :], scalar=w,
                                                   in1=c.X[:, t, :], op0=ALU.mult, op1=ALU.add).then_inc(added, 1)
            for ch in range(CH):
                split_hi(dve, 0, 0, ch)
            for t in range(NT):
                dve.wait_ge(biases_done, t + 1)
                nc.vector.scalar_tensor_tensor(out=c.X[:, t, :], in0=c.X[:, t, :], scalar=float(res),
                                               in1=c.PS[:, 4 + t % 4, :], op0=ALU.mult, op1=ALU.add).then_inc(res_done, 1)
            dve.wait_ge(res_done, NT)
            body(0, 0, True)
            with dve.Fori(0, NE // 2 - 1) as i:
                body(2 * i + 1, 1, True)
                body(2 * i + 2, 0, True)
            body(NE - 1, 1, False)


def phase_keep(c, keep, back):
    nc = c.nc
    with ExitStack() as ctx:
        block = ctx.enter_context(nc.Block())

        @block.vector
        def _(dve):
            nc.vector.tensor_copy(c.X[:] if back else keep[:], keep[:] if back else c.X[:])


def phase_attn1(c):
    nc = c.nc
    GH = 4
    NG = H // GH
    U = GH * B
    SC = 1.0 / float(np.sqrt(DQK)) / (XS * XS)
    with ExitStack() as ctx:
        sb = lambda name, shape, dt: c.sb(ctx, name, shape, dt)
        sem = lambda name: c.sem(ctx, name)
        st = [sb(f"stage{i}", [P, KD, GH * DQK], F32) for i in range(4)]
        wh = [sb(f"wh{i}", [P, KD, GH * DQK], F16) for i in range(4)]
        wl = [sb(f"wl{i}", [P, KD, GH * DQK], F16) for i in range(4)]
        bq = sb("bq", [P, 3, H], F32)
        bo = sb("bo", [P, D], F32)
        tri = sb("tri", [P, P], BF16)
        tri32 = sb("tri32", [P, P], F32)
        Vh = sb("Vh", [P, NT, GH * DQK], F16)
        Vl = sb("Vl", [P, NT, GH * DQK], F16)
        q32 = sb("q32", [P, 2, 2, S], F32)
        Qh = sb("Qh", [P, 2, 2, S], F16)
        Ql = sb("Ql", [P, 2, 2, S], F16)
        Pr = sb("Pr", [P, QT, S], F32)
        PTh = sb("PTh", [P, 2, KD, S], F16)
        PTl = sb("PTl", [P, 2, KD, S], F16)
        z32 = sb("z32", [P, 2, S], F32)
        Zh = sb("Zh", [P, GH, B * S], F16)
        Zl = sb("Zl", [P, GH, B * S], F16)
        nmax = sb("nmax", [P, 2 * QT], F32)
        nbias = sb("nbias", [P, 2 * QT], F32)
        rsum = sb("rsum", [P, 2 * QT], F32)
        rinv = sb("rinv", [P, 2 * QT], F32)
        w_in = [sem(f"w{i}_in") for i in range(4)]
        bias_in, tri_in, const_done = sem("bias_in"), sem("tri_in"), sem("const_done")
        w_hi, w_lo = sem("w_hi"), sem("w_lo")
        v_done, v_hi, v_lo = sem("v_done"), sem("v_hi"), sem("v_lo")
        qk_done, qk_act, qk_lo = sem("qk_done"), sem("qk_act"), sem("qk_lo")
        s_done, max_done, bias_done = sem("s_done"), sem("max_done"), sem("bias_done")
        exp_done, inv_done, norm_done = sem("exp_done"), sem("inv_done"), sem("norm_done")
        t_done, pt_hi, pt_lo = sem("t_done"), sem("pt_hi"), sem("pt_lo")
        z_done, z_act, z_lo = sem("z_done"), sem("z_act"), sem("z_lo")
        o_done, added = sem("o_done"), sem("added")
        block = ctx.enter_context(nc.Block())
        dram = [c.inp[k] for k in ("attn1_WV", "attn1_WQ", "attn1_WK", "attn1_WO")]

        @block.sync
        def _(sp):
            def load(g):
                for i in range(4):
                    need(sp, w_lo, 4 * (g - 1) + i + 1)
                    for h in range(GH):
                        cols = slice(h * DQK, (h + 1) * DQK)
                        head = dram[i][GH * g + h] if isinstance(g, int) else dram[i][bass.ds(GH * g + h, 1)]
                        if i < 3:
                            pat = "(k p) e -> p k e" if isinstance(g, int) else "o (k p) e -> p (o k) e"
                            sp.dma_start(st[i][:, :, cols], head.rearrange(pat, p=P)).then_inc(w_in[i], 16)
                        else:
                            pat = "e d -> e d" if isinstance(g, int) else "o e d -> e (o d)"
                            sp.dma_start(st[i][:, h, :], head.rearrange(pat)).then_inc(w_in[i], 16)
            load(0)
            sp.dma_start(bq[:], c.inp["attn1_bT"]).then_inc(bias_in, 16)
            sp.dma_start(bo[:], c.inp["attn1_bO"].partition_broadcast(P)).then_inc(bias_in, 16)
            sp.dma_start(tri32[:], c.inp["c_tri"]).then_inc(tri_in, 16)
            with sp.Fori(1, NG) as g:
                load(g)

        @block.gpsimd
        def _(pool):
            def z_part(g, u, uu):
                hh, b = divmod(uu, B)
                to = slice(b * S, (b + 1) * S)
                pool.wait_ge(z_act, 2 * u + 2)
                nc.gpsimd.tensor_tensor(Zl[:, hh, to], z32[:, uu % 2, :], Zh[:, hh, to], ALU.subtract).then_inc(z_lo, 1)

            def body(g):
                for uu in range(U):
                    z_part(g, U * g + uu, uu)
            body(0)
            with pool.Fori(1, NG) as g:
                body(g)

        @block.tensor
        def _(pe):
            def qk(g, u, uu):
                hh, b = divmod(uu, B)
                for j in range(2):
                    if uu == 0:
                        pe.wait_ge(v_lo, NT * (g + 1))
                    else:
                        pe.wait_ge(qk_act, 4 * (u - 1) + 2 * j + 2)
                    for k in range(KD):
                        w = slice(hh * DQK, (hh + 1) * DQK)
                        last = products(pe, c.PS[:, j, :], (wh[1 + j][:, k, w], wl[1 + j][:, k, w]),
                                        (c.XTh[:, k, b * S:(b + 1) * S], c.XTl[:, k, b * S:(b + 1) * S]),
                                        start=(k == 0), stop=(k == KD - 1))
                    last.then_inc(qk_done, 1)

            def scores(u, q):
                pe.wait_ge(qk_lo, 2 * u + 2)
                for qt in range(QT):
                    need(pe, exp_done, QT * u + qt - 1)
                    w = (qt + 1) * P
                    out = c.PS[:, 2 + qt % 2, 0:w]
                    tok = slice(qt * P, (qt + 1) * P)
                    products(pe, out, (Qh[:, q, 0, tok], Ql[:, q, 0, tok]),
                             (Qh[:, q, 1, 0:w], Ql[:, q, 1, 0:w]), stop=False)
                    pe.matmul(c.PS[:, 2 + qt % 2, w - P:w], c.identb[:], tri[:], start=False, stop=True,
                              skip_group_check=True).then_inc(s_done, 1)

            def turn(u):
                for qt in range(QT):
                    pe.wait_ge(norm_done, QT * u + qt + 1)
                    need(pe, pt_lo, QT * u + qt - 1)
                    for kt in range(qt + 1):
                        last = pe.transpose(c.PS[:, 4 + qt % 2, kt * P:(kt + 1) * P], Pr[:, qt, kt * P:(kt + 1) * P],
                                            c.ident[:])
                    last.then_inc(t_done, 1)

            def values(u, uu):
                hh, b = divmod(uu, B)
                q = uu % 2
                pe.wait_ge(pt_lo, QT * u + QT)
                need(pe, z_act, 2 * (u - 1))
                for kt in range(KD):
                    v = slice(hh * DQK, (hh + 1) * DQK)
                    last = products(pe, c.PS[:, 6 + q, kt * P:S], (Vh[:, b * QT + kt, v], Vl[:, b * QT + kt, v]),
                                    (PTh[:, q, kt, kt * P:S], PTl[:, q, kt, kt * P:S]),
                                    start=(kt == 0), stop=(kt == KD - 1))
                last.then_inc(z_done, 1)

            def body(g):
                pe.wait_ge(w_lo, 4 * g + 1)
                for t in range(NT):
                    if t < 2:
                        need(pe, added, NT * g)
                    else:
                        pe.wait_ge(v_lo, NT * g + t - 1)
                    for k in range(KD):
                        tok = slice(t * P, (t + 1) * P)
                        last = products(pe, c.PS[:, t % 2, :], (c.XTh[:, k, tok], c.XTl[:, k, tok]),
                                        (wh[0][:, k, :], wl[0][:, k, :]), start=(k == 0), stop=(k == KD - 1))
                    last.then_inc(v_done, 1)
                pe.wait_ge(w_lo, 4 * g + 3)
                qk(g, U * g, 0)
                for uu in range(U):
                    u = U * g + uu
                    scores(u, uu % 2)
                    if uu < U - 1:
                        qk(g, u + 1, uu + 1)
                    turn(u)
                    if uu > 0:
                        values(u - 1, uu - 1)
                values(U * g + U - 1, U - 1)
                pe.wait_ge(w_lo, 4 * g + 4)
                pe.wait_ge(z_lo, U * (g + 1))
                for t in range(NT):
                    if t < 2:
                        pe.wait_ge(qk_act, 4 * U * (g + 1))
                    else:
                        pe.wait_ge(added, NT * g + t - 1)
                    tok = slice(t * P, (t + 1) * P)
                    for hh in range(GH):
                        last = products(pe, c.PS[:, t % 2, :], (Zh[:, hh, tok], Zl[:, hh, tok]),
                                        (wh[3][:, hh, :], wl[3][:, hh, :]), start=(hh == 0), stop=(hh == GH - 1))
                    last.then_inc(o_done, 1)
            pe.wait_ge(const_done, 1)
            body(0)
            with pe.Fori(1, NG) as g:
                body(g)

        @block.scalar
        def _(act):
            def head_bias(i, g, hh):
                return bq[:, i, GH * g + hh:GH * g + hh + 1] if isinstance(g, int) else bq[:, i, bass.ds(GH * g + hh, 1)]

            def qk(g, u, uu):
                hh, q = uu // B, uu % 2
                for j in range(2):
                    act.wait_ge(qk_done, 2 * u + j + 1)
                    need(act, s_done, QT * (u - 1))
                    need(act, qk_lo, 2 * (u - 2) + j + 1)
                    passed(act, c.act_passed, u)
                    nc.scalar.activation(q32[:, q, j, :], c.PS[:, j, :], ACT.Identity, bias=head_bias(j, g, hh),
                                         scale=1.0 / WS).then_inc(qk_act, 1)
                    nc.scalar.activation(Qh[:, q, j, :], c.PS[:, j, :], ACT.Identity, bias=head_bias(j, g, hh),
                                         scale=1.0 / WS).then_inc(qk_act, 1)

            def z_out(g, u, uu):
                hh, b = divmod(uu, B)
                act.wait_ge(z_done, u + 1)
                need(act, z_lo, u - 1)
                if uu == 0:
                    need(act, o_done, NT * g)
                passed(act, c.act_passed, u)
                nc.scalar.activation(z32[:, uu % 2, :], c.PS[:, 6 + uu % 2, :], ACT.Identity,
                                     bias=head_bias(2, g, hh), scale=1.0 / PS_).then_inc(z_act, 1)
                nc.scalar.activation(Zh[:, hh, b * S:(b + 1) * S], c.PS[:, 6 + uu % 2, :], ACT.Identity,
                                     bias=head_bias(2, g, hh), scale=1.0 / PS_).then_inc(z_act, 1)

            def body(g):
                for t in range(NT):
                    act.wait_ge(v_done, NT * g + t + 1)
                    if t == 0:
                        need(act, z_done, U * g)
                    nc.scalar.activation(Vh[:, t, :], c.PS[:, t % 2, :], ACT.Copy, scale=1.0 / WS).then_inc(v_hi, 1)
                qk(g, U * g, 0)
                for uu in range(U):
                    u = U * g + uu
                    for qt in range(QT):
                        i = (uu % 2) * QT + qt
                        w = (qt + 1) * P
                        act.wait_ge(bias_done, QT * u + qt + 1)
                        need(act, t_done, QT * (u - 1) + qt + 1)
                        nc.scalar.activation(Pr[:, qt, 0:w], c.PS[:, 2 + qt % 2, 0:w], ACT.Exp, bias=nbias[:, i:i + 1],
                                             scale=SC, accum_out=rsum[:, i:i + 1]).then_inc(exp_done, 1)
                    if uu < U - 1:
                        qk(g, u + 1, uu + 1)
                    for qt in range(QT):
                        act.wait_ge(t_done, QT * u + qt + 1)
                        if qt == 0:
                            need(act, z_done, u - 1)
                        nc.scalar.activation(PTh[:, uu % 2, 0:qt + 1, qt * P:(qt + 1) * P],
                                             c.PS[:, 4 + qt % 2, 0:(qt + 1) * P].rearrange("p (k q) -> p k q", q=P),
                                             ACT.Copy, scale=PS_).then_inc(pt_hi, 1)
                    if uu > 0:
                        z_out(g, u - 1, uu - 1)
                z_out(g, U * g + U - 1, U - 1)
            act.wait_ge(const_done, 2)
            body(0)
            with act.Fori(1, NG) as g:
                body(g)

        @block.vector
        def _(dve):
            def qk_lo_part(u, uu):
                q = uu % 2
                for j in range(2):
                    dve.wait_ge(qk_act, 4 * u + 2 * j + 2)
                    nc.vector.tensor_tensor(Ql[:, q, j, :], q32[:, q, j, :], Qh[:, q, j, :],
                                            ALU.subtract).then_inc(qk_lo, 1)

            def inverse(u, uu, qt):
                i = (uu % 2) * QT + qt
                dve.wait_ge(exp_done, QT * u + qt + 1)
                nc.vector.reciprocal(rinv[:, i:i + 1], rsum[:, i:i + 1]).then_inc(inv_done, 1)

            def normalize(u, uu, qt):
                i = (uu % 2) * QT + qt
                w = (qt + 1) * P
                dve.wait_ge(inv_done, QT * u + qt + 1)
                nc.vector.tensor_scalar(Pr[:, qt, 0:w], Pr[:, qt, 0:w], rinv[:, i:i + 1], None,
                                        ALU.mult).then_inc(norm_done, 1)

            def body(g):
                for i in range(4):
                    dve.wait_ge(w_in[i], 16 * GH * (g + 1))
                    if i == 0:
                        need(dve, z_done, U * g)
                    if i == 3:
                        need(dve, o_done, NT * g)
                    nc.vector.tensor_scalar(wh[i][:], st[i][:], WS, None, ALU.mult).then_inc(w_hi, 1)
                    dve.wait_ge(w_hi, 4 * g + i + 1)
                    flat = lambda a: a[:].rearrange("p k n -> p (k n)")
                    nc.vector.scalar_tensor_tensor(out=flat(wl[i]), in0=flat(st[i]), scalar=WS, in1=flat(wh[i]),
                                                   op0=ALU.mult, op1=ALU.subtract).then_inc(w_lo, 1)
                for t in range(NT):
                    dve.wait_ge(v_hi, NT * g + t + 1)
                    nc.vector.scalar_tensor_tensor(out=Vl[:, t, :], in0=c.PS[:, t % 2, :], scalar=1.0 / WS,
                                                   in1=Vh[:, t, :], op0=ALU.mult, op1=ALU.subtract).then_inc(v_lo, 1)
                qk_lo_part(U * g, 0)
                for uu in range(U):
                    u = U * g + uu
                    for qt in range(QT):
                        i = (uu % 2) * QT + qt
                        dve.wait_ge(s_done, QT * u + qt + 1)
                        nc.vector.tensor_reduce(nmax[:, i:i + 1], c.PS[:, 2 + qt % 2, 0:(qt + 1) * P], AX.X, ALU.max,
                                                negate=True).then_inc(max_done, 1)
                        dve.wait_ge(max_done, QT * u + qt + 1)
                        nc.vector.tensor_scalar(nbias[:, i:i + 1], nmax[:, i:i + 1], SC, None,
                                                ALU.mult).then_inc(bias_done, 1)
                        if qt > 0:
                            inverse(u, uu, qt - 1)
                        if qt > 1:
                            normalize(u, uu, qt - 2)
                    inverse(u, uu, QT - 1)
                    normalize(u, uu, QT - 2)
                    normalize(u, uu, QT - 1)
                    if uu < U - 1:
                        qk_lo_part(u + 1, uu + 1)
                    for qt in range(QT):
                        dve.wait_ge(pt_hi, QT * u + qt + 1)
                        part = (slice(None), uu % 2, slice(0, qt + 1), slice(qt * P, (qt + 1) * P))
                        nc.vector.scalar_tensor_tensor(
                            out=PTl[part], in0=c.PS[:, 4 + qt % 2, 0:(qt + 1) * P].rearrange("p (k q) -> p k q", q=P),
                            scalar=PS_, in1=PTh[part], op0=ALU.mult, op1=ALU.subtract).then_inc(pt_lo, 1)
                for t in range(NT):
                    dve.wait_ge(o_done, NT * g + t + 1)
                    need(dve, added, NT * (g - 1) + t + 1)
                    nc.vector.scalar_tensor_tensor(out=c.X[:, t, :], in0=c.PS[:, t % 2, :], scalar=1.0 / (XS * WS),
                                                   in1=c.X[:, t, :], op0=ALU.mult, op1=ALU.add).then_inc(added, 1)
            dve.wait_ge(tri_in, 16)
            nc.vector.tensor_copy(tri[:], tri32[:]).then_inc(const_done, 1)
            dve.wait_ge(bias_in, 32)
            nc.vector.tensor_scalar(bq[:], bq[:], XS, None, ALU.mult).then_inc(const_done, 1)
            for t in range(NT):
                last = nc.vector.tensor_tensor(c.X[:, t, :], c.X[:, t, :], bo[:], ALU.add)
            last.then_inc(const_done, 1)
            dve.wait_ge(const_done, 3)
            body(0)
            with dve.Fori(1, NG) as g:
                body(g)


def phase_attn0(c):
    nc = c.nc
    U = REP * B
    TL = U + B
    SC = 1.0 / float(np.sqrt(DQK)) / (XS * XS)
    NS = 3

    def tiles(uu):
        b, hh = divmod(uu, REP)
        first = b * (REP + 1)
        return [first, first + 1] if hh == 0 else [first + 1 + hh]

    with ExitStack() as ctx:
        sb = lambda name, shape, dt: c.sb(ctx, name, shape, dt)
        sem = lambda name: c.sem(ctx, name)
        wq32 = sb("wq32", [P, KD, REP * DQK], F32)
        wk32 = sb("wk32", [P, KD, DQK], F32)
        wv32 = sb("wv32", [P, KD, KVH * DV], F32)
        wo32 = sb("wo32", [P, KD, D], F32)
        wh = sb("wh", [P, REP + 1, KD, DQK], F16)
        wl = sb("wl", [P, REP + 1, KD, DQK], F16)
        wvh, wvl = sb("wvh", [P, KD, KVH * DV], F16), sb("wvl", [P, KD, KVH * DV], F16)
        woh, wol = sb("woh", [P, KD, D], F16), sb("wol", [P, KD, D], F16)
        rot32, rot = sb("rot32", [P, P], F32), sb("rot", [P, P], F16)
        cos, sin = sb("cos", [P, S], F32), sb("sin", [P, S], F32)
        mask32, mask = sb("mask32", [P, 9 * P], F32), sb("mask", [P, 9 * P], BF16)
        Vh, Vl = sb("Vh", [P, NT, KVH * DV], F16), sb("Vl", [P, NT, KVH * DV], F16)
        Ah, Al = sb("Ah", [P, 2, S], F16), sb("Al", [P, 2, S], F16)
        t1, t2, r32 = sb("t1", [P, 2, S], F32), sb("t2", [P, 2, S], F32), sb("r32", [P, 2, S], F32)
        Kh, Kl = sb("Kh", [P, 2, S], F16), sb("Kl", [P, 2, S], F16)
        Qh, Ql = sb("Qh", [P, 2, S], F16), sb("Ql", [P, 2, S], F16)
        Pr = sb("Pr", [P, QT, NS * P], F32)
        PTh, PTl = sb("PTh", [P, 2, QT, NS * P], F16), sb("PTl", [P, 2, QT, NS * P], F16)
        Z = sb("Z", [P, NT, D], F32)
        ZTh, ZTl = sb("ZTh", [P, KD, B * S], F16), sb("ZTl", [P, KD, B * S], F16)
        nmax, nbias = sb("nmax", [P, 2 * QT], F32), sb("nbias", [P, 2 * QT], F32)
        rsum, rinv = sb("rsum", [P, 2 * QT], F32), sb("rinv", [P, 2 * QT], F32)
        wq_in, wk_in, wv_in, wo_in, const_in = sem("wq_in"), sem("wk_in"), sem("wv_in"), sem("wo_in"), sem("const_in")
        const_done = sem("const_done")
        wv_hi, wv_lo, wo_hi, wo_lo = sem("wv_hi"), sem("wv_lo"), sem("wo_hi"), sem("wo_lo")
        w_hi, w_lo = sem("w_hi"), sem("w_lo")
        v_done, v_hi, v_lo = sem("v_done"), sem("v_hi"), sem("v_lo")
        a_done, a_hi, a_lo, a_cos = sem("a_done"), sem("a_hi"), sem("a_lo"), sem("a_cos")
        r_done, r_sin, r_sum, r_hi, r_lo = sem("r_done"), sem("r_sin"), sem("r_sum"), sem("r_hi"), sem("r_lo")
        s_done, max_done, bias_done = sem("s_done"), sem("max_done"), sem("bias_done")
        exp_done, inv_done = sem("exp_done"), sem("inv_done")
        t_done, pt_hi, pt_lo = sem("t_done"), sem("pt_hi"), sem("pt_lo")
        z_done, z_out = sem("z_done"), sem("z_out")
        zt_done, zt_hi, zt_lo = sem("zt_done"), sem("zt_hi"), sem("zt_lo")
        o_done, added = sem("o_done"), sem("added")
        block = ctx.enter_context(nc.Block())

        @block.sync
        def _(sp):
            def load(g):
                need(sp, w_lo, 10 * g)
                if isinstance(g, int):
                    q, k = c.inp["attn0_wq"][g], c.inp["attn0_wk"][g]
                    pat = "(k p) n -> p k n"
                else:
                    q, k = c.inp["attn0_wq"][bass.ds(g, 1)], c.inp["attn0_wk"][bass.ds(g, 1)]
                    pat = "g (k p) n -> p (g k) n"
                sp.dma_start(wk32[:], k.rearrange(pat, p=P)).then_inc(wk_in, 16)
                sp.dma_start(wq32[:], q.rearrange(pat, p=P)).then_inc(wq_in, 16)
            sp.dma_start(wv32[:], c.inp["attn0_wv"].rearrange("(k p) n -> p k n", p=P)).then_inc(wv_in, 16)
            load(0)
            for to, name in ((rot32, "c_rot"), (cos, "c_cos"), (sin, "c_sin"), (mask32, "c_mask0")):
                sp.dma_start(to[:], c.inp[name]).then_inc(const_in, 16)
            sp.dma_start(wo32[:], c.inp["attn0_wo"].rearrange("(k p) n -> p k n", p=P)).then_inc(wo_in, 16)
            with sp.Fori(1, KVH) as g:
                load(g)

        @block.gpsimd
        def _(pool):
            def rotate(g, uu):
                for tl in tiles(uu):
                    n = TL * g + tl
                    b, hh = divmod(tl, REP + 1)
                    q = tl % 2
                    hi, lo = (Kh[:, b, :], Kl[:, b, :]) if hh == 0 else (Qh[:, uu % 2, :], Ql[:, uu % 2, :])
                    pool.wait_ge(r_sin, n + 1)
                    need(pool, r_lo, n - 1)
                    nc.gpsimd.tensor_tensor(r32[:, q, :], t1[:, q, :], t2[:, q, :], ALU.add).then_inc(r_sum, 1)
                    pool.wait_ge(r_hi, n + 1)
                    nc.gpsimd.tensor_tensor(lo, r32[:, q, :], hi, ALU.subtract).then_inc(r_lo, 1)

            def body(g):
                for uu in range(U):
                    rotate(g, uu)
            body(0)
            with pool.Fori(1, KVH) as g:
                body(g)

        @block.tensor
        def _(pe):
            def project(g, uu):
                for tl in tiles(uu):
                    n = TL * g + tl
                    b, hh = divmod(tl, REP + 1)
                    need(pe, a_cos, n - 1)
                    for k in range(KD):
                        last = products(pe, c.PS[:, tl % 2, :], (wh[:, hh, k, :], wl[:, hh, k, :]),
                                        (c.XTh[:, k, b * S:(b + 1) * S], c.XTl[:, k, b * S:(b + 1) * S]),
                                        start=(k == 0), stop=(k == KD - 1))
                    last.then_inc(a_done, 1)

            def rotate(g, uu):
                for tl in tiles(uu):
                    n = TL * g + tl
                    pe.wait_ge(a_lo, n + 1)
                    need(pe, r_sin, n)
                    pe.matmul(c.PS[:, 7, :], rot[:], Ah[:, tl % 2, :], start=True, stop=False)
                    pe.matmul(c.PS[:, 7, :], rot[:], Al[:, tl % 2, :], start=False, stop=True).then_inc(r_done, 1)

            def scores(g, uu):
                u = U * g + uu
                b, hh = divmod(uu, REP)
                pe.wait_ge(r_lo, TL * g + tiles(uu)[-1] + 1)
                for qt in range(QT):
                    need(pe, exp_done, QT * u + qt - 1)
                    bank = c.PS[:, 2 + qt % 2, :]
                    tok = slice(qt * P, (qt + 1) * P)
                    pe.matmul(bank[:, 0:SP0[qt]], c.identb[:], mask[:, SO0[qt]:SO0[qt] + SP0[qt]], start=True,
                              stop=False, skip_group_check=True)
                    runs = [(0, 0, SP0[qt])] if qt < 3 else [(0, 0, P), (P, 2 * P, 2 * P)]
                    for to, of, w in runs:
                        last = products(pe, bank[:, to:to + w], (Qh[:, uu % 2, tok], Ql[:, uu % 2, tok]),
                                        (Kh[:, b, of:of + w], Kl[:, b, of:of + w]), start=False)
                    last.then_inc(s_done, 1)

            def turn(g, uu):
                u = U * g + uu
                for qt in range(QT):
                    pe.wait_ge(exp_done, QT * u + qt + 1)
                    need(pe, pt_lo, QT * u + qt - 1)
                    for i in range(len(KT0[qt])):
                        last = pe.transpose(c.PS[:, 4 + qt % 2, i * P:(i + 1) * P], Pr[:, qt, i * P:(i + 1) * P],
                                            c.ident[:])
                    last.then_inc(t_done, 1)

            def values(g, uu):
                u = U * g + uu
                b = uu // REP
                q = uu % 2
                pe.wait_ge(pt_lo, QT * u + QT)
                need(pe, z_out, QT * u)
                for qt in range(QT):
                    for i, kt in enumerate(KT0[qt]):
                        vh, vl = value_columns(g, b * QT + kt)
                        last = products(pe, c.PS[:, 6, qt * DV:(qt + 1) * DV],
                                        (PTh[:, q, qt, i * P:(i + 1) * P], PTl[:, q, qt, i * P:(i + 1) * P]), (vh, vl),
                                        start=(i == 0), stop=(i == len(KT0[qt]) - 1))
                last.then_inc(z_done, 1)

            def value_columns(g, t):
                if isinstance(g, int):
                    return Vh[:, t, g * DV:(g + 1) * DV], Vl[:, t, g * DV:(g + 1) * DV]
                return Vh[:, t, bass.ds(g * DV, DV)], Vl[:, t, bass.ds(g * DV, DV)]

            pe.wait_ge(wv_lo, 1)
            for t in range(NT):
                need(pe, v_lo, t - 1)
                for k in range(KD):
                    tok = slice(t * P, (t + 1) * P)
                    last = products(pe, c.PS[:, t % 2, 0:KVH * DV], (c.XTh[:, k, tok], c.XTl[:, k, tok]),
                                    (wvh[:, k, :], wvl[:, k, :]), start=(k == 0), stop=(k == KD - 1))
                last.then_inc(v_done, 1)
            pe.wait_ge(const_done, 2)

            def body(g):
                pe.wait_ge(w_lo, 10 * g + 10)
                if isinstance(g, int):
                    pe.wait_ge(v_lo, NT)
                project(g, 0)
                rotate(g, 0)
                project(g, 1)
                for uu in range(U):
                    scores(g, uu)
                    if uu + 1 < U:
                        rotate(g, uu + 1)
                    if uu + 2 < U:
                        project(g, uu + 2)
                    turn(g, uu)
                    if uu > 0:
                        values(g, uu - 1)
                values(g, U - 1)
            body(0)
            with pe.Fori(1, KVH) as g:
                body(g)
            for t in range(NT):
                if t == 0:
                    pe.wait_ge(z_out, QT * U * KVH)
                need(pe, zt_lo, t - 1)
                for k in range(KD):
                    last = pe.transpose(c.PS[:, 4 + t % 2, k * P:(k + 1) * P], Z[:, t, k * P:(k + 1) * P], c.ident[:])
                last.then_inc(zt_done, 1)
            pe.wait_ge(wo_lo, 1)
            for t in range(NT):
                pe.wait_ge(zt_lo, t + 1)
                need(pe, added, t - 1)
                for k in range(KD):
                    tok = slice(t * P, (t + 1) * P)
                    last = products(pe, c.PS[:, t % 2, :], (ZTh[:, k, tok], ZTl[:, k, tok]), (woh[:, k, :], wol[:, k, :]),
                                    start=(k == 0), stop=(k == KD - 1))
                last.then_inc(o_done, 1)

        @block.scalar
        def _(act):
            def a_parts(g, uu):
                for tl in tiles(uu):
                    n = TL * g + tl
                    act.wait_ge(a_done, n + 1)
                    need(act, r_done, n - 1)
                    nc.scalar.activation(Ah[:, tl % 2, :], c.PS[:, tl % 2, :], ACT.Copy, scale=1.0 / WS).then_inc(a_hi, 1)

            def rotated(g, uu):
                for tl in tiles(uu):
                    n = TL * g + tl
                    b, hh = divmod(tl, REP + 1)
                    act.wait_ge(r_sum, n + 1)
                    need(act, s_done, QT * (U * g + uu - (REP + 1 if hh == 0 else 1)))
                    nc.scalar.activation(Kh[:, b, :] if hh == 0 else Qh[:, uu % 2, :], r32[:, tl % 2, :],
                                         ACT.Copy).then_inc(r_hi, 1)

            for t in range(NT):
                act.wait_ge(v_done, t + 1)
                nc.scalar.activation(Vh[:, t, :], c.PS[:, t % 2, 0:KVH * DV], ACT.Copy, scale=1.0 / WS).then_inc(v_hi, 1)

            def body(g):
                a_parts(g, 0)
                rotated(g, 0)
                a_parts(g, 1)
                for uu in range(U):
                    u = U * g + uu
                    for qt in range(QT):
                        i = (uu % 2) * QT + qt
                        w = SP0[qt]
                        act.wait_ge(bias_done, QT * u + qt + 1)
                        need(act, t_done, QT * (u - 1) + qt + 1)
                        nc.scalar.activation(Pr[:, qt, 0:w], c.PS[:, 2 + qt % 2, 0:w], ACT.Exp, bias=nbias[:, i:i + 1],
                                             scale=SC, accum_out=rsum[:, i:i + 1]).then_inc(exp_done, 1)
                    if uu + 1 < U:
                        rotated(g, uu + 1)
                    if uu + 2 < U:
                        a_parts(g, uu + 2)
                    for qt in range(QT):
                        act.wait_ge(t_done, QT * u + qt + 1)
                        if qt == 0:
                            need(act, z_done, u - 1)
                        nc.scalar.activation(PTh[:, uu % 2, qt, 0:SP0[qt]], c.PS[:, 4 + qt % 2, 0:SP0[qt]],
                                             ACT.Copy, scale=PS_).then_inc(pt_hi, 1)
            body(0)
            with act.Fori(1, KVH) as g:
                body(g)
            for t in range(NT):
                act.wait_ge(zt_done, t + 1)
                nc.scalar.activation(ZTh[:, :, t * P:(t + 1) * P], c.PS[:, 4 + t % 2, :].rearrange("p (k q) -> p k q", k=KD),
                                     ACT.Copy, scale=XS).then_inc(zt_hi, 1)

        @block.vector
        def _(dve):
            def weights(g):
                n = 0
                for hh in range(REP + 1):
                    if hh < 2:
                        dve.wait_ge(wk_in if hh == 0 else wq_in, 16 * (g + 1))
                    if hh == 0:
                        need(dve, a_done, TL * g)
                    for o in range(2):
                        src = wk32[:, :, o::2] if hh == 0 else wq32[:, :, (hh - 1) * DQK + o:hh * DQK:2]
                        to = (slice(None), hh, slice(None), slice(o * 64, o * 64 + 64))
                        nc.vector.tensor_scalar(wh[to], src, WS, None, ALU.mult).then_inc(w_hi, 1)
                        n += 1
                        dve.wait_ge(w_hi, 10 * g + n)
                        nc.vector.scalar_tensor_tensor(out=wl[to], in0=src, scalar=WS, in1=wh[to],
                                                       op0=ALU.mult, op1=ALU.subtract).then_inc(w_lo, 1)

            def a_parts(g, uu):
                for tl in tiles(uu):
                    n = TL * g + tl
                    dve.wait_ge(a_hi, n + 1)
                    nc.vector.scalar_tensor_tensor(out=Al[:, tl % 2, :], in0=c.PS[:, tl % 2, :], scalar=1.0 / WS,
                                                   in1=Ah[:, tl % 2, :], op0=ALU.mult, op1=ALU.subtract).then_inc(a_lo, 1)
                    need(dve, r_sum, n - 1)
                    nc.vector.scalar_tensor_tensor(out=t1[:, tl % 2, :], in0=c.PS[:, tl % 2, :], scalar=1.0 / WS,
                                                   in1=cos[:], op0=ALU.mult, op1=ALU.mult).then_inc(a_cos, 1)

            def sines(g, uu):
                for tl in tiles(uu):
                    n = TL * g + tl
                    dve.wait_ge(r_done, n + 1)
                    dve.wait_ge(a_cos, n + 1)
                    need(dve, r_sum, n - 1)
                    nc.vector.tensor_tensor(t2[:, tl % 2, :], c.PS[:, 7, :], sin[:], ALU.mult).then_inc(r_sin, 1)

            def inverse(u, uu, qt):
                i = (uu % 2) * QT + qt
                dve.wait_ge(exp_done, QT * u + qt + 1)
                nc.vector.reciprocal(rinv[:, i:i + 1], rsum[:, i:i + 1]).then_inc(inv_done, 1)

            def outputs(g, uu):
                u = U * g + uu
                b, hh = divmod(uu, REP)
                dve.wait_ge(z_done, u + 1)
                dve.wait_ge(inv_done, QT * (u + 1))
                for qt in range(QT):
                    i = (uu % 2) * QT + qt
                    first = (REP * g + hh) * DV
                    to = Z[:, b * QT + qt, first:first + DV] if isinstance(g, int) else Z[:, b * QT + qt, bass.ds(first, DV)]
                    nc.vector.tensor_scalar(to, c.PS[:, 6, qt * DV:(qt + 1) * DV], rinv[:, i:i + 1],
                                            1.0 / (PS_ * XS), ALU.mult, ALU.mult).then_inc(z_out, 1)

            def body(g):
                weights(g)
                a_parts(g, 0)
                sines(g, 0)
                a_parts(g, 1)
                for uu in range(U):
                    u = U * g + uu
                    for qt in range(QT):
                        i = (uu % 2) * QT + qt
                        dve.wait_ge(s_done, QT * u + qt + 1)
                        nc.vector.tensor_reduce(nmax[:, i:i + 1], c.PS[:, 2 + qt % 2, 0:SP0[qt]], AX.X, ALU.max,
                                                negate=True).then_inc(max_done, 1)
                        dve.wait_ge(max_done, QT * u + qt + 1)
                        nc.vector.tensor_scalar(nbias[:, i:i + 1], nmax[:, i:i + 1], SC, None,
                                                ALU.mult).then_inc(bias_done, 1)
                        if qt > 0:
                            inverse(u, uu, qt - 1)
                    inverse(u, uu, QT - 1)
                    if uu + 1 < U:
                        sines(g, uu + 1)
                    if uu + 2 < U:
                        a_parts(g, uu + 2)
                    for qt in range(QT):
                        dve.wait_ge(pt_hi, QT * u + qt + 1)
                        nc.vector.scalar_tensor_tensor(
                            out=PTl[:, uu % 2, qt, 0:SP0[qt]], in0=c.PS[:, 4 + qt % 2, 0:SP0[qt]], scalar=PS_,
                            in1=PTh[:, uu % 2, qt, 0:SP0[qt]], op0=ALU.mult, op1=ALU.subtract).then_inc(pt_lo, 1)
                    if uu > 0:
                        outputs(g, uu - 1)
                outputs(g, U - 1)
            dve.wait_ge(wv_in, 16)
            nc.vector.tensor_scalar(wvh[:], wv32[:], WS, None, ALU.mult).then_inc(wv_hi, 1)
            dve.wait_ge(wv_hi, 1)
            nc.vector.scalar_tensor_tensor(out=wvl[:], in0=wv32[:], scalar=WS, in1=wvh[:],
                                           op0=ALU.mult, op1=ALU.subtract).then_inc(wv_lo, 1)
            for t in range(NT):
                dve.wait_ge(v_hi, t + 1)
                nc.vector.scalar_tensor_tensor(out=Vl[:, t, :], in0=c.PS[:, t % 2, 0:KVH * DV], scalar=1.0 / WS,
                                               in1=Vh[:, t, :], op0=ALU.mult, op1=ALU.subtract).then_inc(v_lo, 1)
            dve.wait_ge(const_in, 64)
            nc.vector.tensor_copy(rot[:], rot32[:]).then_inc(const_done, 1)
            nc.vector.tensor_copy(mask[:], mask32[:]).then_inc(const_done, 1)
            body(0)
            with dve.Fori(1, KVH) as g:
                body(g)
            dve.wait_ge(wo_in, 16)
            nc.vector.tensor_scalar(woh[:], wo32[:], WS, None, ALU.mult).then_inc(wo_hi, 1)
            dve.wait_ge(wo_hi, 1)
            nc.vector.scalar_tensor_tensor(out=wol[:], in0=wo32[:], scalar=WS, in1=woh[:],
                                           op0=ALU.mult, op1=ALU.subtract).then_inc(wo_lo, 1)
            for t in range(NT):
                part = (slice(None), slice(None), slice(t * P, (t + 1) * P))
                dve.wait_ge(zt_hi, t + 1)
                nc.vector.scalar_tensor_tensor(out=ZTl[part], in0=c.PS[:, 4 + t % 2, :].rearrange("p (k q) -> p k q", k=KD),
                                               scalar=XS, in1=ZTh[part], op0=ALU.mult, op1=ALU.subtract).then_inc(zt_lo, 1)
            for t in range(NT):
                dve.wait_ge(o_done, t + 1)
                nc.vector.scalar_tensor_tensor(out=c.X[:, t, :], in0=c.PS[:, t % 2, :], scalar=1.0 / (XS * WS),
                                               in1=c.X[:, t, :], op0=ALU.mult, op1=ALU.add).then_inc(added, 1)


def phase_cross0(c):
    nc = c.nc
    SC = 1.0 / float(np.sqrt(D)) / (XS * XS)
    NC = B * CT
    with ExitStack() as ctx:
        sb = lambda name, shape, dt: c.sb(ctx, name, shape, dt)
        sem = lambda name: c.sem(ctx, name)
        C32 = sb("C32", [P, NC, D], F32)
        Ch, Cl = sb("Ch", [P, NC, D], F16), sb("Cl", [P, NC, D], F16)
        CTh, CTl = sb("CTh", [P, KD, B, S2], F16), sb("CTl", [P, KD, B, S2], F16)
        m32 = sb("m32", [P, B, S2 // 4], I32)
        m8 = m32[:].bitcast(U8)
        valid = sb("valid", [P, B], F32)
        mrow, ones = sb("mrow", [1, B, S2], BF16), sb("ones", [1, P], BF16)
        Pr = sb("Pr", [P, 2, S2], F32)
        PTh, PTl = sb("PTh", [P, 2, S2], F16), sb("PTl", [P, 2, S2], F16)
        nmax, nbias = sb("nmax", [P, 2], F32), sb("nbias", [P, 2], F32)
        rsum, rinv, rval = sb("rsum", [P, 2], F32), sb("rinv", [P, 2], F32), sb("rval", [P, 2], F32)
        c_in, m_in = [sem(f"c{b}_in") for b in range(B)], sem("m_in")
        m_done, v_done = sem("m_done"), sem("v_done")
        c_hi, c_lo = sem("c_hi"), sem("c_lo")
        ct_done, ct_hi, ct_lo = sem("ct_done"), sem("ct_hi"), sem("ct_lo")
        stored = sem("stored")
        s_done, max_done, bias_done = sem("s_done"), sem("max_done"), sem("bias_done")
        exp_done, inv_done, val_done = sem("exp_done"), sem("inv_done"), sem("val_done")
        t_done, pt_hi, pt_lo = sem("t_done"), sem("pt_hi"), sem("pt_lo")
        z_done, added = sem("z_done"), sem("added")
        block = ctx.enter_context(nc.Block())

        @block.sync
        def _(sp):
            sp.dma_start(m32[:], c.inp["mask"].partition_broadcast(P)).then_inc(m_in, 16)
            for b in range(B):
                sp.dma_start(C32[:, b * CT:(b + 1) * CT, :],
                             c.inp["ctx"][b].rearrange("(t p) d -> p t d", p=P)).then_inc(c_in[b], 16)
            for b in range(B):
                sp.wait_ge(ct_lo, CT * (b + 1))
                for n, part in enumerate((CTh, CTl)):
                    sp.dma_start(c.ctxT[n][b].rearrange("(k p) s -> p k s", p=P), part[:, :, b, :]).then_inc(stored, 16)
            sp.wait_ge(stored, 64)

        @block.tensor
        def _(pe):
            for t in range(NC):
                if t % CT == 0:
                    pe.wait_ge(c_in[t // CT], 16)
                need(pe, ct_lo, t - 1)
                for k in range(KD):
                    last = pe.transpose(c.PS[:, t % 2, k * P:(k + 1) * P], C32[:, t, k * P:(k + 1) * P], c.ident[:])
                last.then_inc(ct_done, 1)

            def scores(t):
                b = t // QT
                need(pe, exp_done, t - 1)
                tok = slice(t * P, (t + 1) * P)
                for half in range(2):
                    bank = c.PS[:, 2 * (t % 2) + half, :]
                    keys = slice(half * 512, half * 512 + 512)
                    pe.matmul(bank, ones[:], mrow[:, b, keys], start=True, stop=False, skip_group_check=True)
                    for k in range(KD):
                        last = products(pe, bank, (c.XTh[:, k, tok], c.XTl[:, k, tok]),
                                        (CTh[:, k, b, keys], CTl[:, k, b, keys]), start=False, stop=(k == KD - 1))
                last.then_inc(s_done, 1)

            def turn(t):
                pe.wait_ge(exp_done, t + 1)
                need(pe, pt_lo, t)
                for k in range(CT):
                    last = pe.transpose(c.PS[:, 4 + k // 4, (k % 4) * P:(k % 4 + 1) * P], Pr[:, t % 2, k * P:(k + 1) * P],
                                        c.ident[:])
                last.then_inc(t_done, 1)

            def values(t):
                pe.wait_ge(pt_lo, t + 1)
                need(pe, added, t - 1)
                for k in range(CT):
                    at = (t // QT) * CT + k
                    last = products(pe, c.PS[:, 6 + t % 2, :], (PTh[:, t % 2, k * P:(k + 1) * P], PTl[:, t % 2, k * P:(k + 1) * P]),
                                    (Ch[:, at, :], Cl[:, at, :]), start=(k == 0), stop=(k == CT - 1))
                last.then_inc(z_done, 1)

            pe.wait_ge(m_done, 2)
            pe.wait_ge(ct_lo, NC)
            pe.wait_ge(c_lo, NC)
            scores(0)
            for t in range(NT):
                if t + 1 < NT:
                    scores(t + 1)
                turn(t)
                if t > 0:
                    values(t - 1)
            values(NT - 1)

        @block.scalar
        def _(act):
            for t in range(NC):
                act.wait_ge(ct_done, t + 1)
                nc.scalar.activation(CTh[:, :, t // CT, (t % CT) * P:(t % CT + 1) * P],
                                     c.PS[:, t % 2, :].rearrange("p (k q) -> p k q", k=KD),
                                     ACT.Copy, scale=XS).then_inc(ct_hi, 1)
                nc.scalar.activation(Ch[:, t, :], C32[:, t, :], ACT.Copy, scale=XS).then_inc(c_hi, 1)
            for t in range(NT):
                q = t % 2
                act.wait_ge(bias_done, t + 1)
                need(act, t_done, t - 1)
                nc.scalar.activation(Pr[:, q, :], c.PS[:, 2 * q:2 * q + 2, :].rearrange("p a b -> p (a b)"), ACT.Exp,
                                     bias=nbias[:, q:q + 1], scale=SC, accum_out=rsum[:, q:q + 1]).then_inc(exp_done, 1)
                act.wait_ge(t_done, t + 1)
                need(act, z_done, t - 1)
                nc.scalar.activation(PTh[:, q, :], c.PS[:, 4:6, :].rearrange("p a b -> p (a b)"), ACT.Copy,
                                     scale=PS_).then_inc(pt_hi, 1)

        @block.vector
        def _(dve):
            dve.wait_ge(m_in, 16)
            nc.vector.tensor_scalar(mrow[:], m8[0:1], 1.0, -NEG, ALU.subtract, ALU.mult).then_inc(m_done, 1)
            nc.vector.memset(ones[:], 1.0).then_inc(m_done, 1)
            nc.vector.tensor_reduce(valid[:], m8, AX.X, ALU.max).then_inc(v_done, 1)
            dve.wait_ge(v_done, 1)
            nc.vector.tensor_scalar(valid[:], valid[:], 1.0 / (PS_ * XS), None, ALU.mult).then_inc(v_done, 1)
            for t in range(NC):
                dve.wait_ge(ct_hi, t + 1)
                to = (slice(None), slice(None), t // CT, slice((t % CT) * P, (t % CT + 1) * P))
                nc.vector.scalar_tensor_tensor(out=CTl[to], in0=c.PS[:, t % 2, :].rearrange("p (k q) -> p k q", k=KD),
                                               scalar=XS, in1=CTh[to], op0=ALU.mult, op1=ALU.subtract).then_inc(ct_lo, 1)
                dve.wait_ge(c_hi, t + 1)
                nc.vector.scalar_tensor_tensor(out=Cl[:, t, :], in0=C32[:, t, :], scalar=XS, in1=Ch[:, t, :],
                                               op0=ALU.mult, op1=ALU.subtract).then_inc(c_lo, 1)

            def maximum(t):
                q = t % 2
                dve.wait_ge(s_done, t + 1)
                nc.vector.tensor_reduce(nmax[:, q:q + 1], c.PS[:, 2 * q:2 * q + 2, :], AX.XY, ALU.max,
                                        negate=True).then_inc(max_done, 1)
                dve.wait_ge(max_done, t + 1)
                nc.vector.tensor_scalar(nbias[:, q:q + 1], nmax[:, q:q + 1], SC, None, ALU.mult).then_inc(bias_done, 1)

            def output(t):
                dve.wait_ge(z_done, t + 1)
                nc.vector.scalar_tensor_tensor(out=c.X[:, t, :], in0=c.PS[:, 6 + t % 2, :], scalar=rval[:, t % 2:t % 2 + 1],
                                               in1=c.X[:, t, :], op0=ALU.mult, op1=ALU.add).then_inc(added, 1)

            dve.wait_ge(v_done, 2)
            maximum(0)
            for t in range(NT):
                q = t % 2
                if t + 1 < NT:
                    maximum(t + 1)
                dve.wait_ge(exp_done, t + 1)
                nc.vector.reciprocal(rinv[:, q:q + 1], rsum[:, q:q + 1]).then_inc(inv_done, 1)
                dve.wait_ge(pt_hi, t + 1)
                nc.vector.scalar_tensor_tensor(out=PTl[:, q, :], in0=c.PS[:, 4:6, :].rearrange("p a b -> p (a b)"),
                                               scalar=PS_, in1=PTh[:, q, :], op0=ALU.mult, op1=ALU.subtract).then_inc(pt_lo, 1)
                if t > 0:
                    output(t - 1)
                dve.wait_ge(inv_done, t + 1)
                nc.vector.tensor_tensor(rval[:, q:q + 1], rinv[:, q:q + 1], valid[:, t // QT:t // QT + 1],
                                        ALU.mult).then_inc(val_done, 1)
                dve.wait_ge(val_done, t + 1)
            output(NT - 1)


def phase_cross1(c):
    nc = c.nc
    SC = 1.0 / float(np.sqrt(DV)) / (XS * XS)
    OFF = S2 - S
    K0 = OFF // P
    R = 3 * DV
    MS = 32.0
    N = B * H
    GS = 4
    LEAD = GS + 2
    VW = 2 * DV + 1
    SLOTS = 4
    RING = CT + 4
    ON_POOL = (1, 3, 5, 6)
    with ExitStack() as ctx:
        sb = lambda name, shape, dt: c.sb(ctx, name, shape, dt)
        sem = lambda name: c.sem(ctx, name)
        KS = [sb(f"KS{b}", [P, H, S2], F16) for b in range(B)]
        QS = [sb(f"QS{b}", [P, H, S], F16) for b in range(B)]
        P32 = sb("P32", [P, SLOTS, S], F32)
        V = sb("V", [P, B * CT, H, VW], F16)
        tri32, triT32 = sb("tri32", [P, P], F32), sb("triT32", [P, P], F32)
        tri, triT = sb("tri", [P, P], BF16), sb("triT", [P, P], BF16)
        comb = sb("comb", [VW, DV + 1], F32)
        M = sb("M", [P, B, QT, H], F32)
        mt = sb("mt", [GS, S], F32)
        mh, ml = sb("mh", [GS, S], F16), sb("ml", [GS, S], F16)
        PTh, PTl = sb("PTh", [P, RING, S], F16), sb("PTl", [P, RING, S], F16)
        Zs = sb("Zs", [VW, 2, S], F32)
        rinv = sb("rinv", [P, QT], F32)
        z = sb("z", [P, 2, QT, DV], F32)
        stack_in = [sem(f"stack{b}_in") for b in range(B)]
        const_in, const_done = sem("const_in"), sem("const_done")
        ctx_in = [sem(f"ctx{i}_in") for i in range(SLOTS)]
        v_hi, v_lo = sem("v_hi"), sem("v_lo")
        ones_done = sem("ones_done")
        s_done, max_done = sem("s_done"), sem("max_done")
        m_turned, m_shift, m_hi, m_lo, m_in = sem("m_turned"), sem("m_shift"), sem("m_hi"), sem("m_lo"), sem("m_in")
        e_done, exp_done = sem("e_done"), sem("exp_done")
        lo_dve, lo_pool = sem("lo_dve"), sem("lo_pool")
        z_done, z_copied, c_done = sem("z_done"), sem("z_copied"), sem("c_done")
        inv_done, z_out, added = sem("inv_done"), sem("z_out"), sem("added")
        block = ctx.enter_context(nc.Block())

        def wait_lo(engine, n, kt):
            on_pool = kt in ON_POOL
            mine = [k for k in range(CT) if (k in ON_POOL) == on_pool]
            engine.wait_ge(lo_pool if on_pool else lo_dve, len(mine) * n + mine.index(kt) + 1)

        def first_query(kt):
            return max(kt - K0, 0) * P

        def turn_group(n):
            m = n + LEAD - 1
            return m // GS if m % GS == GS - 1 and GS <= m < N else None

        def low_part(engine, ops, n, kt, done):
            cols = slice(first_query(kt), S)
            engine.wait_ge(exp_done, CT * n + kt + 1)
            ops.tensor_tensor(PTl[:, (CT * n + kt) % RING, cols], P32[:, kt % SLOTS, cols], PTh[:, (CT * n + kt) % RING, cols],
                                 ALU.subtract).then_inc(done, 1)

        @block.sync
        def _(sp):
            def stacks(b):
                for h4 in range(4):
                    rows = slice(h4 * DV, (h4 + 1) * DV)
                    for n, (qp, kp) in enumerate(((c.XTh, 0), (c.XTh, 1), (c.XTl, 0))):
                        to = slice(n * DV, (n + 1) * DV)
                        sp.dma_start(QS[b][to, h4::4, :], qp[rows, :, b * S:(b + 1) * S]).then_inc(stack_in[b], 16)
                        src = c.ctxT[kp][b].rearrange("(k f p) s -> f p k s", f=4, p=DV)[h4]
                        sp.dma_start(KS[b][to, h4::4, :], src).then_inc(stack_in[b], 16)

            def shift_rows(g):
                b, h = divmod(GS * g, H)
                sp.wait_ge(m_lo, g + 1)
                sp.dma_start(QS[b][R:R + 1, h:h + GS, :], mh[:]).then_inc(m_in, 16)
                sp.dma_start(QS[b][R + 1:R + 2, h:h + GS, :], ml[:]).then_inc(m_in, 16)

            for to, name in ((tri32, "c_tri"), (triT32, "c_triT"), (comb, "c_comb")):
                sp.dma_start(to[:], c.inp[name]).then_inc(const_in, 16)
            stacks(0)
            for t in range(B * CT):
                need(sp, v_lo, t - SLOTS + 1)
                sp.dma_start(P32[:, t % SLOTS, :], c.inp["ctx"][t // CT, (t % CT) * P:(t % CT + 1) * P, :]).then_inc(ctx_in[t % SLOTS], 16)
            shift_rows(0)
            stacks(1)
            for g in range(1, N // GS):
                shift_rows(g)

        @block.gpsimd
        def _(pool):
            nc.gpsimd.memset(V[:, :, :, 2 * DV:VW], XS).then_inc(ones_done, 1)
            pool.wait_ge(ones_done, 1)
            nc.gpsimd.memset(KS[0][R:P, :, :], -MS).then_inc(ones_done, 1)
            pool.wait_ge(ones_done, 2)
            nc.gpsimd.memset(KS[1][R:P, :, :], -MS).then_inc(ones_done, 1)
            pool.wait_ge(ones_done, 3)

            def add(n):
                b, h = divmod(n, H)
                pool.wait_ge(z_out, n + 1)
                x = c.X[:, b * QT:(b + 1) * QT, h * DV:(h + 1) * DV]
                nc.gpsimd.tensor_tensor(x, x, z[:, n % 2], ALU.add).then_inc(added, 1)

            for n in range(N + 2):
                if n < N:
                    for kt in ON_POOL:
                        low_part(pool, nc.gpsimd, n, kt, lo_pool)
                if n >= 2:
                    add(n - 2)

        @block.tensor
        def _(pe):
            def max_tile(n, qt):
                b, h = divmod(n, H)
                i = QT * n + qt
                need(pe, max_done, i - 1)
                w = OFF + (qt + 1) * P
                lhs = QS[b][0:R, h, qt * P:(qt + 1) * P]
                pe.matmul(c.PS[:, 2 * (i % 2), :], lhs, KS[b][0:R, h, 0:512], start=True, stop=True)
                pe.matmul(c.PS[:, 2 * (i % 2) + 1, 0:w - 512], lhs, KS[b][0:R, h, 512:w], start=True, stop=False,
                          skip_group_check=True)
                pe.matmul(c.PS[:, 2 * (i % 2) + 1, w - 512 - P:w - 512], c.identb[:], tri[:], start=False, stop=True,
                          skip_group_check=True).then_inc(s_done, 1)

            def turn_maxima(g):
                b, h = divmod(GS * g, H)
                pe.wait_ge(max_done, QT * GS * (g + 1))
                need(pe, z_out, GS * (g + 1) - LEAD - 1)
                for qt in range(QT):
                    last = pe.transpose(c.PS[0:GS, 7, qt * P:(qt + 1) * P], M[:, b, qt, h:h + GS], c.ident[:])
                last.then_inc(m_turned, 1)

            def exp_tile(n, kt):
                b, h = divmod(n, H)
                i = CT * n + kt
                if kt == 0 and n % GS == 0:
                    pe.wait_ge(m_in, 32 * (n // GS + 1))
                need(pe, exp_done, i - 1)
                q0 = first_query(kt)
                bank = c.PS[:, 4 + i % 2, :]
                last = pe.matmul(bank[:, q0:S], KS[b][0:R + 2, h, kt * P:(kt + 1) * P], QS[b][0:R + 2, h, q0:S],
                                 start=True, stop=(kt < K0), skip_group_check=True)
                if kt >= K0:
                    last = pe.matmul(bank[:, q0:q0 + P], c.identb[:], triT[:], start=False, stop=True,
                                     skip_group_check=True)
                last.then_inc(e_done, 1)

            def value_tile(n, kt):
                b, h = divmod(n, H)
                wait_lo(pe, n, kt)
                if kt == 0:
                    need(pe, z_copied, n)
                cols = slice(first_query(kt), S)
                v, slot = V[:, b * CT + kt, h, :], (CT * n + kt) % RING
                pe.matmul(c.PS[0:VW, 6, cols], v, PTh[:, slot, cols], start=(kt == 0), stop=False,
                          skip_group_check=True)
                last = pe.matmul(c.PS[0:VW, 6, cols], v, PTl[:, slot, cols], start=False, stop=(kt == CT - 1),
                                 skip_group_check=True)
                last.then_inc(z_done, 1)

            def combine(n):
                pe.wait_ge(z_copied, n + 1)
                need(pe, z_out, n)
                pe.wait_ge(m_shift, 1 + sum(turn_group(i) is not None for i in range(n + 2)))
                for qt in range(QT):
                    last = pe.matmul(c.PS[:, 7, qt * (DV + 1):(qt + 1) * (DV + 1)], Zs[:, n % 2, qt * P:(qt + 1) * P],
                                     comb[:], start=True, stop=True, skip_group_check=True)
                last.then_inc(c_done, 1)

            pe.wait_ge(const_done, 2)
            pe.wait_ge(const_in, 48)
            pe.wait_ge(stack_in[0], 16 * 24)
            for n in range(LEAD):
                for qt in range(QT):
                    max_tile(n, qt)
                if n == GS:
                    turn_maxima(0)
            pe.wait_ge(ones_done, 3)
            pe.wait_ge(v_lo, B * CT)
            for n in range(N + 2):
                if n + LEAD == H:
                    pe.wait_ge(stack_in[1], 16 * 24)
                for kt in range(CT):
                    if n < N:
                        exp_tile(n, kt)
                    if kt % 2 == 1 and n + LEAD < N:
                        max_tile(n + LEAD, kt // 2)
                    if 1 <= n <= N:
                        value_tile(n - 1, kt)
                    if kt == 3 and n >= 2:
                        combine(n - 2)
                    if kt == 5 and turn_group(n) is not None:
                        turn_maxima(turn_group(n))

        @block.scalar
        def _(act):
            for t in range(B * CT):
                act.wait_ge(ctx_in[t % SLOTS], 16 * (t // SLOTS + 1))
                nc.scalar.activation(V[:, t, :, 0:DV], P32[:, t % SLOTS, :].rearrange("p (h e) -> p h e", h=H),
                                     ACT.Copy, scale=XS).then_inc(v_hi, 1)
            act.wait_ge(v_lo, B * CT)
            for n in range(N + 2):
                if n >= 2:
                    act.wait_ge(z_done, CT * (n - 1))
                    need(act, c_done, n - 3)
                    nc.scalar.activation(Zs[:, n % 2, :], c.PS[0:VW, 6, :], ACT.Copy).then_inc(z_copied, 1)
                for kt in range(CT if n < N else 0):
                    i = CT * n + kt
                    cols = slice(first_query(kt), S)
                    act.wait_ge(e_done, i + 1)
                    if i >= SLOTS:
                        wait_lo(act, *divmod(i - SLOTS, CT))
                    need(act, z_done, i + 1 - RING)
                    nc.scalar.activation(P32[:, kt % SLOTS, cols], c.PS[:, 4 + i % 2, cols], ACT.Exp, scale=SC)
                    nc.scalar.activation(PTh[:, i % RING, cols], c.PS[:, 4 + i % 2, cols], ACT.Exp,
                                         scale=SC).then_inc(exp_done, 1)

        @block.vector
        def _(dve):
            def max_tile(n, qt):
                b, h = divmod(n, H)
                i = QT * n + qt
                w = OFF + (qt + 1) * P
                dve.wait_ge(s_done, i + 1)
                nc.vector.tensor_reduce(M[:, b, qt, h:h + 1],
                                        c.PS[:, 2 * (i % 2):2 * (i % 2) + 2, :].rearrange("p a b -> p (a b)")[:, 0:w],
                                        AX.X, ALU.max).then_inc(max_done, 1)

            def shift_parts(g):
                dve.wait_ge(m_turned, g + 1)
                nc.vector.tensor_scalar(mt[:], c.PS[0:GS, 7, :], 1.0 / MS, -float(np.log(PS_)) / SC / MS,
                                        ALU.mult, ALU.add).then_inc(m_shift, 1)
                dve.wait_ge(m_shift, g + 1)
                need(dve, m_in, 32 * g)
                nc.vector.tensor_copy(mh[:], mt[:]).then_inc(m_hi, 1)
                dve.wait_ge(m_hi, g + 1)
                nc.vector.tensor_tensor(ml[:], mt[:], mh[:], ALU.subtract).then_inc(m_lo, 1)

            def output(n):
                dve.wait_ge(c_done, n + 1)
                need(dve, added, n - 1)
                bank = c.PS[:, 7, 0:QT * (DV + 1)].rearrange("p (q e) -> p q e", q=QT)
                need(dve, z_out, n)
                nc.vector.reciprocal(rinv[:].unsqueeze(2), bank[:, :, DV:DV + 1]).then_inc(inv_done, 1)
                dve.wait_ge(inv_done, n + 1)
                nc.vector.tensor_tensor(z[:, n % 2], bank[:, :, 0:DV], rinv[:].unsqueeze(2).broadcast_to([P, QT, DV]),
                                        ALU.mult).then_inc(z_out, 1)

            def value_lows(first, last):
                for t in range(first, last):
                    dve.wait_ge(v_hi, t + 1)
                    nc.vector.scalar_tensor_tensor(out=V[:, t, :, DV:2 * DV],
                                                   in0=P32[:, t % SLOTS, :].rearrange("p (h e) -> p h e", h=H), scalar=XS,
                                                   in1=V[:, t, :, 0:DV], op0=ALU.mult, op1=ALU.subtract).then_inc(v_lo, 1)

            dve.wait_ge(const_in, 48)
            nc.vector.tensor_copy(tri[:], tri32[:]).then_inc(const_done, 1)
            nc.vector.tensor_copy(triT[:], triT32[:]).then_inc(const_done, 1)
            for n in range(LEAD):
                for qt in range(QT):
                    max_tile(n, qt)
                if n == GS:
                    shift_parts(0)
                value_lows(B * CT * n // LEAD, B * CT * (n + 1) // LEAD)
            for n in range(N + 2):
                for kt in range(CT):
                    if n < N and kt not in ON_POOL:
                        low_part(dve, nc.vector, n, kt, lo_dve)
                    if kt % 2 == 1 and n + LEAD < N:
                        max_tile(n + LEAD, kt // 2)
                    if kt == 4 and n >= 2:
                        output(n - 2)
                    if kt == 6 and turn_group(n) is not None:
                        shift_parts(turn_group(n))


def ffn0(c, W, norm, gate0, gate1):
    with ExitStack() as ctx:
        c.wide = (c.sb(ctx, "XRh", [P, KD, B * S], F32R), c.sb(ctx, "XRl", [P, KD, B * S], F32R), 1.0)
        keep = c.sb(ctx, "keep", [P, NT, D], F32)
        phase_norm(c, norm=norm, wide=True)
        phase_keep(c, keep, False)
        phase_gate(c, W, *gate0, NE, NE - 2, wide=True)
        phase_ffn0(c, W, 1.0)
        phase_norm(c, norm=False, wide=True)
        phase_gate(c, W, *gate1, NE, NE - 2, wide=True)
        phase_keep(c, keep, True)
        phase_ffn0(c, W, 2.0)


def decoder(nc, inputs, out, phases):
    ctx = ExitStack()
    with ctx:
        c = Core(nc, ctx, inputs, out)
        W = c.sb(ctx, "W", [P, NT, NE], F32)
        phase_load(c)
        for p in phases:
            p(c, W)


PHASES = [
    lambda c, W: phase_norm(c, norm=False),
    lambda c, W: phase_attn0(c),
    lambda c, W: phase_norm(c),
    lambda c, W: phase_cross0(c),
    lambda c, W: ffn0(c, W, True, (c.inp["gate0_w0"], c.inp["gate0_b0"]), (c.inp["gate0_w1"], c.inp["gate0_b1"])),
    lambda c, W: phase_norm(c),
    lambda c, W: phase_attn1(c),
    lambda c, W: phase_norm(c),
    lambda c, W: phase_cross1(c),
    lambda c, W: phase_norm(c),
    lambda c, W: phase_gate(c, W, c.inp["gate1_w"], c.inp["gate1_b"], 7, 3, c.inp["gate1_sel"]),
    lambda c, W: phase_ffn1(c, W),
    lambda c, W: phase_norm(c, transpose=False, store=True),
]


def constants():
    i, j = np.arange(S)[:, None], np.arange(S)[None, :]
    seen = ((j <= i) & (j > i - WIN)) | ((j < FRONT) & (j <= i - WIN))
    window = np.where(seen, 0.0, NEG)
    causal = np.where(np.tril(np.ones((P, P))) > 0, 0.0, NEG)
    freq = 1.0 / 10000.0 ** (np.arange(0, DQK, 2).astype(np.float32) / DQK)
    angle = np.outer(np.arange(S, dtype=np.float32), freq).T
    half = np.eye(DQK // 2)
    zero = np.zeros_like(half)
    out = {
        "c_ident": np.eye(P),
        "c_below": np.tril(np.ones((8, 8)), -1),
        "c_tri": causal,
        "c_triT": causal.T,
        "c_comb": np.eye(2 * DV + 1)[:, np.r_[0:DV, 2 * DV]] + np.eye(2 * DV + 1, k=-DV)[:, :DV + 1] * (np.arange(DV + 1) < DV),
        "c_mask0": np.concatenate([window[q * P:(q + 1) * P, k * P:(k + 1) * P] for q in range(QT) for k in KT0[q]], 1),
        "c_cos": np.concatenate([np.cos(angle)] * 2),
        "c_sin": np.concatenate([np.sin(angle)] * 2),
        "c_rot": np.block([[zero, half], [-half, zero]]),
    }
    return {k: np.ascontiguousarray(v, dtype=np.float32) for k, v in out.items()}


def laid_out(v):
    v = {k: np.asarray(a) for k, a in v.items()}

    def by_tile(b):
        return b.reshape(NE, E0 // P, P).transpose(2, 0, 1)

    n = NE - 2
    twice = lambda a: np.stack([a, a])
    out = {
        "x": v["x"].reshape(B * S, D),
        "ctx": v["ctx_2048"],
        "mask": np.ascontiguousarray(v["mask_BxS2_bk0"]).view(np.int32),
        "attn0_wq": v["L0_attn_wq"].reshape(D, KVH, REP * DQK).transpose(1, 0, 2),
        "attn0_wk": v["L0_attn_wk"].reshape(D, KVH, DQK).transpose(1, 0, 2),
        "attn0_wv": v["L0_attn_wv"],
        "attn0_wo": v["L0_attn_wo"],
        "gate0_w0": v["L0_ffn_Wg"][0], "gate0_w1": v["L0_ffn_Wg"][1],
        "gate0_b0": v["L0_ffn_bg"][0], "gate0_b1": v["L0_ffn_bg"][1],
        "ffn0_Wup": np.concatenate([v["L0_ffn_Wup"], v["L0_ffn_Wsu"].reshape(D, 2, E0).transpose(1, 0, 2)]),
        "ffn0_Wsw": np.concatenate([v["L0_ffn_Wsw"], twice(v["L0_ffn_Wsa"])]),
        "ffn0_Wdn": np.concatenate([v["L0_ffn_Wdn"], v["L0_ffn_Wsd"].reshape(2, E0, D)]),
        "ffn0_bup": by_tile(np.concatenate([v["L0_ffn_bup"], v["L0_ffn_bsu"].reshape(2, E0)])),
        "ffn0_bsw": by_tile(np.concatenate([v["L0_ffn_bsw"], twice(v["L0_ffn_bsa"])])),
        "ffn0_bdn": np.concatenate([v["L0_ffn_bdn"], v["L0_ffn_bsd"][None], np.zeros((1, D), np.float32)]),
        "attn1_WQ": v["L1_attn_W_Q"], "attn1_WK": v["L1_attn_W_K"],
        "attn1_WV": v["L1_attn_W_V"], "attn1_WO": v["L1_attn_W_O"],
        "attn1_bT": np.stack([v["L1_attn_b_Q"].T, v["L1_attn_b_K"].T, v["L1_attn_b_V"].T], 1),
        "attn1_bO": v["L1_attn_b_O"],
        "gate1_w": v["L1_ffn_gate_w"], "gate1_b": v["L1_ffn_gate_b"], "gate1_sel": v["L1_ffn_biases"],
        "ffn1_W1": np.concatenate([v["L1_ffn_W1"], v["L1_ffn_Ws1"][None]]),
        "ffn1_Wg": np.concatenate([v["L1_ffn_Wg"], v["L1_ffn_Wsg"][None]]),
        "ffn1_W2": np.concatenate([v["L1_ffn_W2"], v["L1_ffn_Ws2"][None]]),
    }
    return {k: np.ascontiguousarray(a) for k, a in out.items()}


def kernel(**inputs):
    import concourse.bacc as bacc
    from concourse.bass_utils import run_bass_kernel_spmd

    arrays = {**laid_out(inputs), **constants()}
    nc = bacc.Bacc("TRN2", target_bir_lowering=False, num_devices=1)
    dram = {
        k: nc.dram_tensor(f"in_{k}", a.shape, mybir.dt.from_np(a.dtype), kind="ExternalInput").ap()
        for k, a in arrays.items()
    }
    out = nc.dram_tensor("out", (B * S, D), F32, kind="ExternalOutput").ap()
    decoder(nc, dram, out, PHASES)
    got = run_bass_kernel_spmd(nc, [{f"in_{k}": a for k, a in arrays.items()}], core_ids=[0])
    return got.results[0]["out"].reshape(B, S, D)
```

```python
from contextlib import ExitStack

import numpy as np

import concourse.bass as bass
from concourse import mybir

ALU = mybir.AluOpType
ACT = mybir.ActivationFunctionType
AX = mybir.AxisListType
F32 = mybir.dt.float32
F16 = mybir.dt.float16
F32R = mybir.dt.float32r
BF16 = mybir.dt.bfloat16
U8 = mybir.dt.uint8
I32 = mybir.dt.int32

P = 128
B, S, D = 2, 512, 512
NT = B * S // P
KD = D // P
QT = S // P
S2 = 1024
CT = S2 // P
H = 16
DQK = 128
KVH = 4
REP = H // KVH
DV = D // H
WIN, FRONT = 128, 64
NE = 8
E0 = 256
EPS = 1e-5
NEG = -2.0 ** 100

XS = 2.0 ** 5
WS = 2.0 ** 8
PS_ = 2.0 ** 10
SP0 = [P, 2 * P, 3 * P, 3 * P]
SO0 = [0, P, 3 * P, 6 * P]
KT0 = [(0,), (0, 1), (0, 1, 2), (0, 2, 3)]


def need(engine, sem, value):
    if isinstance(value, int) and value <= 0:
        return
    engine.wait_ge(sem, value)


def passed(engine, sem, n):
    if not isinstance(n, int):
        engine.sem_inc(sem, 1)


def products(pe, out, a, b, start=True, stop=True):
    pe.matmul(out, a[0], b[0], start=start, stop=False, skip_group_check=True)
    pe.matmul(out, a[0], b[1], start=False, stop=False, skip_group_check=True)
    return pe.matmul(out, a[1], b[0], start=False, stop=stop, skip_group_check=True)


def plain(a):
    return a.bitcast(F32) if a.dtype == F32R else a


class Core:

    def __init__(self, nc, ctx, inputs, out):
        self.nc, self.ctx, self.inp, self.out = nc, ctx, inputs, out
        self.n = 0
        self.sems = []
        self.X = self.sb(ctx, "X", [P, NT, D], F32)
        self.XTh = self.sb(ctx, "XTh", [P, KD, B * S], F16)
        self.XTl = self.sb(ctx, "XTl", [P, KD, B * S], F16)
        self.ident = self.sb(ctx, "ident", [P, P], F32)
        self.identb = self.sb(ctx, "identb", [P, P], BF16)
        self.PS = ctx.enter_context(nc.psum_tensor("PS", [P, 8, 512], F32))
        self.pool_passed = ctx.enter_context(nc.semaphore("pool_passed"))
        self.act_passed = ctx.enter_context(nc.semaphore("act_passed"))
        self.ctxT = [nc.dram_tensor(f"ctxT_{n}", [B, D, S2], F16, kind="Internal").ap() for n in ("hi", "lo")]

    def sb(self, ctx, name, shape, dt):
        self.n += 1
        return ctx.enter_context(self.nc.sbuf_tensor(f"{name}_{self.n}", shape, dt))

    def sem(self, ctx, name):
        self.n += 1
        if not self.sems:
            ctx.callback(self.free_sems)
        self.sems.append(self.nc.alloc_semaphore(f"{name}_{self.n}"))
        return self.sems[-1]

    def free_sems(self):
        self.nc.clear_and_free_semaphores(self.sems)
        self.nc.all_engine_barrier()
        self.sems = []


class Norm:
    LATE = 3

    def __init__(self, c, ctx, ready, banks, to=None, norm=True, X=None, store=False):
        self.c, self.ready, self.banks, self.norm, self.to_dram = c, ready, banks, norm, store
        self.X = c.X if X is None else X
        self.XTh, self.XTl, self.scale = to or (c.XTh, c.XTl, XS)
        self.stats = c.sb(ctx, "stats", [P, NT, 6], F32)
        self.mv = c.sb(ctx, "mv", [P, NT, 2], F32)
        self.veps = c.sb(ctx, "veps", [P, NT], F32)
        self.std = c.sb(ctx, "std", [P, NT], F32)
        self.rstd = c.sb(ctx, "rstd", [P, NT], F32)
        self.stats_done = c.sem(ctx, "stats_done")
        self.mv_done = c.sem(ctx, "mv_done")
        self.veps_done = c.sem(ctx, "veps_done")
        self.std_done = c.sem(ctx, "std_done")
        self.rstd_done = c.sem(ctx, "rstd_done")
        self.normed = c.sem(ctx, "normed")
        self.turned = c.sem(ctx, "turned")
        self.xt_hi = c.sem(ctx, "xt_hi")
        self.xt_lo = c.sem(ctx, "xt_lo")
        self.stored = c.sem(ctx, "stored")

    def moments(self, dve, t):
        nc = self.c.nc
        dve.wait_ge(*self.ready(t))
        nc.vector.bn_stats(self.stats[:, t, :], self.X[:, t, :]).then_inc(self.stats_done, 1)
        dve.wait_ge(self.stats_done, t + 1)
        nc.vector.bn_aggr(self.mv[:, t, :], self.stats[:, t, :]).then_inc(self.mv_done, 1)
        dve.wait_ge(self.mv_done, t + 1)
        nc.vector.tensor_scalar(self.veps[:, t:t + 1], self.mv[:, t, 1:2], EPS, None, ALU.add).then_inc(self.veps_done, 1)

    def root(self, act, t):
        act.wait_ge(self.veps_done, t + 1)
        self.c.nc.scalar.activation(self.std[:, t:t + 1], self.veps[:, t:t + 1], ACT.Sqrt).then_inc(self.std_done, 1)

    def normalize(self, dve, t):
        nc = self.c.nc
        dve.wait_ge(self.std_done, t + 1)
        nc.vector.reciprocal(self.rstd[:, t:t + 1], self.std[:, t:t + 1]).then_inc(self.rstd_done, 1)
        dve.wait_ge(self.rstd_done, t + 1)
        nc.vector.tensor_scalar(self.X[:, t, :], self.X[:, t, :], self.mv[:, t, 0:1], self.rstd[:, t:t + 1],
                                ALU.subtract, ALU.mult).then_inc(self.normed, 1)

    def bank(self, t):
        return self.c.PS[:, self.banks[t % len(self.banks)], :]

    def turn(self, pe, t):
        if self.norm:
            pe.wait_ge(self.normed, t + 1)
        else:
            pe.wait_ge(*self.ready(t))
        need(pe, self.xt_lo, t + 1 - len(self.banks))
        for k in range(KD):
            cols = slice(k * P, (k + 1) * P)
            last = pe.transpose(self.bank(t)[:, cols], self.X[:, t, cols], self.c.ident[:])
        last.then_inc(self.turned, 1)

    def high(self, act, t):
        act.wait_ge(self.turned, t + 1)
        self.c.nc.scalar.activation(self.XTh[:, :, t * P:(t + 1) * P], self.bank(t).rearrange("p (k q) -> p k q", k=KD),
                                    ACT.Copy, scale=self.scale).then_inc(self.xt_hi, 1)

    def low(self, dve, t):
        part = (slice(None), slice(None), slice(t * P, (t + 1) * P))
        dve.wait_ge(self.xt_hi, t + 1)
        self.c.nc.vector.scalar_tensor_tensor(out=self.XTl[part], in0=self.bank(t).rearrange("p (k q) -> p k q", k=KD),
                                              scalar=self.scale, in1=plain(self.XTh[part]), op0=ALU.mult,
                                              op1=ALU.subtract).then_inc(self.xt_lo, 1)

    def dve_step(self, dve, t):
        if self.norm and t < NT:
            self.moments(dve, t)
        if self.norm and 1 <= t <= NT:
            self.normalize(dve, t - 1)
        if not self.to_dram and 3 <= t < NT + 3:
            self.low(dve, t - 3)

    def act_step(self, act, t):
        if self.norm and t < NT:
            self.root(act, t)
        if not self.to_dram and 2 <= t < NT + 2:
            self.high(act, t - 2)

    def pe_step(self, pe, t):
        if not self.to_dram and 2 <= t < NT + 2:
            self.turn(pe, t - 2)

    def late(self, step, engine):
        for t in range(NT, NT + self.LATE):
            step(engine, t)

    def store(self, sp):
        if self.to_dram:
            y = self.c.out.rearrange("(t p) d -> p t d", p=P)
            for t in range(NT):
                sp.wait_ge(self.normed, t + 1)
                sp.dma_start(y[:, t, :], self.X[:, t, :]).then_inc(self.stored, 16)
            sp.wait_ge(self.stored, 16 * NT)


def phase_load(c):
    nc = c.nc
    with ExitStack() as ctx:
        x_in = [c.sem(ctx, f"x{t}_in") for t in range(NT)]
        ident_in = c.sem(ctx, "ident_in")
        norm = Norm(c, ctx, lambda t: (x_in[t], 16), (0, 1, 2, 3), norm=False)
        block = ctx.enter_context(nc.Block())

        @block.sync
        def _(sp):
            sp.dma_start(c.ident[:], c.inp["c_ident"]).then_inc(ident_in, 16)
            for t in range(NT):
                sp.dma_start(c.X[:, t, :], c.inp["x"][t * P:(t + 1) * P, :]).then_inc(x_in[t], 16)

        @block.tensor
        def _(pe):
            pe.wait_ge(ident_in, 16)
            for t in range(NT + norm.LATE):
                norm.pe_step(pe, t)

        @block.scalar
        def _(act):
            for t in range(NT + norm.LATE):
                norm.act_step(act, t)

        @block.vector
        def _(dve):
            dve.wait_ge(ident_in, 16)
            nc.vector.tensor_copy(c.identb[:], c.ident[:])
            for t in range(NT + norm.LATE):
                norm.dve_step(dve, t)


class Gate:
    BANK = 5

    def __init__(self, c, ctx, W, wg, bias, n, top, selection_bias=None, xt=None):
        self.c, self.W, self.wg, self.bias, self.n, self.top, self.selection_bias = c, W, wg, bias, n, top, selection_bias
        self.XTh, self.XTl, self.xs = xt or (c.XTh, c.XTl, XS)
        part, self.wsc = (F32R, 1.0) if xt else (F16, WS)
        self.w32 = c.sb(ctx, "gate_w32", [P, KD, n], F32)
        self.wh = c.sb(ctx, "gate_wh", [P, KD, n], part)
        self.wl = c.sb(ctx, "gate_wl", [P, KD, n], part)
        self.bb = c.sb(ctx, "gate_bias", [P, n], F32)
        self.sel_b = c.sb(ctx, "gate_selection", [P, n], F32)
        self.below = c.sb(ctx, "below", [P, 8, 8], F32)
        self.G = c.sb(ctx, "G", [P, NT, n], F32)
        self.K = c.sb(ctx, "keys", [P, NT, n], F32)
        self.E = c.sb(ctx, "E", [P, NT, n], F32)
        self.gt = c.sb(ctx, "gt", [P, NT, n, n], F32)
        self.eq = c.sb(ctx, "eq", [P, NT, n, n], F32)
        self.rank = c.sb(ctx, "rank", [P, NT, n], F32)
        self.m = c.sb(ctx, "m", [P, NT], F32)
        self.total = c.sb(ctx, "total", [P, NT], F32)
        self.gate_in = c.sem(ctx, "gate_in")
        self.gate_parts = c.sem(ctx, "gate_parts")
        self.gT = c.sb(ctx, "gT", [n, B, S], F32)
        self.products_done = c.sem(ctx, "gate_products")
        self.copied = c.sem(ctx, "gate_copied")
        self.gates = c.sem(ctx, "gates")
        self.step = c.sem(ctx, "gate_step")
        self.shifted = c.sem(ctx, "shifted")
        self.exp_done = c.sem(ctx, "gate_exp")
        self.chosen = c.sem(ctx, "chosen")

    def load(self, sp):
        sp.dma_start(self.w32[:], self.wg.rearrange("(k p) n -> p k n", p=P)).then_inc(self.gate_in, 16)
        sp.dma_start(self.bb[:], self.bias.partition_broadcast(P)).then_inc(self.gate_in, 16)
        sp.dma_start(self.below[:], self.c.inp["c_below"].partition_broadcast(P)).then_inc(self.gate_in, 16)
        selection = self.selection_bias if self.selection_bias is not None else self.bias
        sp.dma_start(self.sel_b[:], selection.partition_broadcast(P)).then_inc(self.gate_in, 16)

    def logits(self, pe):
        pe.wait_ge(self.gate_parts, 2)
        for b in range(B):
            for k in range(KD):
                tok = slice(b * S, (b + 1) * S)
                last = products(pe, self.c.PS[0:self.n, 6 + b, :], (self.wh[:, k, :], self.wl[:, k, :]),
                                (self.XTh[:, k, tok], self.XTl[:, k, tok]), start=(k == 0), stop=(k == KD - 1))
            last.then_inc(self.products_done, 1)
        for b in range(B):
            pe.wait_ge(self.copied, b + 1)
            for q in range(QT):
                t = b * QT + q
                last = pe.transpose(self.c.PS[:, self.BANK, t * 8:t * 8 + self.n], self.gT[:, b, q * P:(q + 1) * P],
                                    self.c.ident[0:self.n, 0:self.n])
        last.then_inc(self.gates, 1)

    def copy(self, act):
        for b in range(B):
            act.wait_ge(self.products_done, b + 1)
            self.c.nc.scalar.activation(self.gT[:, b, :], self.c.PS[0:self.n, 6 + b, :], ACT.Copy,
                                        scale=1.0 / (self.xs * self.wsc)).then_inc(self.copied, 1)

    def exp(self, act):
        act.wait_ge(self.shifted, 1)
        self.c.nc.scalar.activation(self.E[:], self.E[:], ACT.Exp).then_inc(self.exp_done, 1)

    def split(self, dve):
        nc = self.c.nc
        dve.wait_ge(self.gate_in, 64)
        nc.vector.tensor_scalar(self.wh[:], self.w32[:], self.wsc, None, ALU.mult).then_inc(self.gate_parts, 1)
        dve.wait_ge(self.gate_parts, 1)
        nc.vector.scalar_tensor_tensor(out=self.wl[:], in0=self.w32[:], scalar=self.wsc, in1=plain(self.wh[:]),
                                       op0=ALU.mult, op1=ALU.subtract).then_inc(self.gate_parts, 1)

    def choose(self, dve):
        nc, n, W = self.c.nc, self.n, self.W
        G, K, E, gt, eq, rank, m, total = self.G, self.K, self.E, self.gt, self.eq, self.rank, self.m, self.total
        count = [0]

        def link(instruction):
            count[0] += 1
            instruction.then_inc(self.step, 1)
            dve.wait_ge(self.step, count[0])

        def over_e(a, k=n):
            return a[:].unsqueeze(2).broadcast_to([P, NT, k])

        link(nc.vector.memset(W[:], 1.0))
        dve.wait_ge(self.gates, 1)
        logits = self.c.PS[:, self.BANK, 0:64].rearrange("p (t e) -> p t e", e=8)[:, :, 0:n]
        link(nc.vector.tensor_tensor(G[:], logits, self.bb[:].unsqueeze(1).broadcast_to([P, NT, n]), ALU.add))
        link(nc.vector.tensor_reduce(m[:], G[:], AX.X, ALU.max))
        nc.vector.tensor_tensor(E[:], G[:], over_e(m), ALU.subtract).then_inc(self.shifted, 1)
        dve.wait_ge(self.exp_done, 1)
        if self.selection_bias is None:
            keys = G
        else:
            keys = K
            link(nc.vector.tensor_reduce(total[:], E[:], AX.X, ALU.add))
            link(nc.vector.reciprocal(m[:], total[:]))
            link(nc.vector.tensor_tensor(E[:], E[:], over_e(m), ALU.mult))
            link(nc.vector.tensor_tensor(K[:], E[:], self.sel_b[:].unsqueeze(1).broadcast_to([P, NT, n]), ALU.add))
        for i in range(n):
            me = keys[:, :, i:i + 1].broadcast_to([P, NT, n])
            nc.vector.tensor_tensor(gt[:, :, i, :], keys[:], me, ALU.is_gt)
            a = nc.vector.tensor_tensor(eq[:, :, i, :], keys[:], me, ALU.is_equal)
        link(a)
        for t in range(NT):
            a = nc.vector.tensor_tensor(eq[:, t], eq[:, t], self.below[:, 0:n, 0:n], ALU.mult)
        link(a)
        link(nc.vector.tensor_tensor(gt[:], gt[:], eq[:], ALU.add))
        link(nc.vector.tensor_reduce(rank[:], gt[:], AX.X, ALU.add))
        link(nc.vector.scalar_tensor_tensor(out=E[:], in0=rank[:], scalar=float(self.top), in1=E[:],
                                            op0=ALU.is_lt, op1=ALU.mult))
        link(nc.vector.tensor_reduce(total[:], E[:], AX.X, ALU.add))
        link(nc.vector.reciprocal(m[:], total[:]))
        routed = NE - 2 if self.selection_bias is None else NE - 1
        nc.vector.tensor_tensor(W[:, :, 0:routed], E[:, :, 0:routed], over_e(m, routed), ALU.mult).then_inc(self.chosen, 1)


def phase_ffn1(c, W, gate, **end):
    nc = c.nc
    with ExitStack() as ctx:
        st = [c.sb(ctx, f"stage{i}", [P, KD, D], F32) for i in range(3)]
        wh = [[c.sb(ctx, f"wh{i}{q}", [P, KD, D], F16) for i in range(3)] for q in range(2)]
        wl = [[c.sb(ctx, f"wl{i}{q}", [P, KD, D], F16) for i in range(3)] for q in range(2)]
        Gh = c.sb(ctx, "Gh", [P, KD, B * S], F16)
        Gl = c.sb(ctx, "Gl", [P, KD, B * S], F16)
        s32 = c.sb(ctx, "s32", [P, 2, S], F32)
        g32 = c.sb(ctx, "g32", [P, 2, S], F32)
        ws = c.sb(ctx, "ws", [P, NT, NE], F32)
        gate = Gate(c, ctx, W, *gate)
        w_in = [c.sem(ctx, f"w{i}_in") for i in range(3)]
        w_hi = c.sem(ctx, "w_hi")
        w_lo = c.sem(ctx, "w_lo")
        ws_done = c.sem(ctx, "ws_done")
        up_done = c.sem(ctx, "up_done")
        silu_done = c.sem(ctx, "silu_done")
        g_done = c.sem(ctx, "g_done")
        g_hi = c.sem(ctx, "g_hi")
        g_lo = c.sem(ctx, "g_lo")
        down_done = c.sem(ctx, "down_done")
        added = c.sem(ctx, "added")
        norm = Norm(c, ctx, lambda t: (added, NT * (NE - 1) + t + 1), (0, 1), **end)
        block = ctx.enter_context(nc.Block())
        UP = B * KD
        CH = 3 * KD
        dram = [c.inp[k] for k in ("ffn1_W1", "ffn1_Wg", "ffn1_W2")]

        @block.sync
        def _(sp):
            def load(e):
                for i in range(3):
                    need(sp, w_lo, CH * (e - 1) + KD * (i + 1))
                    sp.dma_start(st[i][:], dram[i][e].rearrange("(k p) n -> p k n", p=P)
                                 if isinstance(e, int) else
                                 dram[i][bass.ds(e, 1)].rearrange("e (k p) n -> p (e k) n", p=P)).then_inc(w_in[i], 16)
            gate.load(sp)
            load(0)
            with sp.Fori(1, NE) as e:
                load(e)
            norm.store(sp)

        def split_hi(dve, e, q, ch):
            i, k = divmod(ch, KD)
            if k == 0:
                dve.wait_ge(w_in[i], 16 * (e + 1))
                need(dve, down_done, NT * (e - 1))
            nc.vector.tensor_scalar(wh[q][i][:, k, :], st[i][:, k, :], WS, None, ALU.mult).then_inc(w_hi, 1)

        def split_lo(dve, e, q, ch):
            i, k = divmod(ch, KD)
            dve.wait_ge(w_hi, CH * e + ch + 1)
            nc.vector.scalar_tensor_tensor(out=wl[q][i][:, k, :], in0=st[i][:, k, :], scalar=WS,
                                           in1=wh[q][i][:, k, :], op0=ALU.mult, op1=ALU.subtract).then_inc(w_lo, 1)

        def at(buffer, m):
            return buffer[:, m % KD, (m // KD) * S:(m // KD + 1) * S]

        @block.tensor
        def _(pe):
            def body(e, q):
                pe.wait_ge(w_lo, CH * e + 2 * KD)
                for m in range(UP):
                    b, ht = divmod(m, KD)
                    need(pe, g_done, UP * e + m - 1)
                    for i in range(2):
                        for k in range(KD):
                            last = products(pe, c.PS[:, 2 * (m % 2) + i, :],
                                            (wh[q][i][:, k, ht * P:(ht + 1) * P], wl[q][i][:, k, ht * P:(ht + 1) * P]),
                                            (c.XTh[:, k, b * S:(b + 1) * S], c.XTl[:, k, b * S:(b + 1) * S]),
                                            start=(k == 0), stop=(k == KD - 1))
                    last.then_inc(up_done, 1)
                pe.wait_ge(w_lo, CH * (e + 1))
                for t in range(NT):
                    if t % QT == 0:
                        pe.wait_ge(g_lo, UP * e + KD * (t // QT + 1))
                    need(pe, added, NT * e + t - 3)
                    for k in range(KD):
                        tok = slice(t * P, (t + 1) * P)
                        last = products(pe, c.PS[:, 4 + t % 4, :], (Gh[:, k, tok], Gl[:, k, tok]),
                                        (wh[q][2][:, k, :], wl[q][2][:, k, :]), start=(k == 0), stop=(k == KD - 1))
                    last.then_inc(down_done, 1)
                    if isinstance(e, int) and e == NE - 1:
                        if t == 2:
                            pe.wait_ge(g_done, UP * NE)
                        norm.pe_step(pe, t)
            gate.logits(pe)
            body(0, 0)
            with pe.Fori(0, NE // 2 - 1) as i:
                body(2 * i + 1, 1)
                body(2 * i + 2, 0)
            body(NE - 1, 1)
            norm.late(norm.pe_step, pe)

        @block.scalar
        def _(act):
            def g_part(e, m):
                act.wait_ge(g_done, UP * e + m + 1)
                if m == 0:
                    need(act, down_done, NT * e)
                nc.scalar.activation(at(Gh, m), g32[:, m % 2, :], ACT.Copy).then_inc(g_hi, 1)

            def body(e):
                for m in range(UP):
                    n = UP * e + m
                    act.wait_ge(up_done, n + 1)
                    need(act, g_done, n - 1)
                    nc.scalar.activation(s32[:, m % 2, :], c.PS[:, 2 * (m % 2), :], ACT.Silu,
                                         scale=1.0 / (XS * WS)).then_inc(silu_done, 1)
                    if m > 0:
                        g_part(e, m - 1)
                g_part(e, UP - 1)
            gate.copy(act)
            gate.exp(act)
            body(0)
            with act.Fori(1, NE) as e:
                body(e)
            for t in range(NT + norm.LATE):
                norm.act_step(act, t)

        @block.vector
        def _(dve):
            def g_part(e, m):
                dve.wait_ge(g_hi, UP * e + m + 1)
                nc.vector.tensor_tensor(at(Gl, m), g32[:, m % 2, :], at(Gh, m), ALU.subtract).then_inc(g_lo, 1)

            def body(e, q, more):
                for m in range(UP):
                    n = UP * e + m
                    dve.wait_ge(silu_done, n + 1)
                    need(dve, g_lo, n - 1)
                    nc.vector.scalar_tensor_tensor(out=g32[:, m % 2, :], in0=c.PS[:, 2 * (m % 2) + 1, :],
                                                   scalar=1.0 / WS, in1=s32[:, m % 2, :],
                                                   op0=ALU.mult, op1=ALU.mult).then_inc(g_done, 1)
                    mine = range(CH * m // UP, CH * (m + 1) // UP) if more else ()
                    for ch in mine:
                        split_hi(dve, e + 1, 1 - q, ch)
                    if m > 0:
                        g_part(e, m - 1)
                    for ch in mine:
                        split_lo(dve, e + 1, 1 - q, ch)
                g_part(e, UP - 1)
                for t in range(NT):
                    dve.wait_ge(down_done, NT * e + t + 1)
                    need(dve, added, NT * (e - 1) + t + 1)
                    w = ws[:, t, e:e + 1] if isinstance(e, int) else ws[:, t, bass.ds(e, 1)]
                    nc.vector.scalar_tensor_tensor(out=c.X[:, t, :], in0=c.PS[:, 4 + t % 4, :], scalar=w,
                                                   in1=c.X[:, t, :], op0=ALU.mult, op1=ALU.add).then_inc(added, 1)
                    if not more:
                        norm.dve_step(dve, t)
            gate.split(dve)
            for ch in range(2 * KD):
                split_hi(dve, 0, 0, ch)
                if ch > 0:
                    split_lo(dve, 0, 0, ch - 1)
            split_lo(dve, 0, 0, 2 * KD - 1)
            gate.choose(dve)
            dve.wait_ge(gate.chosen, 1)
            nc.vector.tensor_scalar(ws[:], W[:], 1.0 / (XS * WS), None, ALU.mult).then_inc(ws_done, 1)
            for ch in range(2 * KD, CH):
                split_hi(dve, 0, 0, ch)
                split_lo(dve, 0, 0, ch)
            dve.wait_ge(ws_done, 1)
            body(0, 0, True)
            with dve.Fori(0, NE // 2 - 1) as i:
                body(2 * i + 1, 1, True)
                body(2 * i + 2, 0, True)
            body(NE - 1, 1, False)
            norm.late(norm.dve_step, dve)


def phase_ffn0(c, W, gate, src, res, dst, **end):
    nc = c.nc
    XTh, XTl, _ = c.wide
    M0 = E0 // P
    with ExitStack() as ctx:
        st = [c.sb(ctx, f"stage{i}", [P, k, n], F32) for i, (k, n) in enumerate([(KD, E0), (M0, E0), (M0, D)])]
        wh = [[c.sb(ctx, f"wh{i}{q}", [P, k, n], F32R) for i, (k, n) in enumerate([(KD, E0), (M0, E0), (M0, D)])] for q in range(2)]
        wl = [[c.sb(ctx, f"wl{i}{q}", [P, k, n], F32R) for i, (k, n) in enumerate([(KD, E0), (M0, E0), (M0, D)])] for q in range(2)]
        bup = c.sb(ctx, "bup", [P, NE, M0], F32)
        bsw = c.sb(ctx, "bsw", [P, NE, M0], F32)
        bdn = c.sb(ctx, "bdn", [NE, D], F32)
        WT = c.sb(ctx, "WT", [NE, NT, P], F32)
        Hh = c.sb(ctx, "Hh", [P, M0, B * S], F32R)
        Hl = c.sb(ctx, "Hl", [P, M0, B * S], F32R)
        Gh = c.sb(ctx, "Gh", [P, M0, B * S], F32R)
        Gl = c.sb(ctx, "Gl", [P, M0, B * S], F32R)
        UP = B * M0
        h32 = c.sb(ctx, "h32", [P, UP, S], F32)
        s32 = c.sb(ctx, "s32", [P, 2, S], F32)
        g32 = c.sb(ctx, "g32", [P, UP, S], F32)
        gate = Gate(c, ctx, W, *gate, NE, NE - 2, xt=c.wide)
        w_in = [c.sem(ctx, f"w{i}_in") for i in range(3)]
        bias_in = c.sem(ctx, "bias_in")
        w_hi = c.sem(ctx, "w_hi")
        w_lo = c.sem(ctx, "w_lo")
        wt_turned = c.sem(ctx, "wt_turned")
        wt_done = c.sem(ctx, "wt_done")
        res_done = c.sem(ctx, "res_done")
        biases_done = c.sem(ctx, "biases_done")
        up_done = c.sem(ctx, "up_done")
        h_done = c.sem(ctx, "h_done")
        h_hi = c.sem(ctx, "h_hi")
        h_lo = c.sem(ctx, "h_lo")
        sw_done = c.sem(ctx, "sw_done")
        silu_done = c.sem(ctx, "silu_done")
        g_done = c.sem(ctx, "g_done")
        g_hi = c.sem(ctx, "g_hi")
        g_lo = c.sem(ctx, "g_lo")
        g_lo_dve = c.sem(ctx, "g_lo_dve")
        down_done = c.sem(ctx, "down_done")
        added = c.sem(ctx, "added")
        norm = Norm(c, ctx, lambda t: (added, NT * (NE - 1) + t + 1), (0, 1), X=dst, **end)
        block = ctx.enter_context(nc.Block())
        dram = [c.inp[k] for k in ("ffn0_Wup", "ffn0_Wsw", "ffn0_Wdn")]
        parts = [(i, h) for i in range(3) for h in range(2 if i != 1 else 1)]
        CH = len(parts)
        LAST = [2, 3, 5]

        def piece(buffer, ch):
            i, h = parts[ch]
            flat = buffer[i][:].rearrange("p k n -> p (k n)")
            return flat[:, h * 512:(h + 1) * 512]

        def col(a, e, m):
            return a[:, e, m:m + 1] if isinstance(e, int) else a[:, bass.ds(e, 1), m:m + 1].rearrange("p e m -> p (e m)")

        @block.sync
        def _(sp):
            def load(e):
                for i in range(3):
                    need(sp, w_lo, CH * (e - 1) + LAST[i])
                    sp.dma_start(st[i][:], dram[i][e].rearrange("(k p) n -> p k n", p=P)
                                 if isinstance(e, int) else
                                 dram[i][bass.ds(e, 1)].rearrange("e (k p) n -> p (e k) n", p=P)).then_inc(w_in[i], 16)
            gate.load(sp)
            load(0)
            sp.dma_start(bup[:], c.inp["ffn0_bup"]).then_inc(bias_in, 16)
            sp.dma_start(bsw[:], c.inp["ffn0_bsw"]).then_inc(bias_in, 16)
            sp.dma_start(bdn[:], c.inp["ffn0_bdn"]).then_inc(bias_in, 16)
            with sp.Fori(1, NE) as e:
                load(e)
            norm.store(sp)

        def split_hi(dve, e, q, ch):
            i, h = parts[ch]
            if h == 0:
                dve.wait_ge(w_in[i], 16 * (e + 1))
                need(dve, down_done, NT * (e - 1))
            nc.vector.tensor_copy(piece(wh[q], ch), piece(st, ch)).then_inc(w_hi, 1)

        def at(buffer, m):
            return buffer[:, m % M0, (m // M0) * S:(m // M0 + 1) * S]

        @block.gpsimd
        def _(pool):
            def split_lo(e, q, ch):
                pool.wait_ge(w_hi, CH * e + ch + 1)
                nc.gpsimd.tensor_tensor(piece(wl[q], ch), piece(st, ch), plain(piece(wh[q], ch)),
                                        ALU.subtract).then_inc(w_lo, 1)

            def body(e, q, more):
                if more:
                    for ch in range(CH):
                        split_lo(e + 1, 1 - q, ch)
                for m in (0, 2):
                    pool.wait_ge(g_hi, UP * e + m + 1)
                    nc.gpsimd.tensor_tensor(at(Gl, m), g32[:, m, :], plain(at(Gh, m)), ALU.subtract).then_inc(g_lo, 1)
            for ch in range(CH):
                split_lo(0, 0, ch)
            body(0, 0, True)
            with pool.Fori(0, NE // 2 - 1) as i:
                body(2 * i + 1, 1, True)
                body(2 * i + 2, 0, True)
            body(NE - 1, 1, False)

        @block.tensor
        def _(pe):
            def biases():
                pe.wait_ge(wt_done, 1)
                for t in range(NT):
                    need(pe, res_done, t - 3)
                    pe.matmul(c.PS[:, 4 + t % 4, :], WT[:, t, :], bdn[:], start=True, stop=True).then_inc(biases_done, 1)

            def turn_w():
                pe.wait_ge(bias_in, 48)
                pe.wait_ge(gate.chosen, 1)
                for t in range(NT):
                    last = pe.transpose(c.PS[0:NE, 4 + t // 4, (t % 4) * P:(t % 4 + 1) * P], W[:, t, :], c.ident[:])
                last.then_inc(wt_turned, 1)

            def body(e, q):
                pe.wait_ge(w_lo, CH * e + LAST[0])
                for m in range(UP):
                    b, mt = divmod(m, M0)
                    need(pe, h_hi, UP * e + m - 1)
                    for k in range(KD):
                        w = slice(mt * P, (mt + 1) * P)
                        last = products(pe, c.PS[:, m % 2, :], (wh[q][0][:, k, w], wl[q][0][:, k, w]),
                                        (XTh[:, k, b * S:(b + 1) * S], XTl[:, k, b * S:(b + 1) * S]),
                                        start=(k == 0), stop=(k == KD - 1))
                    last.then_inc(up_done, 1)
                if isinstance(e, int) and e == 0:
                    turn_w()
                pe.wait_ge(w_lo, CH * e + LAST[1])
                for m in range(UP):
                    b, mt = divmod(m, M0)
                    pe.wait_ge(h_lo, UP * e + M0 * (b + 1))
                    need(pe, silu_done, UP * e + m - 1)
                    for k in range(M0):
                        w = slice(mt * P, (mt + 1) * P)
                        last = products(pe, c.PS[:, 2 + m % 2, :], (wh[q][1][:, k, w], wl[q][1][:, k, w]),
                                        (Hh[:, k, b * S:(b + 1) * S], Hl[:, k, b * S:(b + 1) * S]),
                                        start=(k == 0), stop=(k == M0 - 1))
                    last.then_inc(sw_done, 1)
                pe.wait_ge(w_lo, CH * e + LAST[2])
                if isinstance(e, int) and e == 0:
                    biases()
                    pe.wait_ge(res_done, NT)
                for t in range(NT):
                    if t % QT == 0:
                        pe.wait_ge(g_lo, UP // 2 * e + M0 // 2 * (t // QT + 1))
                        pe.wait_ge(g_lo_dve, UP // 2 * e + M0 // 2 * (t // QT + 1))
                    need(pe, added, NT * e + t - 3)
                    for k in range(M0):
                        tok = slice(t * P, (t + 1) * P)
                        last = products(pe, c.PS[:, 4 + t % 4, :], (Gh[:, k, tok], Gl[:, k, tok]),
                                        (wh[q][2][:, k, :], wl[q][2][:, k, :]), start=(k == 0), stop=(k == M0 - 1))
                    last.then_inc(down_done, 1)
                    if isinstance(e, int) and e == NE - 1:
                        if t == 2:
                            pe.wait_ge(h_hi, UP * NE)
                        norm.pe_step(pe, t)
            gate.logits(pe)
            body(0, 0)
            with pe.Fori(0, NE // 2 - 1) as i:
                body(2 * i + 1, 1)
                body(2 * i + 2, 0)
            body(NE - 1, 1)
            norm.late(norm.pe_step, pe)

        @block.scalar
        def _(act):
            def g_part(e, m):
                act.wait_ge(g_done, UP * e + m + 1)
                if m == 0:
                    need(act, down_done, NT * e)
                nc.scalar.activation(at(Gh, m), g32[:, m, :], ACT.Copy).then_inc(g_hi, 1)

            def body(e):
                for m in range(UP):
                    n = UP * e + m
                    act.wait_ge(up_done, n + 1)
                    if m == 0:
                        need(act, sw_done, UP * e)
                    need(act, g_done, n - UP + 1)
                    passed(act, c.act_passed, e)
                    nc.scalar.activation(h32[:, m, :], c.PS[:, m % 2, :], ACT.Identity,
                                         bias=col(bup, e, m % M0)).then_inc(h_done, 1)
                    nc.scalar.activation(at(Hh, m), c.PS[:, m % 2, :], ACT.Identity,
                                         bias=col(bup, e, m % M0)).then_inc(h_hi, 1)
                if isinstance(e, int) and e == 0:
                    act.wait_ge(wt_turned, 1)
                    nc.scalar.activation(WT[:].rearrange("e t p -> e (t p)"),
                                         c.PS[0:NE, 4:6, :].rearrange("e a b -> e (a b)"), ACT.Copy).then_inc(wt_done, 1)
                for m in range(UP):
                    n = UP * e + m
                    act.wait_ge(sw_done, n + 1)
                    need(act, g_done, n - 1)
                    passed(act, c.act_passed, e)
                    nc.scalar.activation(s32[:, m % 2, :], c.PS[:, 2 + m % 2, :], ACT.Silu,
                                         bias=col(bsw, e, m % M0)).then_inc(silu_done, 1)
                    if m % 2 == 1:
                        g_part(e, m - 1)
                        g_part(e, m)
            act.wait_ge(bias_in, 48)
            gate.copy(act)
            gate.exp(act)
            body(0)
            with act.Fori(1, NE) as e:
                body(e)
            for t in range(NT + norm.LATE):
                norm.act_step(act, t)

        @block.vector
        def _(dve):
            def g_part(e, m):
                dve.wait_ge(g_hi, UP * e + m + 1)
                nc.vector.tensor_tensor(at(Gl, m), g32[:, m, :], plain(at(Gh, m)), ALU.subtract).then_inc(g_lo_dve, 1)

            def body(e, q, more):
                first = isinstance(e, int) and e == 0
                if more and not first:
                    for ch in range(CH):
                        split_hi(dve, e + 1, 1 - q, ch)
                for m in range(UP):
                    dve.wait_ge(h_hi, UP * e + m + 1)
                    nc.vector.tensor_tensor(at(Hl, m), h32[:, m, :], plain(at(Hh, m)), ALU.subtract).then_inc(h_lo, 1)
                if more and first:
                    for ch in range(CH):
                        split_hi(dve, e + 1, 1 - q, ch)
                for m in range(UP):
                    n = UP * e + m
                    dve.wait_ge(silu_done, n + 1)
                    if m % 2 == 0:
                        need(dve, g_lo, UP // 2 * (e - 1) + m // 2 + 1)
                    nc.vector.tensor_tensor(g32[:, m, :], h32[:, m, :], s32[:, m % 2, :], ALU.mult).then_inc(g_done, 1)
                    if m % 2 == 1:
                        g_part(e, m)
                if first:
                    for t in range(NT):
                        dve.wait_ge(biases_done, t + 1)
                        nc.vector.scalar_tensor_tensor(out=dst[:, t, :], in0=src[:, t, :], scalar=float(res),
                                                       in1=c.PS[:, 4 + t % 4, :], op0=ALU.mult,
                                                       op1=ALU.add).then_inc(res_done, 1)
                    dve.wait_ge(res_done, NT)
                for t in range(NT):
                    dve.wait_ge(down_done, NT * e + t + 1)
                    need(dve, added, NT * (e - 1) + t + 1)
                    w = W[:, t, e:e + 1] if isinstance(e, int) else W[:, t, bass.ds(e, 1)]
                    nc.vector.scalar_tensor_tensor(out=dst[:, t, :], in0=c.PS[:, 4 + t % 4, :], scalar=w,
                                                   in1=dst[:, t, :], op0=ALU.mult, op1=ALU.add).then_inc(added, 1)
                    if not more:
                        norm.dve_step(dve, t)
            gate.split(dve)
            for ch in range(CH):
                split_hi(dve, 0, 0, ch)
            gate.choose(dve)
            body(0, 0, True)
            with dve.Fori(0, NE // 2 - 1) as i:
                body(2 * i + 1, 1, True)
                body(2 * i + 2, 0, True)
            body(NE - 1, 1, False)
            norm.late(norm.dve_step, dve)


def phase_attn1(c, **end):
    nc = c.nc
    GH = 4
    NG = H // GH
    U = GH * B
    EARLY = NT - 2
    SC = 1.0 / float(np.sqrt(DQK)) / (XS * XS)
    with ExitStack() as ctx:
        sb = lambda name, shape, dt: c.sb(ctx, name, shape, dt)
        sem = lambda name: c.sem(ctx, name)
        st = [sb(f"stage{i}", [P, KD, GH * DQK], F32) for i in range(4)]
        wh = [sb(f"wh{i}", [P, KD, GH * DQK], F16) for i in range(4)]
        wl = [sb(f"wl{i}", [P, KD, GH * DQK], F16) for i in range(4)]
        bq = sb("bq", [P, 3, H], F32)
        bo = sb("bo", [P, D], F32)
        tri = sb("tri", [P, P], BF16)
        tri32 = sb("tri32", [P, P], F32)
        Vh = sb("Vh", [P, NT, GH * DQK], F16)
        Vl = sb("Vl", [P, NT, GH * DQK], F16)
        q32 = sb("q32", [P, 2, 2, S], F32)
        Qh = sb("Qh", [P, 2, 2, S], F16)
        Ql = sb("Ql", [P, 2, 2, S], F16)
        Pr = sb("Pr", [P, QT, S], F32)
        PTh = sb("PTh", [P, 2, KD, S], F16)
        PTl = sb("PTl", [P, 2, KD, S], F16)
        z32 = sb("z32", [P, 2, S], F32)
        Zh = sb("Zh", [P, GH, B * S], F16)
        Zl = sb("Zl", [P, GH, B * S], F16)
        nmax = sb("nmax", [P, 2 * QT], F32)
        nbias = sb("nbias", [P, 2 * QT], F32)
        rsum = sb("rsum", [P, 2 * QT], F32)
        rinv = sb("rinv", [P, 2 * QT], F32)
        w_in = [sem(f"w{i}_in") for i in range(4)]
        bias_in, tri_in, const_done = sem("bias_in"), sem("tri_in"), sem("const_done")
        w_hi, w_lo = sem("w_hi"), sem("w_lo")
        v_done, v_hi, v_lo = sem("v_done"), sem("v_hi"), sem("v_lo")
        qk_done, qk_act, qk_lo = sem("qk_done"), sem("qk_act"), sem("qk_lo")
        s_done, max_done, bias_done = sem("s_done"), sem("max_done"), sem("bias_done")
        exp_done, inv_done, norm_done = sem("exp_done"), sem("inv_done"), sem("norm_done")
        t_done, pt_hi, pt_lo = sem("t_done"), sem("pt_hi"), sem("pt_lo")
        z_done, z_act, z_lo = sem("z_done"), sem("z_act"), sem("z_lo")
        o_done, added = sem("o_done"), sem("added")
        norm = Norm(c, ctx, lambda t: (added, NT * (NG - 1) + t + 1), (2, 3), **end)
        block = ctx.enter_context(nc.Block())
        dram = [c.inp[k] for k in ("attn1_WV", "attn1_WQ", "attn1_WK", "attn1_WO")]

        @block.sync
        def _(sp):
            def load(g):
                for i in range(4):
                    need(sp, w_lo, 4 * (g - 1) + i + 1)
                    for h in range(GH):
                        cols = slice(h * DQK, (h + 1) * DQK)
                        head = dram[i][GH * g + h] if isinstance(g, int) else dram[i][bass.ds(GH * g + h, 1)]
                        if i < 3:
                            pat = "(k p) e -> p k e" if isinstance(g, int) else "o (k p) e -> p (o k) e"
                            sp.dma_start(st[i][:, :, cols], head.rearrange(pat, p=P)).then_inc(w_in[i], 16)
                        else:
                            pat = "e d -> e d" if isinstance(g, int) else "o e d -> e (o d)"
                            sp.dma_start(st[i][:, h, :], head.rearrange(pat)).then_inc(w_in[i], 16)
            sp.dma_start(tri32[:], c.inp["c_tri"]).then_inc(tri_in, 16)
            load(0)
            sp.dma_start(bq[:], c.inp["attn1_bT"]).then_inc(bias_in, 16)
            sp.dma_start(bo[:], c.inp["attn1_bO"].partition_broadcast(P)).then_inc(bias_in, 16)
            with sp.Fori(1, NG) as g:
                load(g)
            norm.store(sp)

        @block.gpsimd
        def _(pool):
            def z_part(g, u, uu):
                hh, b = divmod(uu, B)
                to = slice(b * S, (b + 1) * S)
                pool.wait_ge(z_act, 2 * u + 2)
                nc.gpsimd.tensor_tensor(Zl[:, hh, to], z32[:, uu % 2, :], Zh[:, hh, to], ALU.subtract).then_inc(z_lo, 1)

            def body(g):
                for uu in range(U):
                    z_part(g, U * g + uu, uu)
            body(0)
            with pool.Fori(1, NG) as g:
                body(g)

        @block.tensor
        def _(pe):
            def qk(g, u, uu, j):
                hh, b = divmod(uu, B)
                if uu == 0:
                    need(pe, added, NT * g)
                else:
                    pe.wait_ge(qk_act, 4 * (u - 1) + 2 * j + 2)
                for k in range(KD):
                    w = slice(hh * DQK, (hh + 1) * DQK)
                    last = products(pe, c.PS[:, j, :], (wh[1 + j][:, k, w], wl[1 + j][:, k, w]),
                                    (c.XTh[:, k, b * S:(b + 1) * S], c.XTl[:, k, b * S:(b + 1) * S]),
                                    start=(k == 0), stop=(k == KD - 1))
                last.then_inc(qk_done, 1)

            def scores(u, uu, qt):
                q = uu % 2
                if qt == 0:
                    pe.wait_ge(qk_lo, 2 * u + 2)
                need(pe, exp_done, QT * u + qt - 1)
                w = (qt + 1) * P
                out = c.PS[:, 2 + qt % 2, 0:w]
                tok = slice(qt * P, (qt + 1) * P)
                products(pe, out, (Qh[:, q, 0, tok], Ql[:, q, 0, tok]),
                         (Qh[:, q, 1, 0:w], Ql[:, q, 1, 0:w]), stop=False)
                pe.matmul(c.PS[:, 2 + qt % 2, w - P:w], c.identb[:], tri[:], start=False, stop=True,
                          skip_group_check=True).then_inc(s_done, 1)

            def turn(u, half):
                for qt in (2 * half, 2 * half + 1):
                    pe.wait_ge(norm_done, QT * u + qt + 1)
                    need(pe, pt_lo, QT * u + qt - 1)
                    for kt in range(qt + 1):
                        last = pe.transpose(c.PS[:, 4 + qt % 2, kt * P:(kt + 1) * P], Pr[:, qt, kt * P:(kt + 1) * P],
                                            c.ident[:])
                    last.then_inc(t_done, 1)

            def values(u, uu):
                hh, b = divmod(uu, B)
                q = uu % 2
                pe.wait_ge(pt_lo, QT * u + QT)
                need(pe, z_act, 2 * (u - 1))
                for kt in range(KD):
                    v = slice(hh * DQK, (hh + 1) * DQK)
                    last = products(pe, c.PS[:, 6 + q, kt * P:S], (Vh[:, b * QT + kt, v], Vl[:, b * QT + kt, v]),
                                    (PTh[:, q, kt, kt * P:S], PTl[:, q, kt, kt * P:S]),
                                    start=(kt == 0), stop=(kt == KD - 1))
                last.then_inc(z_done, 1)

            def output(g, t):
                if t == 0:
                    pe.wait_ge(w_lo, 4 * g + 4)
                    pe.wait_ge(z_lo, U * g + U - 1)
                if t == QT:
                    pe.wait_ge(z_lo, U * (g + 1))
                if t < 2:
                    pe.wait_ge(qk_act, 4 * U * (g + 1))
                else:
                    pe.wait_ge(added, NT * g + t - 1)
                tok = slice(t * P, (t + 1) * P)
                for hh in range(GH):
                    last = products(pe, c.PS[:, t % 2, :], (Zh[:, hh, tok], Zl[:, hh, tok]),
                                    (wh[3][:, hh, :], wl[3][:, hh, :]), start=(hh == 0), stop=(hh == GH - 1))
                last.then_inc(o_done, 1)
                if isinstance(g, int) and g == NG - 1 and t >= 3:
                    if t == 3:
                        pe.wait_ge(exp_done, QT * U * NG)
                    norm.pe_step(pe, t - 1)

            def v_tile(g, t):
                if t < 2:
                    need(pe, pt_lo, QT * U * g)
                elif t < 4:
                    need(pe, z_act, 2 * U * g)
                else:
                    pe.wait_ge(v_lo, NT * g + t - 3)
                for k in range(KD):
                    tok = slice(t * P, (t + 1) * P)
                    last = products(pe, c.PS[:, 4 + t % 4, :], (c.XTh[:, k, tok], c.XTl[:, k, tok]),
                                    (wh[0][:, k, :], wl[0][:, k, :]), start=(k == 0), stop=(k == KD - 1))
                last.then_inc(v_done, 1)

            def body(g):
                pe.wait_ge(w_lo, 4 * g + 1)
                for t in range(EARLY):
                    v_tile(g, t)
                for j in range(2):
                    pe.wait_ge(w_lo, 4 * g + 2 + j)
                    qk(g, U * g, 0, j)
                for t in range(EARLY, NT):
                    v_tile(g, t)
                for uu in range(U - 1):
                    u = U * g + uu
                    scores(u, uu, 0)
                    scores(u, uu, 1)
                    qk(g, u + 1, uu + 1, 0)
                    scores(u, uu, 2)
                    scores(u, uu, 3)
                    if uu == 0:
                        pe.wait_ge(v_lo, NT * (g + 1))
                    turn(u, 0)
                    qk(g, u + 1, uu + 1, 1)
                    if uu > 0:
                        values(u - 1, uu - 1)
                    turn(u, 1)
                u = U * g + U - 1
                scores(u, U - 1, 0)
                scores(u, U - 1, 1)
                values(u - 1, U - 2)
                scores(u, U - 1, 2)
                scores(u, U - 1, 3)
                turn(u, 0)
                output(g, 0)
                turn(u, 1)
                output(g, 1)
                output(g, 2)
                values(u, U - 1)
                for t in range(3, NT):
                    output(g, t)
            pe.wait_ge(const_done, 1)
            body(0)
            with pe.Fori(1, NG - 1) as g:
                body(g)
            body(NG - 1)
            norm.pe_step(pe, NT - 1)
            norm.late(norm.pe_step, pe)

        @block.scalar
        def _(act):
            def head_bias(i, g, hh):
                return bq[:, i, GH * g + hh:GH * g + hh + 1] if isinstance(g, int) else bq[:, i, bass.ds(GH * g + hh, 1)]

            def qk(g, u, uu, j):
                hh, q = uu // B, uu % 2
                act.wait_ge(qk_done, 2 * u + j + 1)
                need(act, s_done, QT * (u - 1))
                need(act, qk_lo, 2 * (u - 2) + j + 1)
                passed(act, c.act_passed, u)
                nc.scalar.activation(q32[:, q, j, :], c.PS[:, j, :], ACT.Identity, bias=head_bias(j, g, hh),
                                     scale=1.0 / WS).then_inc(qk_act, 1)
                nc.scalar.activation(Qh[:, q, j, :], c.PS[:, j, :], ACT.Identity, bias=head_bias(j, g, hh),
                                     scale=1.0 / WS).then_inc(qk_act, 1)

            def z_out(g, u, uu):
                hh, b = divmod(uu, B)
                act.wait_ge(z_done, u + 1)
                need(act, z_lo, u - 1)
                if uu == 0:
                    need(act, o_done, NT * g)
                passed(act, c.act_passed, u)
                nc.scalar.activation(z32[:, uu % 2, :], c.PS[:, 6 + uu % 2, :], ACT.Identity,
                                     bias=head_bias(2, g, hh), scale=1.0 / PS_).then_inc(z_act, 1)
                nc.scalar.activation(Zh[:, hh, b * S:(b + 1) * S], c.PS[:, 6 + uu % 2, :], ACT.Identity,
                                     bias=head_bias(2, g, hh), scale=1.0 / PS_).then_inc(z_act, 1)

            def v_part(g, t):
                act.wait_ge(v_done, NT * g + t + 1)
                if t == 0:
                    need(act, z_done, U * g)
                nc.scalar.activation(Vh[:, t, :], c.PS[:, 4 + t % 4, :], ACT.Copy, scale=1.0 / WS).then_inc(v_hi, 1)

            def exp(u, uu, qt):
                i = (uu % 2) * QT + qt
                w = (qt + 1) * P
                act.wait_ge(bias_done, QT * u + qt + 1)
                need(act, t_done, QT * (u - 1) + qt + 1)
                nc.scalar.activation(Pr[:, qt, 0:w], c.PS[:, 2 + qt % 2, 0:w], ACT.Exp, bias=nbias[:, i:i + 1],
                                     scale=SC, accum_out=rsum[:, i:i + 1]).then_inc(exp_done, 1)

            def turned(u, uu, qt):
                act.wait_ge(t_done, QT * u + qt + 1)
                if qt == 0:
                    need(act, z_done, u - 1)
                nc.scalar.activation(PTh[:, uu % 2, 0:qt + 1, qt * P:(qt + 1) * P],
                                     c.PS[:, 4 + qt % 2, 0:(qt + 1) * P].rearrange("p (k q) -> p k q", q=P),
                                     ACT.Copy, scale=PS_).then_inc(pt_hi, 1)

            def body(g):
                for t in range(EARLY):
                    v_part(g, t)
                for j in range(2):
                    qk(g, U * g, 0, j)
                for t in range(EARLY, NT):
                    v_part(g, t)
                for uu in range(U):
                    u = U * g + uu
                    exp(u, uu, 0)
                    exp(u, uu, 1)
                    if uu < U - 1:
                        qk(g, u + 1, uu + 1, 0)
                    else:
                        z_out(g, u - 1, uu - 1)
                    exp(u, uu, 2)
                    turned(u, uu, 0)
                    exp(u, uu, 3)
                    turned(u, uu, 1)
                    if uu < U - 1:
                        qk(g, u + 1, uu + 1, 1)
                    turned(u, uu, 2)
                    turned(u, uu, 3)
                    if 0 < uu < U - 1:
                        z_out(g, u - 1, uu - 1)
                z_out(g, U * g + U - 1, U - 1)
            act.wait_ge(const_done, 2)
            body(0)
            with act.Fori(1, NG) as g:
                body(g)
            for t in range(NT + norm.LATE):
                norm.act_step(act, t)

        @block.vector
        def _(dve):
            def qk_lo_part(u, uu, j):
                q = uu % 2
                dve.wait_ge(qk_act, 4 * u + 2 * j + 2)
                nc.vector.tensor_tensor(Ql[:, q, j, :], q32[:, q, j, :], Qh[:, q, j, :], ALU.subtract).then_inc(qk_lo, 1)

            def weight_hi(g, i):
                dve.wait_ge(w_in[i], 16 * GH * (g + 1))
                if i == 0:
                    need(dve, v_done, NT * g)
                if i == 1:
                    need(dve, qk_done, 2 * U * g)
                if i == 3:
                    need(dve, o_done, NT * g)
                nc.vector.tensor_scalar(wh[i][:], st[i][:], WS, None, ALU.mult).then_inc(w_hi, 1)

            def weight_lo(g, i):
                dve.wait_ge(w_hi, 4 * g + i + 1)
                flat = lambda a: a[:].rearrange("p k n -> p (k n)")
                nc.vector.scalar_tensor_tensor(out=flat(wl[i]), in0=flat(st[i]), scalar=WS, in1=flat(wh[i]),
                                               op0=ALU.mult, op1=ALU.subtract).then_inc(w_lo, 1)

            def add_output(g, t):
                dve.wait_ge(o_done, NT * g + t + 1)
                need(dve, added, NT * (g - 1) + t + 1)
                nc.vector.scalar_tensor_tensor(out=c.X[:, t, :], in0=c.PS[:, t % 2, :], scalar=1.0 / (XS * WS),
                                               in1=c.X[:, t, :], op0=ALU.mult, op1=ALU.add).then_inc(added, 1)

            def inverse(u, uu, qt):
                i = (uu % 2) * QT + qt
                dve.wait_ge(exp_done, QT * u + qt + 1)
                nc.vector.reciprocal(rinv[:, i:i + 1], rsum[:, i:i + 1]).then_inc(inv_done, 1)

            def normalize(u, uu, qt):
                i = (uu % 2) * QT + qt
                w = (qt + 1) * P
                dve.wait_ge(inv_done, QT * u + qt + 1)
                nc.vector.tensor_scalar(Pr[:, qt, 0:w], Pr[:, qt, 0:w], rinv[:, i:i + 1], None,
                                        ALU.mult).then_inc(norm_done, 1)

            def v_part(g, t):
                dve.wait_ge(v_hi, NT * g + t + 1)
                nc.vector.scalar_tensor_tensor(out=Vl[:, t, :], in0=c.PS[:, 4 + t % 4, :], scalar=1.0 / WS,
                                               in1=Vh[:, t, :], op0=ALU.mult, op1=ALU.subtract).then_inc(v_lo, 1)

            def maximum(u, uu, qt):
                i = (uu % 2) * QT + qt
                dve.wait_ge(s_done, QT * u + qt + 1)
                nc.vector.tensor_reduce(nmax[:, i:i + 1], c.PS[:, 2 + qt % 2, 0:(qt + 1) * P], AX.X, ALU.max,
                                        negate=True).then_inc(max_done, 1)
                dve.wait_ge(max_done, QT * u + qt + 1)
                nc.vector.tensor_scalar(nbias[:, i:i + 1], nmax[:, i:i + 1], SC, None, ALU.mult).then_inc(bias_done, 1)

            def turned(u, uu, qt):
                dve.wait_ge(pt_hi, QT * u + qt + 1)
                part = (slice(None), uu % 2, slice(0, qt + 1), slice(qt * P, (qt + 1) * P))
                nc.vector.scalar_tensor_tensor(
                    out=PTl[part], in0=c.PS[:, 4 + qt % 2, 0:(qt + 1) * P].rearrange("p (k q) -> p k q", q=P),
                    scalar=PS_, in1=PTh[part], op0=ALU.mult, op1=ALU.subtract).then_inc(pt_lo, 1)

            def body(g, more):
                for t in range(EARLY):
                    v_part(g, t)
                    if t < 4:
                        (weight_hi if t % 2 == 0 else weight_lo)(g, 1 + t // 2)
                for j in range(2):
                    qk_lo_part(U * g, 0, j)
                for t in range(EARLY, NT):
                    v_part(g, t)
                for uu in range(U):
                    u = U * g + uu
                    for qt in range(2):
                        maximum(u, uu, qt)
                    for qt in range(2):
                        inverse(u, uu, qt)
                        normalize(u, uu, qt)
                    if uu < U - 1:
                        qk_lo_part(u + 1, uu + 1, 0)
                    for qt in range(2, QT):
                        maximum(u, uu, qt)
                    inverse(u, uu, 2)
                    normalize(u, uu, 2)
                    turned(u, uu, 0)
                    inverse(u, uu, 3)
                    normalize(u, uu, 3)
                    turned(u, uu, 1)
                    if uu < U - 1:
                        qk_lo_part(u + 1, uu + 1, 1)
                    else:
                        add_output(g, 0)
                    turned(u, uu, 2)
                    turned(u, uu, 3)
                    if uu in (1, 2):
                        (weight_hi if uu == 1 else weight_lo)(g, 3)
                    if uu in (3, 4) and more:
                        (weight_hi if uu == 3 else weight_lo)(g + 1, 0)
                for t in range(1, NT):
                    add_output(g, t)
                    if not more:
                        if t == 1:
                            norm.dve_step(dve, 0)
                        norm.dve_step(dve, t)
            dve.wait_ge(tri_in, 16)
            nc.vector.tensor_copy(tri[:], tri32[:]).then_inc(const_done, 1)
            weight_hi(0, 0)
            weight_lo(0, 0)
            dve.wait_ge(bias_in, 32)
            nc.vector.tensor_scalar(bq[:], bq[:], XS, None, ALU.mult).then_inc(const_done, 1)
            for t in range(NT):
                last = nc.vector.tensor_tensor(c.X[:, t, :], c.X[:, t, :], bo[:], ALU.add)
            last.then_inc(const_done, 1)
            dve.wait_ge(const_done, 3)
            body(0, True)
            with dve.Fori(1, NG - 1) as g:
                body(g, True)
            body(NG - 1, False)
            norm.late(norm.dve_step, dve)


def phase_attn0(c, **end):
    nc = c.nc
    U = REP * B
    TL = U + B
    SC = 1.0 / float(np.sqrt(DQK)) / (XS * XS)
    NS = 3

    TURNS = [(0, 1), (2,), (3,)]
    NTU = len(TURNS)

    def turn_columns(j):
        first = SO0[TURNS[j][0]]
        return first, first + sum(SP0[qt] for qt in TURNS[j])

    def tiles(uu):
        b, hh = divmod(uu, REP)
        first = b * (REP + 1)
        return [first, first + 1] if hh == 0 else [first + 1 + hh]

    def ahead(g, uu, d, more):
        if uu + d < U:
            return [(g, uu + d)]
        return [(g + 1, uu + d - U)] if more else []

    with ExitStack() as ctx:
        sb = lambda name, shape, dt: c.sb(ctx, name, shape, dt)
        sem = lambda name: c.sem(ctx, name)
        wq32 = sb("wq32", [P, KD, REP * DQK], F32)
        wk32 = sb("wk32", [P, KD, DQK], F32)
        wv32 = sb("wv32", [P, KD, KVH * DV], F32)
        wo32 = sb("wo32", [P, KD, D], F32)
        wh = sb("wh", [P, KVH, REP + 1, KD, DQK], F16)
        wl = sb("wl", [P, KVH, REP + 1, KD, DQK], F16)
        wvh, wvl = sb("wvh", [P, KD, KVH * DV], F16), sb("wvl", [P, KD, KVH * DV], F16)
        woh, wol = sb("woh", [P, KD, D], F16), sb("wol", [P, KD, D], F16)
        rot32, rot = sb("rot32", [P, P], F32), sb("rot", [P, P], F16)
        cos, sin = sb("cos", [P, S], F32), sb("sin", [P, S], F32)
        mask32, mask = sb("mask32", [P, 9 * P], F32), sb("mask", [P, 9 * P], BF16)
        Vh, Vl = sb("Vh", [P, NT, KVH * DV], F16), sb("Vl", [P, NT, KVH * DV], F16)
        Ah, Al = sb("Ah", [P, 2, S], F16), sb("Al", [P, 2, S], F16)
        t1, t2, r32 = sb("t1", [P, 2, S], F32), sb("t2", [P, 2, S], F32), sb("r32", [P, 2, S], F32)
        Kh, Kl = sb("Kh", [P, 2, S], F16), sb("Kl", [P, 2, S], F16)
        Qh, Ql = sb("Qh", [P, 2, S], F16), sb("Ql", [P, 2, S], F16)
        Pr = sb("Pr", [P, QT, NS * P], F32)
        PTh, PTl = sb("PTh", [P, 2, sum(SP0)], F16), sb("PTl", [P, 2, sum(SP0)], F16)
        Z = sb("Z", [P, NT, D], F32)
        ZTh, ZTl = sb("ZTh", [P, KD, B * S], F16), sb("ZTl", [P, KD, B * S], F16)
        nmax, nbias = sb("nmax", [P, 2 * QT], F32), sb("nbias", [P, 2 * QT], F32)
        rsum, rinv = sb("rsum", [P, 2 * QT], F32), sb("rinv", [P, 2 * QT], F32)
        wq_in, wk_in, wv_in, wo_in, const_in = sem("wq_in"), sem("wk_in"), sem("wv_in"), sem("wo_in"), sem("const_in")
        const_done = sem("const_done")
        wv_hi, wv_lo, wo_hi, wo_lo = sem("wv_hi"), sem("wv_lo"), sem("wo_hi"), sem("wo_lo")
        w_hi, w_lo = sem("w_hi"), sem("w_lo")
        v_done, v_hi, v_lo = sem("v_done"), sem("v_hi"), sem("v_lo")
        a_done, a_hi, a_lo, a_cos = sem("a_done"), sem("a_hi"), sem("a_lo"), sem("a_cos")
        r_done, r_sin, r_sum, r_hi, r_lo = sem("r_done"), sem("r_sin"), sem("r_sum"), sem("r_hi"), sem("r_lo")
        s_done, max_done, bias_done = sem("s_done"), sem("max_done"), sem("bias_done")
        exp_done, inv_done = sem("exp_done"), sem("inv_done")
        t_done, pt_hi, pt_lo = sem("t_done"), sem("pt_hi"), sem("pt_lo")
        z_done, z_out = sem("z_done"), sem("z_out")
        zt_done, zt_hi, zt_lo = sem("zt_done"), sem("zt_hi"), sem("zt_lo")
        o_done, added = sem("o_done"), sem("added")
        norm = Norm(c, ctx, lambda t: (added, t + 1), (2, 3), **end)
        block = ctx.enter_context(nc.Block())

        def block_of(w, g, hh, cols=slice(0, DQK)):
            if isinstance(g, int):
                return w[:, g, hh, :, cols]
            return w[:, bass.ds(g, 1), hh, :, cols].rearrange("p g k n -> p (g k) n")

        @block.sync
        def _(sp):
            def load(g):
                need(sp, w_lo, 10 * g)
                if isinstance(g, int):
                    q, k = c.inp["attn0_wq"][g], c.inp["attn0_wk"][g]
                    pat = "(k p) n -> p k n"
                else:
                    q, k = c.inp["attn0_wq"][bass.ds(g, 1)], c.inp["attn0_wk"][bass.ds(g, 1)]
                    pat = "g (k p) n -> p (g k) n"
                sp.dma_start(wk32[:], k.rearrange(pat, p=P)).then_inc(wk_in, 16)
                sp.dma_start(wq32[:], q.rearrange(pat, p=P)).then_inc(wq_in, 16)
            sp.dma_start(wv32[:], c.inp["attn0_wv"].rearrange("(k p) n -> p k n", p=P)).then_inc(wv_in, 16)
            load(0)
            for to, name in ((rot32, "c_rot"), (cos, "c_cos"), (sin, "c_sin"), (mask32, "c_mask0")):
                sp.dma_start(to[:], c.inp[name]).then_inc(const_in, 16)
            sp.dma_start(wo32[:], c.inp["attn0_wo"].rearrange("(k p) n -> p k n", p=P)).then_inc(wo_in, 16)
            with sp.Fori(1, KVH) as g:
                load(g)
            norm.store(sp)

        @block.gpsimd
        def _(pool):
            def rotate(g, uu):
                for tl in tiles(uu):
                    n = TL * g + tl
                    b, hh = divmod(tl, REP + 1)
                    q = tl % 2
                    hi, lo = (Kh[:, b, :], Kl[:, b, :]) if hh == 0 else (Qh[:, uu % 2, :], Ql[:, uu % 2, :])
                    pool.wait_ge(r_sin, n + 1)
                    need(pool, r_lo, n - 1)
                    nc.gpsimd.tensor_tensor(r32[:, q, :], t1[:, q, :], t2[:, q, :], ALU.add).then_inc(r_sum, 1)
                    pool.wait_ge(r_hi, n + 1)
                    nc.gpsimd.tensor_tensor(lo, r32[:, q, :], hi, ALU.subtract).then_inc(r_lo, 1)

            def body(g, more):
                for uu in range(U):
                    for a in ahead(g, uu, 1, more):
                        rotate(*a)
            rotate(0, 0)
            body(0, True)
            with pool.Fori(1, KVH - 1) as g:
                body(g, True)
            body(KVH - 1, False)

        @block.tensor
        def _(pe):
            def project(g, uu):
                for tl in tiles(uu):
                    n = TL * g + tl
                    b, hh = divmod(tl, REP + 1)
                    pe.wait_ge(w_lo, 2 * (REP + 1) * g + 2 * (hh + 1))
                    need(pe, a_cos, n - 1)
                    for k in range(KD):
                        w = [x[:, g, hh, k, :] if isinstance(g, int) else
                             x[:, bass.ds(g, 1), hh, k, :].rearrange("p g n -> p (g n)") for x in (wh, wl)]
                        last = products(pe, c.PS[:, tl % 2, :], w,
                                        (c.XTh[:, k, b * S:(b + 1) * S], c.XTl[:, k, b * S:(b + 1) * S]),
                                        start=(k == 0), stop=(k == KD - 1))
                    last.then_inc(a_done, 1)

            def rotate(g, uu):
                for tl in tiles(uu):
                    n = TL * g + tl
                    pe.wait_ge(a_lo, n + 1)
                    need(pe, r_sin, n)
                    pe.matmul(c.PS[:, 7, :], rot[:], Ah[:, tl % 2, :], start=True, stop=False)
                    pe.matmul(c.PS[:, 7, :], rot[:], Al[:, tl % 2, :], start=False, stop=True).then_inc(r_done, 1)

            def scores(g, uu, qt):
                u = U * g + uu
                b, hh = divmod(uu, REP)
                if qt == 0:
                    pe.wait_ge(r_lo, TL * g + tiles(uu)[-1] + 1)
                need(pe, exp_done, QT * u + qt - 1)
                bank = c.PS[:, 2 + qt % 2, :]
                tok = slice(qt * P, (qt + 1) * P)
                pe.matmul(bank[:, 0:SP0[qt]], c.identb[:], mask[:, SO0[qt]:SO0[qt] + SP0[qt]], start=True,
                          stop=False, skip_group_check=True)
                runs = [(0, 0, SP0[qt])] if qt < 3 else [(0, 0, P), (P, 2 * P, 2 * P)]
                for to, of, w in runs:
                    last = products(pe, bank[:, to:to + w], (Qh[:, uu % 2, tok], Ql[:, uu % 2, tok]),
                                    (Kh[:, b, of:of + w], Kl[:, b, of:of + w]), start=False)
                last.then_inc(s_done, 1)

            def turn(g, uu, j):
                u = U * g + uu
                pe.wait_ge(exp_done, QT * u + TURNS[j][-1] + 1)
                need(pe, pt_lo, NTU * u + j - 1)
                first, _ = turn_columns(j)
                for qt in TURNS[j]:
                    for i in range(len(KT0[qt])):
                        to = SO0[qt] - first + i * P
                        last = pe.transpose(c.PS[:, 4 + (NTU * uu + j) % 2, to:to + P], Pr[:, qt, i * P:(i + 1) * P],
                                            c.ident[:])
                last.then_inc(t_done, 1)

            def values(g, uu):
                u = U * g + uu
                b = uu // REP
                q = uu % 2
                pe.wait_ge(pt_lo, NTU * (u + 1))
                need(pe, z_out, u)
                for qt in range(QT):
                    for i, kt in enumerate(KT0[qt]):
                        part = slice(SO0[qt] + i * P, SO0[qt] + (i + 1) * P)
                        vh, vl = value_columns(g, b * QT + kt)
                        last = products(pe, c.PS[:, 6, qt * DV:(qt + 1) * DV],
                                        (PTh[:, q, part], PTl[:, q, part]), (vh, vl),
                                        start=(i == 0), stop=(i == len(KT0[qt]) - 1))
                last.then_inc(z_done, 1)

            def value_columns(g, t):
                if isinstance(g, int):
                    return Vh[:, t, g * DV:(g + 1) * DV], Vl[:, t, g * DV:(g + 1) * DV]
                return Vh[:, t, bass.ds(g * DV, DV)], Vl[:, t, bass.ds(g * DV, DV)]

            pe.wait_ge(wv_lo, 1)
            for t in range(NT):
                need(pe, v_lo, t - 3)
                for k in range(KD):
                    tok = slice(t * P, (t + 1) * P)
                    last = products(pe, c.PS[:, 4 + t % 4, 0:KVH * DV], (c.XTh[:, k, tok], c.XTl[:, k, tok]),
                                    (wvh[:, k, :], wvl[:, k, :]), start=(k == 0), stop=(k == KD - 1))
                last.then_inc(v_done, 1)

            def turn_z(t):
                pe.wait_ge(z_out, U * KVH - (REP if t < QT else 0))
                need(pe, zt_lo, t - 1)
                for k in range(KD):
                    last = pe.transpose(c.PS[:, 4 + t % 2, k * P:(k + 1) * P], Z[:, t, k * P:(k + 1) * P], c.ident[:])
                last.then_inc(zt_done, 1)

            def output(t):
                pe.wait_ge(zt_lo, t + 1)
                need(pe, added, t - 1)
                for k in range(KD):
                    tok = slice(t * P, (t + 1) * P)
                    last = products(pe, c.PS[:, t % 2, :], (ZTh[:, k, tok], ZTl[:, k, tok]), (woh[:, k, :], wol[:, k, :]),
                                    start=(k == 0), stop=(k == KD - 1))
                last.then_inc(o_done, 1)

            def body(g, more):
                for uu in range(U):
                    scores(g, uu, 0)
                    scores(g, uu, 1)
                    for a in ahead(g, uu, 1, more):
                        rotate(*a)
                    for a in ahead(g, uu, 2, more):
                        project(*a)
                    scores(g, uu, 2)
                    scores(g, uu, 3)
                    turn(g, uu, 0)
                    if uu > 0:
                        values(g, uu - 1)
                    elif not isinstance(g, int) or g > 0:
                        values(g - 1, U - 1)
                    turn(g, uu, 1)
                    turn(g, uu, 2)
            project(0, 0)
            pe.wait_ge(const_done, 2)
            pe.wait_ge(v_lo, NT)
            rotate(0, 0)
            project(0, 1)
            body(0, True)
            with pe.Fori(1, KVH - 1) as g:
                body(g, True)
            body(KVH - 1, False)
            pe.wait_ge(pt_lo, NTU * U * KVH)
            turn_z(0)
            turn_z(1)
            values(KVH - 1, U - 1)
            pe.wait_ge(wo_lo, 1)
            for t in range(NT):
                output(t)
                if t + 2 < NT:
                    turn_z(t + 2)
                if t == 2:
                    pe.wait_ge(exp_done, QT * U * KVH)
                norm.pe_step(pe, t)
            norm.late(norm.pe_step, pe)

        @block.scalar
        def _(act):
            def a_parts(g, uu):
                for tl in tiles(uu):
                    n = TL * g + tl
                    act.wait_ge(a_done, n + 1)
                    need(act, r_done, n - 1)
                    nc.scalar.activation(Ah[:, tl % 2, :], c.PS[:, tl % 2, :], ACT.Copy, scale=1.0 / WS).then_inc(a_hi, 1)

            def rotated(g, uu):
                for tl in tiles(uu):
                    n = TL * g + tl
                    b, hh = divmod(tl, REP + 1)
                    act.wait_ge(r_sum, n + 1)
                    need(act, s_done, QT * (U * g + uu - (REP if hh == 0 else 1)))
                    nc.scalar.activation(Kh[:, b, :] if hh == 0 else Qh[:, uu % 2, :], r32[:, tl % 2, :],
                                         ACT.Copy).then_inc(r_hi, 1)

            for t in range(NT):
                act.wait_ge(v_done, t + 1)
                nc.scalar.activation(Vh[:, t, :], c.PS[:, 4 + t % 4, 0:KVH * DV], ACT.Copy, scale=1.0 / WS).then_inc(v_hi, 1)

            def exp(u, uu, qt):
                i = (uu % 2) * QT + qt
                w = SP0[qt]
                act.wait_ge(bias_done, QT * u + qt + 1)
                need(act, t_done, NTU * (u - 1) + (1, 1, 2, 3)[qt])
                nc.scalar.activation(Pr[:, qt, 0:w], c.PS[:, 2 + qt % 2, 0:w], ACT.Exp, bias=nbias[:, i:i + 1],
                                     scale=SC, accum_out=rsum[:, i:i + 1]).then_inc(exp_done, 1)

            def turned(u, uu, j):
                act.wait_ge(t_done, NTU * u + j + 1)
                if j == 0:
                    need(act, z_done, u - 1)
                first, last = turn_columns(j)
                nc.scalar.activation(PTh[:, uu % 2, first:last], c.PS[:, 4 + (NTU * uu + j) % 2, 0:last - first],
                                     ACT.Copy, scale=PS_).then_inc(pt_hi, 1)

            def body(g, more):
                for uu in range(U):
                    u = U * g + uu
                    exp(u, uu, 0)
                    exp(u, uu, 1)
                    for a in ahead(g, uu, 1, more):
                        rotated(*a)
                    exp(u, uu, 2)
                    turned(u, uu, 0)
                    exp(u, uu, 3)
                    turned(u, uu, 1)
                    for a in ahead(g, uu, 2, more):
                        a_parts(*a)
                    turned(u, uu, 2)
            a_parts(0, 0)
            rotated(0, 0)
            a_parts(0, 1)
            body(0, True)
            with act.Fori(1, KVH - 1) as g:
                body(g, True)
            body(KVH - 1, False)
            for t in range(NT):
                act.wait_ge(zt_done, t + 1)
                nc.scalar.activation(ZTh[:, :, t * P:(t + 1) * P], c.PS[:, 4 + t % 2, :].rearrange("p (k q) -> p k q", k=KD),
                                     ACT.Copy, scale=XS).then_inc(zt_hi, 1)
                if t >= 2:
                    norm.act_step(act, t - 2)
            for t in range(NT - 2, NT + norm.LATE):
                norm.act_step(act, t)

        @block.vector
        def _(dve):
            def weights(g, hh):
                if hh < 2:
                    dve.wait_ge(wk_in if hh == 0 else wq_in, 16 * (g + 1))
                for o in range(2):
                    src = wk32[:, :, o::2] if hh == 0 else wq32[:, :, (hh - 1) * DQK + o:hh * DQK:2]
                    hi, lo = (block_of(w, g, hh, slice(o * 64, o * 64 + 64)) for w in (wh, wl))
                    nc.vector.tensor_scalar(hi, src, WS, None, ALU.mult).then_inc(w_hi, 1)
                    dve.wait_ge(w_hi, 2 * (REP + 1) * g + 2 * hh + o + 1)
                    nc.vector.scalar_tensor_tensor(out=lo, in0=src, scalar=WS, in1=hi,
                                                   op0=ALU.mult, op1=ALU.subtract).then_inc(w_lo, 1)

            def a_parts(g, uu):
                for tl in tiles(uu):
                    n = TL * g + tl
                    dve.wait_ge(a_hi, n + 1)
                    nc.vector.scalar_tensor_tensor(out=Al[:, tl % 2, :], in0=c.PS[:, tl % 2, :], scalar=1.0 / WS,
                                                   in1=Ah[:, tl % 2, :], op0=ALU.mult, op1=ALU.subtract).then_inc(a_lo, 1)
                    need(dve, r_sum, n - 1)
                    nc.vector.scalar_tensor_tensor(out=t1[:, tl % 2, :], in0=c.PS[:, tl % 2, :], scalar=1.0 / WS,
                                                   in1=cos[:], op0=ALU.mult, op1=ALU.mult).then_inc(a_cos, 1)

            def sines(g, uu):
                for tl in tiles(uu):
                    n = TL * g + tl
                    dve.wait_ge(r_done, n + 1)
                    dve.wait_ge(a_cos, n + 1)
                    need(dve, r_sum, n - 1)
                    nc.vector.tensor_tensor(t2[:, tl % 2, :], c.PS[:, 7, :], sin[:], ALU.mult).then_inc(r_sin, 1)

            def inverse(u, uu):
                i = (uu % 2) * QT
                dve.wait_ge(exp_done, QT * (u + 1))
                nc.vector.reciprocal(rinv[:, i:i + QT], rsum[:, i:i + QT]).then_inc(inv_done, 1)

            def outputs(g, uu):
                u = U * g + uu
                b, hh = divmod(uu, REP)
                dve.wait_ge(z_done, u + 1)
                dve.wait_ge(inv_done, u + 1)
                i = (uu % 2) * QT
                first = (REP * g + hh) * DV
                cols = slice(first, first + DV) if isinstance(g, int) else bass.ds(first, DV)
                nc.vector.scalar_tensor_tensor(
                    out=Z[:, b * QT:(b + 1) * QT, cols], in0=c.PS[:, 6, 0:QT * DV].rearrange("p (q e) -> p q e", q=QT),
                    scalar=1.0 / (PS_ * XS), in1=rinv[:, i:i + QT].unsqueeze(2).broadcast_to([P, QT, DV]),
                    op0=ALU.mult, op1=ALU.mult).then_inc(z_out, 1)

            def maximum(u, uu, qt):
                i = (uu % 2) * QT + qt
                dve.wait_ge(s_done, QT * u + qt + 1)
                nc.vector.tensor_reduce(nmax[:, i:i + 1], c.PS[:, 2 + qt % 2, 0:SP0[qt]], AX.X, ALU.max,
                                        negate=True).then_inc(max_done, 1)
                dve.wait_ge(max_done, QT * u + qt + 1)
                nc.vector.tensor_scalar(nbias[:, i:i + 1], nmax[:, i:i + 1], SC, None, ALU.mult).then_inc(bias_done, 1)

            def turned(u, uu, j):
                dve.wait_ge(pt_hi, NTU * u + j + 1)
                first, last = turn_columns(j)
                nc.vector.scalar_tensor_tensor(
                    out=PTl[:, uu % 2, first:last], in0=c.PS[:, 4 + (NTU * uu + j) % 2, 0:last - first], scalar=PS_,
                    in1=PTh[:, uu % 2, first:last], op0=ALU.mult, op1=ALU.subtract).then_inc(pt_lo, 1)

            def body(g, more):
                for uu in range(U):
                    u = U * g + uu
                    maximum(u, uu, 0)
                    maximum(u, uu, 1)
                    for a in ahead(g, uu, 1, more):
                        sines(*a)
                    maximum(u, uu, 2)
                    maximum(u, uu, 3)
                    turned(u, uu, 0)
                    if uu > 0:
                        outputs(g, uu - 1)
                    elif not isinstance(g, int) or g > 0:
                        outputs(g - 1, U - 1)
                    inverse(u, uu)
                    turned(u, uu, 1)
                    for a in ahead(g, uu, 2, more):
                        a_parts(*a)
                    turned(u, uu, 2)
                    for hh in {0: (0,), 1: (1,), 4: (2, 3), 5: (4,)}.get(uu, ()) if more else ():
                        weights(g + 1, hh)
                    if not more and uu == U - 2:
                        output_weights()

            def output_weights():
                dve.wait_ge(wo_in, 16)
                nc.vector.tensor_scalar(woh[:], wo32[:], WS, None, ALU.mult).then_inc(wo_hi, 1)
                dve.wait_ge(wo_hi, 1)
                nc.vector.scalar_tensor_tensor(out=wol[:], in0=wo32[:], scalar=WS, in1=woh[:],
                                               op0=ALU.mult, op1=ALU.subtract).then_inc(wo_lo, 1)

            def z_part(t):
                part = (slice(None), slice(None), slice(t * P, (t + 1) * P))
                dve.wait_ge(zt_hi, t + 1)
                nc.vector.scalar_tensor_tensor(out=ZTl[part], in0=c.PS[:, 4 + t % 2, :].rearrange("p (k q) -> p k q", k=KD),
                                               scalar=XS, in1=ZTh[part], op0=ALU.mult, op1=ALU.subtract).then_inc(zt_lo, 1)

            dve.wait_ge(wv_in, 16)
            nc.vector.tensor_scalar(wvh[:], wv32[:], WS, None, ALU.mult).then_inc(wv_hi, 1)
            dve.wait_ge(wv_hi, 1)
            nc.vector.scalar_tensor_tensor(out=wvl[:], in0=wv32[:], scalar=WS, in1=wvh[:],
                                           op0=ALU.mult, op1=ALU.subtract).then_inc(wv_lo, 1)
            weights(0, 0)
            for t in range(NT):
                dve.wait_ge(v_hi, t + 1)
                nc.vector.scalar_tensor_tensor(out=Vl[:, t, :], in0=c.PS[:, 4 + t % 4, 0:KVH * DV], scalar=1.0 / WS,
                                               in1=Vh[:, t, :], op0=ALU.mult, op1=ALU.subtract).then_inc(v_lo, 1)
            weights(0, 1)
            dve.wait_ge(const_in, 64)
            nc.vector.tensor_copy(rot[:], rot32[:]).then_inc(const_done, 1)
            nc.vector.tensor_copy(mask[:], mask32[:]).then_inc(const_done, 1)
            a_parts(0, 0)
            weights(0, 2)
            sines(0, 0)
            a_parts(0, 1)
            weights(0, 3)
            weights(0, 4)
            body(0, True)
            with dve.Fori(1, KVH - 1) as g:
                body(g, True)
            body(KVH - 1, False)
            z_part(0)
            z_part(1)
            outputs(KVH - 1, U - 1)
            for t in range(NT):
                if t + 2 < NT:
                    z_part(t + 2)
                dve.wait_ge(o_done, t + 1)
                nc.vector.scalar_tensor_tensor(out=c.X[:, t, :], in0=c.PS[:, t % 2, :], scalar=1.0 / (XS * WS),
                                               in1=c.X[:, t, :], op0=ALU.mult, op1=ALU.add).then_inc(added, 1)
                norm.dve_step(dve, t)
            norm.late(norm.dve_step, dve)


def phase_cross0(c, **end):
    nc = c.nc
    SC = 1.0 / float(np.sqrt(D)) / (XS * XS)
    NC = B * CT
    with ExitStack() as ctx:
        sb = lambda name, shape, dt: c.sb(ctx, name, shape, dt)
        sem = lambda name: c.sem(ctx, name)
        C32 = sb("C32", [P, NC, D], F32)
        Ch, Cl = sb("Ch", [P, NC, D], F16), sb("Cl", [P, NC, D], F16)
        CTh, CTl = sb("CTh", [P, KD, B, S2], F16), sb("CTl", [P, KD, B, S2], F16)
        m32 = sb("m32", [P, B, S2 // 4], I32)
        m8 = m32[:].bitcast(U8)
        valid = sb("valid", [P, B], F32)
        mrow, ones = sb("mrow", [1, B, S2], BF16), sb("ones", [1, P], BF16)
        Pr = sb("Pr", [P, 2, S2], F32)
        PTh, PTl = sb("PTh", [P, 2, S2], F16), sb("PTl", [P, 2, S2], F16)
        nmax, nbias = sb("nmax", [P, 2], F32), sb("nbias", [P, 2], F32)
        rsum, rinv, rval = sb("rsum", [P, 2], F32), sb("rinv", [P, 2], F32), sb("rval", [P, 2], F32)
        c_in, m_in = [sem(f"c{i}_in") for i in range(NC // 2)], sem("m_in")
        m_done, v_done = sem("m_done"), sem("v_done")
        c_hi, c_lo = sem("c_hi"), sem("c_lo")
        ct_done, ct_hi, ct_lo = sem("ct_done"), sem("ct_hi"), sem("ct_lo")
        stored = sem("stored")
        s_done, max_done, bias_done = sem("s_done"), sem("max_done"), sem("bias_done")
        exp_done, inv_done, val_done = sem("exp_done"), sem("inv_done"), sem("val_done")
        t_done, pt_hi, pt_lo = sem("t_done"), sem("pt_hi"), sem("pt_lo")
        z_done, added = sem("z_done"), sem("added")
        norm = Norm(c, ctx, lambda t: (added, t + 1), (0, 1, 2, 3), **end)
        block = ctx.enter_context(nc.Block())

        def slot(i):
            return (CT + 2 * i, CT + 2 * i + 1) if i < CT // 2 else ()

        SLOT_BANKS = (4, 6, 6, 4)

        def context_bank(t):
            return c.PS[:, t % 2 + (0 if t < CT else SLOT_BANKS[(t - CT) // 2]), :]

        @block.sync
        def _(sp):
            tiles = c.inp["ctx"].rearrange("b (t p) d -> p (b t) d", p=P)
            for i in range(NC // 2):
                sp.dma_start(C32[:, 2 * i:2 * i + 2, :], tiles[:, 2 * i:2 * i + 2, :]).then_inc(c_in[i], 16)
                if i == 0:
                    sp.dma_start(m32[:], c.inp["mask"].partition_broadcast(P)).then_inc(m_in, 16)
            for b in range(B):
                sp.wait_ge(ct_lo, CT * (b + 1))
                for n, part in enumerate((CTh, CTl)):
                    sp.dma_start(c.ctxT[n][b].rearrange("(k p) s -> p k s", p=P), part[:, :, b, :]).then_inc(stored, 16)
            sp.wait_ge(stored, 64)
            norm.store(sp)

        @block.tensor
        def _(pe):
            def turn_context(t):
                if t % 2 == 0:
                    pe.wait_ge(c_in[t // 2], 16)
                need(pe, ct_lo, t - 1)
                for k in range(KD):
                    last = pe.transpose(context_bank(t)[:, k * P:(k + 1) * P], C32[:, t, k * P:(k + 1) * P], c.ident[:])
                last.then_inc(ct_done, 1)

            def scores(t):
                b = t // QT
                pe.wait_ge(ct_lo, CT * (b + 1))
                need(pe, exp_done, t - 1)
                tok = slice(t * P, (t + 1) * P)
                for half in range(2):
                    bank = c.PS[:, 2 * (t % 2) + half, :]
                    keys = slice(half * 512, half * 512 + 512)
                    pe.matmul(bank, ones[:], mrow[:, b, keys], start=True, stop=False, skip_group_check=True)
                    for k in range(KD):
                        last = products(pe, bank, (c.XTh[:, k, tok], c.XTl[:, k, tok]),
                                        (CTh[:, k, b, keys], CTl[:, k, b, keys]), start=False, stop=(k == KD - 1))
                last.then_inc(s_done, 1)

            def turn(t):
                pe.wait_ge(exp_done, t + 1)
                need(pe, pt_lo, t)
                pe.wait_ge(ct_lo, CT + 2 if t < 2 else NC)
                for k in range(CT):
                    last = pe.transpose(c.PS[:, 4 + k // 4, (k % 4) * P:(k % 4 + 1) * P], Pr[:, t % 2, k * P:(k + 1) * P],
                                        c.ident[:])
                last.then_inc(t_done, 1)

            def values(t):
                pe.wait_ge(pt_lo, t + 1)
                pe.wait_ge(c_lo, CT * (t // QT + 1))
                need(pe, added, t - 1)
                if t == 0:
                    pe.wait_ge(ct_lo, CT + 6)
                for k in range(CT):
                    at = (t // QT) * CT + k
                    last = products(pe, c.PS[:, 6 + t % 2, :], (PTh[:, t % 2, k * P:(k + 1) * P], PTl[:, t % 2, k * P:(k + 1) * P]),
                                    (Ch[:, at, :], Cl[:, at, :]), start=(k == 0), stop=(k == CT - 1))
                last.then_inc(z_done, 1)

            for t in range(CT):
                turn_context(t)
            pe.wait_ge(m_done, 2)
            scores(0)
            for u in (*slot(0), *slot(1)):
                turn_context(u)
            for t in range(NT):
                if t + 1 < NT:
                    scores(t + 1)
                turn(t)
                if t > 0:
                    values(t - 1)
                for u in slot(t + 2):
                    if u % 2 == 0 and t == 1:
                        pe.wait_ge(pt_lo, t + 1)
                    turn_context(u)
            values(NT - 1)
            if not norm.to_dram:
                for t in range(NT):
                    norm.turn(pe, t)

        @block.scalar
        def _(act):
            def context_high(t):
                act.wait_ge(ct_done, t + 1)
                nc.scalar.activation(CTh[:, :, t // CT, (t % CT) * P:(t % CT + 1) * P],
                                     context_bank(t).rearrange("p (k q) -> p k q", k=KD),
                                     ACT.Copy, scale=XS).then_inc(ct_hi, 1)
                nc.scalar.activation(Ch[:, t, :], C32[:, t, :], ACT.Copy, scale=XS).then_inc(c_hi, 1)

            for t in (*range(CT), *slot(0), *slot(1)):
                context_high(t)
            for t in range(NT):
                q = t % 2
                act.wait_ge(bias_done, t + 1)
                need(act, t_done, t - 1)
                nc.scalar.activation(Pr[:, q, :], c.PS[:, 2 * q:2 * q + 2, :].rearrange("p a b -> p (a b)"), ACT.Exp,
                                     bias=nbias[:, q:q + 1], scale=SC, accum_out=rsum[:, q:q + 1]).then_inc(exp_done, 1)
                act.wait_ge(t_done, t + 1)
                need(act, z_done, t - 1)
                nc.scalar.activation(PTh[:, q, :], c.PS[:, 4:6, :].rearrange("p a b -> p (a b)"), ACT.Copy,
                                     scale=PS_).then_inc(pt_hi, 1)
                for u in slot(t + 2):
                    context_high(u)
            for t in range(NT):
                norm.root(act, t)
            if not norm.to_dram:
                for t in range(NT):
                    norm.high(act, t)

        @block.vector
        def _(dve):
            def context_low(t):
                dve.wait_ge(ct_hi, t + 1)
                to = (slice(None), slice(None), t // CT, slice((t % CT) * P, (t % CT + 1) * P))
                nc.vector.scalar_tensor_tensor(out=CTl[to], in0=context_bank(t).rearrange("p (k q) -> p k q", k=KD),
                                               scalar=XS, in1=CTh[to], op0=ALU.mult, op1=ALU.subtract).then_inc(ct_lo, 1)
                dve.wait_ge(c_hi, t + 1)
                nc.vector.scalar_tensor_tensor(out=Cl[:, t, :], in0=C32[:, t, :], scalar=XS, in1=Ch[:, t, :],
                                               op0=ALU.mult, op1=ALU.subtract).then_inc(c_lo, 1)

            for t in range(CT):
                context_low(t)
            dve.wait_ge(m_in, 16)
            nc.vector.tensor_scalar(mrow[:], m8[0:1], 1.0, -NEG, ALU.subtract, ALU.mult).then_inc(m_done, 1)
            nc.vector.memset(ones[:], 1.0).then_inc(m_done, 1)
            for t in slot(0):
                context_low(t)

            def maximum(t):
                q = t % 2
                dve.wait_ge(s_done, t + 1)
                nc.vector.tensor_reduce(nmax[:, q:q + 1], c.PS[:, 2 * q:2 * q + 2, :], AX.XY, ALU.max,
                                        negate=True).then_inc(max_done, 1)
                dve.wait_ge(max_done, t + 1)
                nc.vector.tensor_scalar(nbias[:, q:q + 1], nmax[:, q:q + 1], SC, None, ALU.mult).then_inc(bias_done, 1)

            def output(t):
                dve.wait_ge(z_done, t + 1)
                nc.vector.scalar_tensor_tensor(out=c.X[:, t, :], in0=c.PS[:, 6 + t % 2, :], scalar=rval[:, t % 2:t % 2 + 1],
                                               in1=c.X[:, t, :], op0=ALU.mult, op1=ALU.add).then_inc(added, 1)

            maximum(0)
            for t in slot(1):
                context_low(t)
            for t in range(NT):
                q = t % 2
                if t + 1 < NT:
                    maximum(t + 1)
                dve.wait_ge(exp_done, t + 1)
                nc.vector.reciprocal(rinv[:, q:q + 1], rsum[:, q:q + 1]).then_inc(inv_done, 1)
                dve.wait_ge(pt_hi, t + 1)
                nc.vector.scalar_tensor_tensor(out=PTl[:, q, :], in0=c.PS[:, 4:6, :].rearrange("p a b -> p (a b)"),
                                               scalar=PS_, in1=PTh[:, q, :], op0=ALU.mult, op1=ALU.subtract).then_inc(pt_lo, 1)
                if t > 0:
                    output(t - 1)
                    norm.moments(dve, t - 1)
                if t == 0:
                    nc.vector.tensor_reduce(valid[:], m8, AX.X, ALU.max).then_inc(v_done, 1)
                    dve.wait_ge(v_done, 1)
                    nc.vector.tensor_scalar(valid[:], valid[:], 1.0 / (PS_ * XS), None, ALU.mult).then_inc(v_done, 1)
                    dve.wait_ge(v_done, 2)
                dve.wait_ge(inv_done, t + 1)
                nc.vector.tensor_tensor(rval[:, q:q + 1], rinv[:, q:q + 1], valid[:, t // QT:t // QT + 1],
                                        ALU.mult).then_inc(val_done, 1)
                dve.wait_ge(val_done, t + 1)
                for u in slot(t + 2):
                    context_low(u)
            for t in range(NT - 1):
                norm.normalize(dve, t)
            output(NT - 1)
            norm.moments(dve, NT - 1)
            norm.normalize(dve, NT - 1)
            if not norm.to_dram:
                for t in range(NT):
                    norm.low(dve, t)


def phase_cross1(c, **end):
    nc = c.nc
    SC = 1.0 / float(np.sqrt(DV)) / (XS * XS)
    OFF = S2 - S
    K0 = OFF // P
    R = 3 * DV
    MS = 32.0
    N = B * H
    GS = 4
    LEAD = GS + 2
    VW = 2 * DV + 1
    SLOTS = 4
    RING = CT + 4
    ON_POOL = (2, 4, 6, 7)
    with ExitStack() as ctx:
        sb = lambda name, shape, dt: c.sb(ctx, name, shape, dt)
        sem = lambda name: c.sem(ctx, name)
        KS = [sb(f"KS{b}", [P, H, S2], F16) for b in range(B)]
        QS = [sb(f"QS{b}", [P, H, S], F16) for b in range(B)]
        P32 = sb("P32", [P, SLOTS, S], F32)
        V = sb("V", [P, B * CT, H, VW], F16)
        tri32, triT32 = sb("tri32", [P, P], F32), sb("triT32", [P, P], F32)
        tri, triT = sb("tri", [P, P], BF16), sb("triT", [P, P], BF16)
        comb = sb("comb", [VW, DV + 1], F32)
        M = sb("M", [P, B, QT, H], F32)
        mt = sb("mt", [GS, S], F32)
        mh, ml = sb("mh", [GS, S], F16), sb("ml", [GS, S], F16)
        PTh, PTl = sb("PTh", [P, RING, S], F16), sb("PTl", [P, RING, S], F16)
        Zs = sb("Zs", [VW, 2, S], F32)
        rinv = sb("rinv", [P, QT], F32)
        z = sb("z", [P, 2, QT, DV], F32)
        stack_in = [sem(f"stack{g}_in") for g in range(N // GS)]
        const_in, const_done = sem("const_in"), sem("const_done")
        ctx_in = [sem(f"ctx{i}_in") for i in range(SLOTS)]
        v_hi, v_lo = sem("v_hi"), sem("v_lo")
        ones_done = sem("ones_done")
        s_done, max_done = sem("s_done"), sem("max_done")
        m_turned, m_shift, m_hi, m_lo, m_in = sem("m_turned"), sem("m_shift"), sem("m_hi"), sem("m_lo"), sem("m_in")
        e_done, exp_done = sem("e_done"), sem("exp_done")
        lo_dve, lo_pool = sem("lo_dve"), sem("lo_pool")
        z_done, z_copied, c_done = sem("z_done"), sem("z_copied"), sem("c_done")
        inv_done, z_out, added = sem("inv_done"), sem("z_out"), sem("added")
        norm = Norm(c, ctx, lambda t: (added, H * (t // QT + 1)), (0, 1, 2, 3), **end)
        block = ctx.enter_context(nc.Block())

        two_shifts = float(np.full(2, -MS, np.float16).view(np.float32)[0])

        def head(n):
            b, i = divmod(n, H)
            return b, i // GS + 4 * (i % GS), i

        def wait_lo(engine, n, kt):
            on_pool = kt in ON_POOL
            mine = [k for k in range(CT) if (k in ON_POOL) == on_pool]
            engine.wait_ge(lo_pool if on_pool else lo_dve, len(mine) * n + mine.index(kt) + 1)

        def first_query(kt):
            return max(kt - K0, 0) * P

        def turn_group(n):
            m = n + LEAD - 1
            return m // GS if m % GS == GS - 1 and GS <= m < N else None

        def low_part(engine, ops, n, kt, done):
            cols = slice(first_query(kt), S)
            engine.wait_ge(exp_done, CT * n + kt + 1)
            ops.tensor_tensor(PTl[:, (CT * n + kt) % RING, cols], P32[:, kt % SLOTS, cols], PTh[:, (CT * n + kt) % RING, cols],
                                 ALU.subtract).then_inc(done, 1)

        @block.sync
        def _(sp):
            def stacks(b):
                for h4 in range(4):
                    rows = slice(h4 * DV, (h4 + 1) * DV)
                    for n, (qp, kp) in enumerate(((c.XTh, 0), (c.XTh, 1), (c.XTl, 0))):
                        to = slice(n * DV, (n + 1) * DV)
                        sp.dma_start(QS[b][to, h4::4, :], qp[rows, :, b * S:(b + 1) * S]).then_inc(stack_in[b * 4 + h4], 16)
                        src = c.ctxT[kp][b].rearrange("(k f p) s -> f p k s", f=4, p=DV)[h4]
                        sp.dma_start(KS[b][to, h4::4, :], src).then_inc(stack_in[b * 4 + h4], 16)

            def shift_rows(g):
                b, h4 = divmod(g, H // GS)
                sp.wait_ge(m_lo, g + 1)
                sp.dma_start(QS[b][R:R + 1, h4::4, :], mh[:]).then_inc(m_in, 16)
                sp.dma_start(QS[b][R + 1:R + 2, h4::4, :], ml[:]).then_inc(m_in, 16)

            for to, name in ((tri32, "c_tri"), (triT32, "c_triT"), (comb, "c_comb")):
                sp.dma_start(to[:], c.inp[name]).then_inc(const_in, 16)
            stacks(0)
            for t in range(B * CT):
                need(sp, v_lo, t - SLOTS + 1)
                sp.dma_start(P32[:, t % SLOTS, :], c.inp["ctx"][t // CT, (t % CT) * P:(t % CT + 1) * P, :]).then_inc(ctx_in[t % SLOTS], 16)
            shift_rows(0)
            stacks(1)
            for g in range(1, N // GS):
                shift_rows(g)
            norm.store(sp)

        @block.gpsimd
        def _(pool):
            nc.gpsimd.memset(V[:, :, :, 2 * DV:VW], XS).then_inc(ones_done, 1)
            pool.wait_ge(ones_done, 1)
            nc.gpsimd.memset(KS[0][R:P].bitcast(F32), two_shifts).then_inc(ones_done, 1)
            pool.wait_ge(ones_done, 2)
            for t in range(B * CT):
                pool.wait_ge(v_hi, 2 * t + 2)
                nc.gpsimd.tensor_tensor(V[:, t, :, DV:2 * DV], P32[:, t % SLOTS, :].rearrange("p (h e) -> p h e", h=H),
                                        V[:, t, :, 0:DV], ALU.subtract).then_inc(v_lo, 1)
            pool.wait_ge(v_lo, B * CT)
            nc.gpsimd.memset(KS[1][R:P].bitcast(F32), two_shifts).then_inc(ones_done, 1)
            pool.wait_ge(ones_done, 3)

            def add(n):
                b, h, _ = head(n)
                pool.wait_ge(z_out, n + 1)
                x = c.X[:, b * QT:(b + 1) * QT, h * DV:(h + 1) * DV]
                nc.gpsimd.tensor_tensor(x, x, z[:, n % 2], ALU.add).then_inc(added, 1)

            for n in range(N + 2):
                if n < N:
                    for kt in ON_POOL:
                        low_part(pool, nc.gpsimd, n, kt, lo_pool)
                if n >= 2:
                    add(n - 2)

        @block.tensor
        def _(pe):
            def max_tile(n, qt):
                b, h, _ = head(n)
                i = QT * n + qt
                if qt == 0 and n % GS == 0:
                    pe.wait_ge(stack_in[n // GS], 16 * 6)
                need(pe, max_done, i - 1)
                w = OFF + (qt + 1) * P
                lhs = QS[b][0:R, h, qt * P:(qt + 1) * P]
                pe.matmul(c.PS[:, 2 * (i % 2), :], lhs, KS[b][0:R, h, 0:512], start=True, stop=True)
                pe.matmul(c.PS[:, 2 * (i % 2) + 1, 0:w - 512], lhs, KS[b][0:R, h, 512:w], start=True, stop=False,
                          skip_group_check=True)
                pe.matmul(c.PS[:, 2 * (i % 2) + 1, w - 512 - P:w - 512], c.identb[:], tri[:], start=False, stop=True,
                          skip_group_check=True).then_inc(s_done, 1)

            def turn_maxima(g):
                b, h = divmod(GS * g, H)
                pe.wait_ge(max_done, QT * GS * (g + 1))
                need(pe, z_out, GS * (g + 1) - LEAD - 1)
                for qt in range(QT):
                    last = pe.transpose(c.PS[0:GS, 7, qt * P:(qt + 1) * P], M[:, b, qt, h:h + GS], c.ident[:])
                last.then_inc(m_turned, 1)

            def exp_tile(n, kt):
                b, h, _ = head(n)
                i = CT * n + kt
                if n == H and kt == 0:
                    pe.wait_ge(ones_done, 3)
                if kt == 0 and n % GS == 0:
                    pe.wait_ge(m_in, 32 * (n // GS + 1))
                need(pe, exp_done, i - 1)
                q0 = first_query(kt)
                bank = c.PS[:, 4 + i % 2, :]
                last = pe.matmul(bank[:, q0:S], KS[b][0:R + 2, h, kt * P:(kt + 1) * P], QS[b][0:R + 2, h, q0:S],
                                 start=True, stop=(kt < K0), skip_group_check=True)
                if kt >= K0:
                    last = pe.matmul(bank[:, q0:q0 + P], c.identb[:], triT[:], start=False, stop=True,
                                     skip_group_check=True)
                last.then_inc(e_done, 1)

            def value_tile(n, kt):
                b, h, _ = head(n)
                wait_lo(pe, n, kt)
                if kt == 0:
                    need(pe, z_copied, n)
                cols = slice(first_query(kt), S)
                v, slot = V[:, b * CT + kt, h, :], (CT * n + kt) % RING
                pe.matmul(c.PS[0:VW, 6, cols], v, PTh[:, slot, cols], start=(kt == 0), stop=False,
                          skip_group_check=True)
                last = pe.matmul(c.PS[0:VW, 6, cols], v, PTl[:, slot, cols], start=False, stop=(kt == CT - 1),
                                 skip_group_check=True)
                last.then_inc(z_done, 1)

            def combine(n):
                pe.wait_ge(z_copied, n + 1)
                need(pe, z_out, n)
                pe.wait_ge(m_shift, 1 + sum(turn_group(i) is not None for i in range(n + 2)))
                for qt in range(QT):
                    last = pe.matmul(c.PS[:, 7, qt * (DV + 1):(qt + 1) * (DV + 1)], Zs[:, n % 2, qt * P:(qt + 1) * P],
                                     comb[:], start=True, stop=True, skip_group_check=True)
                last.then_inc(c_done, 1)

            pe.wait_ge(const_done, 2)
            pe.wait_ge(const_in, 48)
            for n in range(LEAD):
                for qt in range(QT):
                    max_tile(n, qt)
                if n == GS:
                    turn_maxima(0)
            pe.wait_ge(ones_done, 2)
            pe.wait_ge(v_lo, B * CT)
            for n in range(N + 2):
                for kt in range(CT):
                    if n < N:
                        exp_tile(n, kt)
                    if kt % 2 == 1 and n + LEAD < N:
                        max_tile(n + LEAD, kt // 2)
                    if 1 <= n <= N:
                        value_tile(n - 1, kt)
                    if kt == 3 and n >= 2:
                        combine(n - 2)
                    if kt == 5 and turn_group(n) is not None:
                        turn_maxima(turn_group(n))
            if not norm.to_dram:
                for t in range(NT):
                    norm.turn(pe, t)

        @block.scalar
        def _(act):
            for t in range(B * CT):
                act.wait_ge(ctx_in[t % SLOTS], 16 * (t // SLOTS + 1))
                nc.scalar.activation(V[:, t, :, 0:DV], P32[:, t % SLOTS, :].rearrange("p (h e) -> p h e", h=H),
                                     ACT.Copy, scale=XS).then_inc(v_hi, 1)
                nc.scalar.activation(P32[:, t % SLOTS, :], P32[:, t % SLOTS, :], ACT.Copy, scale=XS).then_inc(v_hi, 1)
            act.wait_ge(v_lo, B * CT)
            for n in range(N + 2):
                if n >= 2:
                    act.wait_ge(z_done, CT * (n - 1))
                    need(act, c_done, n - 3)
                    nc.scalar.activation(Zs[:, n % 2, :], c.PS[0:VW, 6, :], ACT.Copy).then_inc(z_copied, 1)
                if n == N:
                    for t in range(QT):
                        norm.root(act, t)
                for kt in range(CT if n < N else 0):
                    i = CT * n + kt
                    cols = slice(first_query(kt), S)
                    act.wait_ge(e_done, i + 1)
                    if i >= SLOTS:
                        wait_lo(act, *divmod(i - SLOTS, CT))
                    need(act, z_done, i + 1 - RING)
                    nc.scalar.activation(P32[:, kt % SLOTS, cols], c.PS[:, 4 + i % 2, cols], ACT.Exp, scale=SC)
                    nc.scalar.activation(PTh[:, i % RING, cols], c.PS[:, 4 + i % 2, cols], ACT.Exp,
                                         scale=SC).then_inc(exp_done, 1)
            for t in range(QT, NT):
                norm.root(act, t)
            if not norm.to_dram:
                for t in range(NT):
                    norm.high(act, t)

        @block.vector
        def _(dve):
            def max_tile(n, qt):
                b, _, h = head(n)
                i = QT * n + qt
                w = OFF + (qt + 1) * P
                dve.wait_ge(s_done, i + 1)
                nc.vector.tensor_reduce(M[:, b, qt, h:h + 1],
                                        c.PS[:, 2 * (i % 2):2 * (i % 2) + 2, :].rearrange("p a b -> p (a b)")[:, 0:w],
                                        AX.X, ALU.max).then_inc(max_done, 1)

            def shift_parts(g):
                dve.wait_ge(m_turned, g + 1)
                nc.vector.tensor_scalar(mt[:], c.PS[0:GS, 7, :], 1.0 / MS, -float(np.log(PS_)) / SC / MS,
                                        ALU.mult, ALU.add).then_inc(m_shift, 1)
                dve.wait_ge(m_shift, g + 1)
                need(dve, m_in, 32 * g)
                nc.vector.tensor_copy(mh[:], mt[:]).then_inc(m_hi, 1)
                dve.wait_ge(m_hi, g + 1)
                nc.vector.tensor_tensor(ml[:], mt[:], mh[:], ALU.subtract).then_inc(m_lo, 1)

            def output(n):
                dve.wait_ge(c_done, n + 1)
                need(dve, added, n - 1)
                bank = c.PS[:, 7, 0:QT * (DV + 1)].rearrange("p (q e) -> p q e", q=QT)
                need(dve, z_out, n)
                nc.vector.reciprocal(rinv[:].unsqueeze(2), bank[:, :, DV:DV + 1]).then_inc(inv_done, 1)
                dve.wait_ge(inv_done, n + 1)
                nc.vector.tensor_tensor(z[:, n % 2], bank[:, :, 0:DV], rinv[:].unsqueeze(2).broadcast_to([P, QT, DV]),
                                        ALU.mult).then_inc(z_out, 1)

            dve.wait_ge(const_in, 48)
            nc.vector.tensor_copy(tri[:], tri32[:]).then_inc(const_done, 1)
            nc.vector.tensor_copy(triT[:], triT32[:]).then_inc(const_done, 1)
            for n in range(LEAD):
                for qt in range(QT):
                    max_tile(n, qt)
                if n == GS:
                    shift_parts(0)
            for n in range(N + 2):
                for kt in range(CT):
                    if n < N and kt not in ON_POOL:
                        low_part(dve, nc.vector, n, kt, lo_dve)
                    if kt % 2 == 1 and n + LEAD < N:
                        max_tile(n + LEAD, kt // 2)
                    if kt == 4 and n >= 2:
                        output(n - 2)
                    if kt == 6 and turn_group(n) is not None:
                        shift_parts(turn_group(n))
                if H + 4 <= n < H + 4 + QT:
                    norm.moments(dve, n - H - 4)
                if n == N:
                    for t in range(QT):
                        norm.normalize(dve, t)
            for t in range(QT, NT):
                norm.moments(dve, t)
                if t > QT:
                    norm.normalize(dve, t - 1)
            norm.normalize(dve, NT - 1)
            if not norm.to_dram:
                for t in range(NT):
                    norm.low(dve, t)


def mixture_of_two_rounds(c, W, first, gate0, gate1, **end):
    with ExitStack() as ctx:
        c.wide = (c.sb(ctx, "XRh", [P, KD, B * S], F32R), c.sb(ctx, "XRl", [P, KD, B * S], F32R), 1.0)
        first(c.wide)
        Y = c.sb(ctx, "Y", [P, NT, D], F32)
        phase_ffn0(c, W, gate0, c.X, 1.0, Y, norm=False, to=c.wide)
        phase_ffn0(c, W, gate1, c.X, 2.0, c.X, **end)


def decoder(nc, inputs, out, phases):
    ctx = ExitStack()
    with ctx:
        c = Core(nc, ctx, inputs, out)
        W = c.sb(ctx, "W", [P, NT, NE], F32)
        phase_load(c)
        for p in phases:
            p(c, W)


PHASES = [
    lambda c, W: phase_attn0(c),
    lambda c, W: mixture_of_two_rounds(c, W, lambda to: phase_cross0(c, to=to),
                                       (c.inp["gate0_w0"], c.inp["gate0_b0"]), (c.inp["gate0_w1"], c.inp["gate0_b1"])),
    lambda c, W: phase_attn1(c),
    lambda c, W: phase_cross1(c),
    lambda c, W: phase_ffn1(c, W, (c.inp["gate1_w"], c.inp["gate1_b"], 7, 3, c.inp["gate1_sel"]), store=True),
]


def constants():
    i, j = np.arange(S)[:, None], np.arange(S)[None, :]
    seen = ((j <= i) & (j > i - WIN)) | ((j < FRONT) & (j <= i - WIN))
    window = np.where(seen, 0.0, NEG)
    causal = np.where(np.tril(np.ones((P, P))) > 0, 0.0, NEG)
    freq = 1.0 / 10000.0 ** (np.arange(0, DQK, 2).astype(np.float32) / DQK)
    angle = np.outer(np.arange(S, dtype=np.float32), freq).T
    half = np.eye(DQK // 2)
    zero = np.zeros_like(half)
    out = {
        "c_ident": np.eye(P),
        "c_below": np.tril(np.ones((8, 8)), -1),
        "c_tri": causal,
        "c_triT": causal.T,
        "c_comb": np.eye(2 * DV + 1)[:, np.r_[0:DV, 2 * DV]] + np.eye(2 * DV + 1, k=-DV)[:, :DV + 1] * (np.arange(DV + 1) < DV),
        "c_mask0": np.concatenate([window[q * P:(q + 1) * P, k * P:(k + 1) * P] for q in range(QT) for k in KT0[q]], 1),
        "c_cos": np.concatenate([np.cos(angle)] * 2),
        "c_sin": np.concatenate([np.sin(angle)] * 2),
        "c_rot": np.block([[zero, half], [-half, zero]]),
    }
    return {k: np.ascontiguousarray(v, dtype=np.float32) for k, v in out.items()}


def laid_out(v):
    v = {k: np.asarray(a) for k, a in v.items()}

    def by_tile(b):
        return b.reshape(NE, E0 // P, P).transpose(2, 0, 1)

    n = NE - 2
    twice = lambda a: np.stack([a, a])
    out = {
        "x": v["x"].reshape(B * S, D),
        "ctx": v["ctx_2048"],
        "mask": np.ascontiguousarray(v["mask_BxS2_bk0"]).view(np.int32),
        "attn0_wq": v["L0_attn_wq"].reshape(D, KVH, REP * DQK).transpose(1, 0, 2),
        "attn0_wk": v["L0_attn_wk"].reshape(D, KVH, DQK).transpose(1, 0, 2),
        "attn0_wv": v["L0_attn_wv"],
        "attn0_wo": v["L0_attn_wo"],
        "gate0_w0": v["L0_ffn_Wg"][0], "gate0_w1": v["L0_ffn_Wg"][1],
        "gate0_b0": v["L0_ffn_bg"][0], "gate0_b1": v["L0_ffn_bg"][1],
        "ffn0_Wup": np.concatenate([v["L0_ffn_Wup"], v["L0_ffn_Wsu"].reshape(D, 2, E0).transpose(1, 0, 2)]),
        "ffn0_Wsw": np.concatenate([v["L0_ffn_Wsw"], twice(v["L0_ffn_Wsa"])]),
        "ffn0_Wdn": np.concatenate([v["L0_ffn_Wdn"], v["L0_ffn_Wsd"].reshape(2, E0, D)]),
        "ffn0_bup": by_tile(np.concatenate([v["L0_ffn_bup"], v["L0_ffn_bsu"].reshape(2, E0)])),
        "ffn0_bsw": by_tile(np.concatenate([v["L0_ffn_bsw"], twice(v["L0_ffn_bsa"])])),
        "ffn0_bdn": np.concatenate([v["L0_ffn_bdn"], v["L0_ffn_bsd"][None], np.zeros((1, D), np.float32)]),
        "attn1_WQ": v["L1_attn_W_Q"], "attn1_WK": v["L1_attn_W_K"],
        "attn1_WV": v["L1_attn_W_V"], "attn1_WO": v["L1_attn_W_O"],
        "attn1_bT": np.stack([v["L1_attn_b_Q"].T, v["L1_attn_b_K"].T, v["L1_attn_b_V"].T], 1),
        "attn1_bO": v["L1_attn_b_O"],
        "gate1_w": v["L1_ffn_gate_w"], "gate1_b": v["L1_ffn_gate_b"], "gate1_sel": v["L1_ffn_biases"],
        "ffn1_W1": np.concatenate([v["L1_ffn_W1"], v["L1_ffn_Ws1"][None]]),
        "ffn1_Wg": np.concatenate([v["L1_ffn_Wg"], v["L1_ffn_Wsg"][None]]),
        "ffn1_W2": np.concatenate([v["L1_ffn_W2"], v["L1_ffn_Ws2"][None]]),
    }
    return {k: np.ascontiguousarray(a) for k, a in out.items()}


def kernel(**inputs):
    import concourse.bacc as bacc
    from concourse.bass_utils import run_bass_kernel_spmd

    arrays = {**laid_out(inputs), **constants()}
    nc = bacc.Bacc("TRN2", target_bir_lowering=False, num_devices=1)
    dram = {
        k: nc.dram_tensor(f"in_{k}", a.shape, mybir.dt.from_np(a.dtype), kind="ExternalInput").ap()
        for k, a in arrays.items()
    }
    out = nc.dram_tensor("out", (B * S, D), F32, kind="ExternalOutput").ap()
    decoder(nc, dram, out, PHASES)
    got = run_bass_kernel_spmd(nc, [{f"in_{k}": a for k, a in arrays.items()}], core_ids=[0])
    return got.results[0]["out"].reshape(B, S, D)
```
